# Optimizing a Trainium2 kernel written in Bass

```python
import numpy as np
import jax
import jax.numpy as jnp

def _softmax(x, axis=-1):
    return jax.nn.softmax(x, axis=axis)

def _gelu(x):
    return jax.nn.gelu(x, approximate=True)

def _silu(x):
    return jax.nn.silu(x)

def _sigmoid(x):
    return jax.nn.sigmoid(x)

def _layernorm(x, axis=-1, eps=1e-05):
    m = jnp.mean(x, axis=axis, keepdims=True)
    v = jnp.var(x, axis=axis, keepdims=True)
    return (x - m) / jnp.sqrt(v + eps)

def _scatter_add(tgt, idx, src, axis=0):
    return tgt.at[idx].add(src)

def _segment_sum(src, seg, n):
    return jax.ops.segment_sum(src, seg, n)
kernel_name = 'mk_gnn_preln_d4_gnn_r8_1f9471'

def setup_inputs(seed: int=0):
    np.random.seed(seed)
    _w = jnp.asarray

    def _rec_inputs():
        import jax
        import jax.numpy as jnp
        _gk = jax.random.key(seed)
        x = -0.0003713 + 1 * jax.random.normal(jax.random.fold_in(_gk, 1), (6250, 128), jnp.float32)
        src = jax.random.randint(jax.random.fold_in(_gk, 2), (100000,), 0, 6250, jnp.int32)
        dst = jnp.minimum((6250 * jax.random.uniform(jax.random.fold_in(_gk, 3), (100000,)) ** 2.0).astype(jnp.int32), 49999)
        _o = jnp.argsort(dst, stable=True)
        src = src[_o]
        dst = dst[_o]
        edge_attr_128 = 5.93493e-05 + 1.00006 * jax.random.normal(jax.random.fold_in(_gk, 12), (100000, 128), jnp.float32)
        edge_attr_4 = jax.random.uniform(jax.random.fold_in(_gk, 13), (100000, 4), jnp.float32, 0.0, 1)
        edge_type_16 = jax.random.randint(jax.random.fold_in(_gk, 15), (100000,), 0, 16, jnp.int32)
        edge_type_3 = jax.random.randint(jax.random.fold_in(_gk, 16), (100000,), 0, 3, jnp.int32)
        return (x, src, dst, edge_attr_128, edge_attr_4, edge_type_16, edge_type_3)
    x, src, dst, edge_attr_128, edge_attr_4, edge_type_16, edge_type_3 = _rec_inputs()

    def _L0_gnn_setup():
        import jax, jax.numpy as jnp
        import numpy as np
        N_NODES = 12500
        N_EDGES = 200000
        HIDDEN = 128
        N_ETYPES = 4
        N_STEPS = 4

        def _gru_cell(x, h, W_ih, W_hh, b_ih, b_hh):
            gi = x @ W_ih.T + b_ih
            gh = h @ W_hh.T + b_hh
            ir, iz, inn = jnp.split(gi, 3, axis=1)
            hr, hz, hn = jnp.split(gh, 3, axis=1)
            r = jax.nn.sigmoid(ir + hr)
            z = jax.nn.sigmoid(iz + hz)
            n = jnp.tanh(inn + r * hn)
            return (1.0 - z) * n + z * h
        key = jax.random.key(seed)
        ks = jax.random.split(key, 10)
        s = 1.0 / np.sqrt(HIDDEN)
        node_feat = jax.random.normal(ks[0], (N_NODES, HIDDEN), dtype=jnp.float32)
        edge_index = jax.random.randint(ks[1], (2, N_EDGES), 0, N_NODES)
        edge_feat = jax.random.uniform(ks[2], (N_EDGES, N_ETYPES), dtype=jnp.float32)
        W_edge = jax.random.uniform(ks[3], (N_ETYPES, HIDDEN, HIDDEN), minval=-s, maxval=s, dtype=jnp.float32)
        b_edge = jax.random.uniform(ks[4], (N_ETYPES, HIDDEN), minval=-s, maxval=s, dtype=jnp.float32)
        W_ih = jax.random.uniform(ks[5], (3 * HIDDEN, HIDDEN), minval=-s, maxval=s, dtype=jnp.float32)
        W_hh = jax.random.uniform(ks[6], (3 * HIDDEN, HIDDEN), minval=-s, maxval=s, dtype=jnp.float32)
        b_ih = jax.random.uniform(ks[7], (3 * HIDDEN,), minval=-s, maxval=s, dtype=jnp.float32)
        b_hh = jax.random.uniform(ks[8], (3 * HIDDEN,), minval=-s, maxval=s, dtype=jnp.float32)
        return {'node_feat': node_feat, 'edge_index': edge_index, 'edge_feat': edge_feat, 'W_edge': W_edge, 'b_edge': b_edge, 'W_ih': W_ih, 'W_hh': W_hh, 'b_ih': b_ih, 'b_hh': b_hh}
    _L0_gnn_all = _L0_gnn_setup()
    _L0_gnn_in = {k: v for k, v in _L0_gnn_all.items() if k in ('W_edge', 'b_edge', 'W_ih', 'W_hh', 'b_ih', 'b_hh')}
    del _L0_gnn_all

    def _L1_gnn_setup():
        import jax, jax.numpy as jnp
        import numpy as np
        N_NODES = 12500
        N_EDGES = 75000
        D = 128
        HID = 512
        N_GRAPHS = 16
        MLP_IN = D + 3 * D + 1
        key = jax.random.key(seed)
        ks = jax.random.split(key, 9)
        x = jax.random.normal(ks[0], (N_NODES, D), dtype=jnp.float32)
        edge_index = jax.random.randint(ks[1], (2, N_EDGES), 0, N_NODES, dtype=jnp.int64)
        edge_attr = jax.random.normal(ks[2], (N_EDGES, D), dtype=jnp.float32)
        u = jax.random.normal(ks[3], (N_GRAPHS, 1), dtype=jnp.float32)
        batch = jnp.sort(jax.random.randint(ks[4], (N_NODES,), 0, N_GRAPHS, dtype=jnp.int64))
        s1 = 1.0 / np.sqrt(MLP_IN)
        s2 = 1.0 / np.sqrt(HID)
        W1 = jax.random.uniform(ks[5], (MLP_IN, HID), jnp.float32, -s1, s1)
        b1 = jax.random.uniform(ks[6], (HID,), jnp.float32, -s1, s1)
        W2 = jax.random.uniform(ks[7], (HID, D), jnp.float32, -s2, s2)
        b2 = jax.random.uniform(ks[8], (D,), jnp.float32, -s2, s2)
        return {'x': x, 'edge_index': edge_index, 'edge_attr': edge_attr, 'u': u, 'batch': batch, 'W1': W1, 'b1': b1, 'W2': W2, 'b2': b2}
    _L1_gnn_all = _L1_gnn_setup()
    _L1_gnn_in = {k: v for k, v in _L1_gnn_all.items() if k in ('u', 'W1', 'b1', 'W2', 'b2')}
    del _L1_gnn_all

    def _L2_gnn_setup():
        import jax, jax.numpy as jnp
        import numpy as np
        N, E, R = (6250, 32000, 3)
        D_IN, D_HID, D_OUT = (128, 768, 128)

        def _p(k, shape):
            return jax.random.normal(k, shape, dtype=jnp.float32) * 0.02

        def _rgcn(x, src, tgt, edge_type, w_rel, w_root, b):
            n, r = (x.shape[0], w_rel.shape[0])
            h = jnp.einsum('ni,rio->rno', x, w_rel)
            msg = h[edge_type, src]
            seg = tgt * r + edge_type
            sums = jax.ops.segment_sum(msg, seg, num_segments=n * r).reshape(n, r, -1)
            cnt = jax.ops.segment_sum(jnp.ones(seg.shape, x.dtype), seg, num_segments=n * r).reshape(n, r, 1)
            mean = sums / jnp.maximum(cnt, 1.0)
            return mean.sum(axis=1) + x @ w_root + b
        key = jax.random.key(seed)
        ks = jax.random.split(key, 10)
        return {'x': jax.random.normal(ks[0], (N, D_IN), dtype=jnp.float32), 'edge_index': jax.random.randint(ks[1], (2, E), 0, N, dtype=jnp.int32), 'edge_type': jax.random.randint(ks[2], (E,), 0, R, dtype=jnp.int32), 'q_w1': _p(ks[3], (D_IN, D_HID)), 'q_b1': jnp.zeros((D_HID,), jnp.float32), 'q_w2': _p(ks[4], (D_HID, D_IN)), 'q_b2': jnp.zeros((D_IN,), jnp.float32), 'c1_wrel': _p(ks[5], (R, D_IN, D_HID)), 'c1_wroot': _p(ks[6], (D_IN, D_HID)), 'c1_b': jnp.zeros((D_HID,), jnp.float32), 'c2_wrel': _p(ks[7], (R, D_HID, D_OUT)), 'c2_wroot': _p(ks[8], (D_HID, D_OUT)), 'c2_b': jnp.zeros((D_OUT,), jnp.float32), 'lin_w': _p(ks[9], (D_OUT, D_OUT)), 'lin_b': jnp.zeros((D_OUT,), jnp.float32)}
    _L2_gnn_all = _L2_gnn_setup()
    _L2_gnn_in = {k: v for k, v in _L2_gnn_all.items() if k in ('q_w1', 'q_b1', 'q_w2', 'q_b2', 'c1_wrel', 'c1_wroot', 'c1_b', 'c2_wrel', 'c2_wroot', 'c2_b', 'lin_w', 'lin_b')}
    del _L2_gnn_all

    def _L3_gnn_setup():
        import jax, jax.numpy as jnp
        import numpy as np
        N = 6250
        R = 16
        D = 128
        B = 4
        d = D // B
        E = 100000

        def _rgcn_conv(x, src, dst, et, W, root, bias):
            n = x.shape[0]
            allR = jnp.einsum('nbi,rbio->rnbo', x.reshape(n, B, d), W).reshape(R, n, D)
            msg = allR[et, src]
            seg = dst * R + et
            cnt = jax.ops.segment_sum(jnp.ones_like(et, x.dtype), seg, num_segments=n * R)
            norm = 1.0 / jnp.maximum(cnt[seg], 1.0)
            agg = jax.ops.segment_sum(msg * norm[:, None], dst, num_segments=n)
            return agg + x @ root + bias
        key = jax.random.key(seed)
        ks = jax.random.split(key, 9)
        s = 1.0 / np.sqrt(D)
        return {'edge_index': jax.random.randint(ks[0], (2, E), 0, N), 'edge_type': jax.random.randint(ks[1], (E,), 0, R), 'node_emb': jax.random.normal(ks[2], (N, D), jnp.float32) * s, 'W1': jax.random.normal(ks[3], (R, B, d, d), jnp.float32) * s, 'root1': jax.random.normal(ks[4], (D, D), jnp.float32) * s, 'bias1': jax.random.normal(ks[5], (D,), jnp.float32) * 0.01, 'W2': jax.random.normal(ks[6], (R, B, d, d), jnp.float32) * s, 'root2': jax.random.normal(ks[7], (D, D), jnp.float32) * s, 'bias2': jax.random.normal(ks[8], (D,), jnp.float32) * 0.01}
    _L3_gnn_all = _L3_gnn_setup()
    _L3_gnn_in = {k: v for k, v in _L3_gnn_all.items() if k in ('W1', 'root1', 'bias1', 'W2', 'root2', 'bias2')}
    del _L3_gnn_all
    return {'x': x, 'src': src, 'dst': dst, 'edge_attr_128': edge_attr_128, 'edge_attr_4': edge_attr_4, 'edge_type_16': edge_type_16, 'edge_type_3': edge_type_3, 'L0_gnn_W_edge': _L0_gnn_in['W_edge'], 'L0_gnn_b_edge': _L0_gnn_in['b_edge'], 'L0_gnn_W_ih': _L0_gnn_in['W_ih'], 'L0_gnn_W_hh': _L0_gnn_in['W_hh'], 'L0_gnn_b_ih': _L0_gnn_in['b_ih'], 'L0_gnn_b_hh': _L0_gnn_in['b_hh'], 'L1_gnn_u': _L1_gnn_in['u'], 'L1_gnn_W1': _L1_gnn_in['W1'], 'L1_gnn_b1': _L1_gnn_in['b1'], 'L1_gnn_W2': _L1_gnn_in['W2'], 'L1_gnn_b2': _L1_gnn_in['b2'], 'L2_gnn_q_w1': _L2_gnn_in['q_w1'], 'L2_gnn_q_b1': _L2_gnn_in['q_b1'], 'L2_gnn_q_w2': _L2_gnn_in['q_w2'], 'L2_gnn_q_b2': _L2_gnn_in['q_b2'], 'L2_gnn_c1_wrel': _L2_gnn_in['c1_wrel'], 'L2_gnn_c1_wroot': _L2_gnn_in['c1_wroot'], 'L2_gnn_c1_b': _L2_gnn_in['c1_b'], 'L2_gnn_c2_wrel': _L2_gnn_in['c2_wrel'], 'L2_gnn_c2_wroot': _L2_gnn_in['c2_wroot'], 'L2_gnn_c2_b': _L2_gnn_in['c2_b'], 'L2_gnn_lin_w': _L2_gnn_in['lin_w'], 'L2_gnn_lin_b': _L2_gnn_in['lin_b'], 'L3_gnn_W1': _L3_gnn_in['W1'], 'L3_gnn_root1': _L3_gnn_in['root1'], 'L3_gnn_bias1': _L3_gnn_in['bias1'], 'L3_gnn_W2': _L3_gnn_in['W2'], 'L3_gnn_root2': _L3_gnn_in['root2'], 'L3_gnn_bias2': _L3_gnn_in['bias2']}

def reference(x, src, dst, edge_attr_128, edge_attr_4, edge_type_16, edge_type_3, L0_gnn_W_edge, L0_gnn_b_edge, L0_gnn_W_ih, L0_gnn_W_hh, L0_gnn_b_ih, L0_gnn_b_hh, L1_gnn_u, L1_gnn_W1, L1_gnn_b1, L1_gnn_W2, L1_gnn_b2, L2_gnn_q_w1, L2_gnn_q_b1, L2_gnn_q_w2, L2_gnn_q_b2, L2_gnn_c1_wrel, L2_gnn_c1_wroot, L2_gnn_c1_b, L2_gnn_c2_wrel, L2_gnn_c2_wroot, L2_gnn_c2_b, L2_gnn_lin_w, L2_gnn_lin_b, L3_gnn_W1, L3_gnn_root1, L3_gnn_bias1, L3_gnn_W2, L3_gnn_root2, L3_gnn_bias2):
    import jax
    import jax.numpy as jnp

    def _L0_gnn_ref(node_feat, edge_index, edge_feat, W_edge, b_edge, W_ih, W_hh, b_ih, b_hh):
        import jax, jax.numpy as jnp
        import numpy as np
        N_NODES = 12500
        N_EDGES = 200000
        HIDDEN = 128
        N_ETYPES = 4
        N_STEPS = 4

        def _gru_cell(x, h, W_ih, W_hh, b_ih, b_hh):
            gi = x @ W_ih.T + b_ih
            gh = h @ W_hh.T + b_hh
            ir, iz, inn = jnp.split(gi, 3, axis=1)
            hr, hz, hn = jnp.split(gh, 3, axis=1)
            r = jax.nn.sigmoid(ir + hr)
            z = jax.nn.sigmoid(iz + hz)
            n = jnp.tanh(inn + r * hn)
            return (1.0 - z) * n + z * h
        etypes = jnp.argmax(edge_feat, axis=1)
        src, dst = (edge_index[0], edge_index[1])
        N = node_feat.shape[0]
        h = node_feat
        for _ in range(N_STEPS):
            trans = jnp.einsum('nd,tod->tno', h, W_edge) + b_edge[:, None, :]
            msg = trans[etypes, src]
            a = jax.ops.segment_sum(msg, dst, num_segments=N)
            h = _gru_cell(a, h, W_ih, W_hh, b_ih, b_hh)
        return h

    def _L1_gnn_ref(x, edge_index, edge_attr, u, batch, W1, b1, W2, b2):
        import jax, jax.numpy as jnp
        import numpy as np
        N_NODES = 12500
        N_EDGES = 75000
        D = 128
        HID = 512
        N_GRAPHS = 16
        MLP_IN = D + 3 * D + 1
        N = x.shape[0]
        row = edge_index[0]
        ones = jnp.ones((edge_attr.shape[0], 1), dtype=edge_attr.dtype)
        cnt = jax.ops.segment_sum(ones, row, num_segments=N)
        agg_sum = jax.ops.segment_sum(edge_attr, row, num_segments=N)
        agg_max = jax.ops.segment_max(edge_attr, row, num_segments=N)
        agg_max = jnp.where(cnt > 0, agg_max, jnp.zeros((), edge_attr.dtype))
        agg_mean = agg_sum / jnp.maximum(cnt, 1.0)
        h = jnp.concatenate([x, agg_sum, agg_max, agg_mean, u[batch]], axis=1)
        h = jax.nn.relu(h @ W1 + b1) @ W2 + b2
        return h + x

    def _L2_gnn_ref(x, edge_index, edge_type, q_w1, q_b1, q_w2, q_b2, c1_wrel, c1_wroot, c1_b, c2_wrel, c2_wroot, c2_b, lin_w, lin_b):
        import jax, jax.numpy as jnp
        import numpy as np
        N, E, R = (6250, 32000, 3)
        D_IN, D_HID, D_OUT = (128, 768, 128)

        def _p(k, shape):
            return jax.random.normal(k, shape, dtype=jnp.float32) * 0.02

        def _rgcn(x, src, tgt, edge_type, w_rel, w_root, b):
            n, r = (x.shape[0], w_rel.shape[0])
            h = jnp.einsum('ni,rio->rno', x, w_rel)
            msg = h[edge_type, src]
            seg = tgt * r + edge_type
            sums = jax.ops.segment_sum(msg, seg, num_segments=n * r).reshape(n, r, -1)
            cnt = jax.ops.segment_sum(jnp.ones(seg.shape, x.dtype), seg, num_segments=n * r).reshape(n, r, 1)
            mean = sums / jnp.maximum(cnt, 1.0)
            return mean.sum(axis=1) + x @ w_root + b
        src, tgt = (edge_index[0], edge_index[1])
        q = jax.nn.relu(x @ q_w1 + q_b1) @ q_w2 + q_b2
        h = jax.nn.relu(_rgcn(q, src, tgt, edge_type, c1_wrel, c1_wroot, c1_b))
        h = jax.nn.relu(_rgcn(h, src, tgt, edge_type, c2_wrel, c2_wroot, c2_b))
        return h @ lin_w + lin_b

    def _L3_gnn_ref(edge_index, edge_type, node_emb, W1, root1, bias1, W2, root2, bias2):
        import jax, jax.numpy as jnp
        import numpy as np
        N = 6250
        R = 16
        D = 128
        B = 4
        d = D // B
        E = 100000

        def _rgcn_conv(x, src, dst, et, W, root, bias):
            n = x.shape[0]
            allR = jnp.einsum('nbi,rbio->rnbo', x.reshape(n, B, d), W).reshape(R, n, D)
            msg = allR[et, src]
            seg = dst * R + et
            cnt = jax.ops.segment_sum(jnp.ones_like(et, x.dtype), seg, num_segments=n * R)
            norm = 1.0 / jnp.maximum(cnt[seg], 1.0)
            agg = jax.ops.segment_sum(msg * norm[:, None], dst, num_segments=n)
            return agg + x @ root + bias
        src, dst = (edge_index[0], edge_index[1])
        h = _rgcn_conv(node_emb, src, dst, edge_type, W1, root1, bias1)
        h = jax.nn.relu(h)
        return _rgcn_conv(h, src, dst, edge_type, W2, root2, bias2)
    edge_index = jnp.stack([src, dst])
    batch0 = jnp.zeros((6250,), jnp.int32)
    h = jnp.maximum(_layernorm(x, axis=-1), 0.0)
    x = x + _L0_gnn_ref(h, edge_index, edge_attr_4, L0_gnn_W_edge, L0_gnn_b_edge, L0_gnn_W_ih, L0_gnn_W_hh, L0_gnn_b_ih, L0_gnn_b_hh)
    h = jnp.maximum(_layernorm(x, axis=-1), 0.0)
    x = x + _L1_gnn_ref(h, edge_index, edge_attr_128, L1_gnn_u, batch0, L1_gnn_W1, L1_gnn_b1, L1_gnn_W2, L1_gnn_b2)
    h = jnp.maximum(_layernorm(x, axis=-1), 0.0)
    x = x + _L2_gnn_ref(h, edge_index, edge_type_3, L2_gnn_q_w1, L2_gnn_q_b1, L2_gnn_q_w2, L2_gnn_q_b2, L2_gnn_c1_wrel, L2_gnn_c1_wroot, L2_gnn_c1_b, L2_gnn_c2_wrel, L2_gnn_c2_wroot, L2_gnn_c2_b, L2_gnn_lin_w, L2_gnn_lin_b)
    h = jnp.maximum(_layernorm(x, axis=-1), 0.0)
    x = x + _L3_gnn_ref(edge_index, edge_type_16, h, L3_gnn_W1, L3_gnn_root1, L3_gnn_bias1, L3_gnn_W2, L3_gnn_root2, L3_gnn_bias2)
    return x

_drawn_inputs = setup_inputs


def setup_inputs(seed=0):
    import zlib

    import numpy as np

    out = dict(_drawn_inputs(seed))
    spreads = {'L2_gnn_q_b1': (0.0, 0.8),
     'L2_gnn_q_b2': (0.0, 0.8),
     'L2_gnn_c1_b': (0.0, 0.8),
     'L2_gnn_c2_b': (0.0, 2.0),
     'L2_gnn_lin_b': (0.0, 2.0)}
    factors = {'L1_gnn_u': 23.426,
     'L1_gnn_b1': 8.0,
     'L1_gnn_b2': 4.311,
     'L2_gnn_q_w1': 8.0,
     'L2_gnn_q_w2': 8.0,
     'L2_gnn_c1_wrel': 8.0,
     'L2_gnn_c1_wroot': 8.0,
     'L2_gnn_c2_wrel': 8.0,
     'L2_gnn_c2_wroot': 8.0,
     'L2_gnn_lin_w': 5.136,
     'L3_gnn_bias1': 64.0,
     'L3_gnn_bias2': 200.0,
     'L0_gnn_b_hh': 2.968,
     'L3_gnn_W1': 3.916,
     'L3_gnn_root1': 5.35,
     'L3_gnn_W2': 3.362,
     'L3_gnn_root2': 4.878}
    for name, (base, spread) in spreads.items():
        noise = np.random.default_rng([zlib.crc32(name.encode()), seed]).standard_normal(out[name].shape)
        drawn = base * np.exp(spread * noise) if base else spread * noise
        out[name] = jnp.asarray(drawn.astype(out[name].dtype))
    for name, factor in factors.items():
        out[name] = (out[name] * factor).astype(out[name].dtype)
    return out
```

```python
import math
from contextlib import ExitStack

import concourse.bass as bass
from concourse import mybir

F32 = mybir.dt.float32
I32 = mybir.dt.int32
U8 = mybir.dt.uint8
BF16 = mybir.dt.bfloat16
ALU = mybir.AluOpType
ACT = mybir.ActivationFunctionType

P = 128
D = 128
N = 6250
E = 100000
BLOCKS = math.ceil(N / P)
LAST = N - (BLOCKS - 1) * P
PAIR = 2 * P
STEPS = math.ceil(N / PAIR)
NB = 2 * STEPS
NP = NB * P
J = 16
GROUPS = math.ceil(E / (P * J))
TAIL = (E - (GROUPS - 1) * P * J) // J
EC = GROUPS * J
T = 16 * math.ceil((math.ceil(E / P) + BLOCKS - 1) / 16)
U = 16
PADT = 52
AHEAD = 2
SLOTS = P * T
NONE = P
ROW = D + 2
HALF = 8
BIG = 2.0 ** 126
FMAX = 3.4028234663852886e38
EPS = 1e-5
T4, T3, T16 = 4, 3, 16
RT = T16 + T3
H1, H2 = 512, 768
C1, C2 = H1 // P, H2 // P
SRC_BITS, LO_BITS = 13, 8
LO_AT, E4_AT, E3_AT, E16_AT = 13, 21, 23, 25


class Count:

    def __init__(self, sem, unit=1):
        self.sem, self.unit, self.base = sem, unit, 0

    def at(self, n):
        return n * self.unit + self.base

    def done(self, n):
        self.base += n * self.unit


def stepped(eng, total, unroll, step, peel=1):
    turns = total // unroll - peel
    for i in range(peel * unroll):
        step(i, i % unroll)
    with eng.Fori(0, turns) as q:
        for s in range(unroll):
            step(q * unroll + (peel * unroll + s), s)
    for i in range(unroll * (turns + peel), total):
        step(i, i % unroll)


def cut(i, n):
    return slice(i, i + n) if isinstance(i, int) else bass.ds(i, n)


def first(i, n):
    return isinstance(i, int) and i < n


def build(nc, a, out):
    ctx = ExitStack()
    sems = {}

    def sem(name, unit=1):
        if name not in sems:
            sems[name] = Count(ctx.enter_context(nc.semaphore(name)), unit)
        return sems[name]

    names = {}

    def sb(name, shape, dt=F32, to=None):
        names[name] = names.get(name, 0) + 1
        name += f"_{names[name]}" if names[name] > 1 else ""
        return (to or ctx).enter_context(nc.sbuf_tensor(name, shape, dt))

    ds = bass.ds
    with ctx:
        edge_list = nc.dram_tensor("edge_list", [SLOTS, 1], I32, kind="Internal").ap()
        attr_rows = nc.dram_tensor("attr_rows", [SLOTS, ROW], F32, kind="Internal").ap()
        table4 = nc.dram_tensor("table4", [NP * T4, D], F32, kind="Internal").ap()
        table1 = nc.dram_tensor("table1", [NP, D], F32, kind="Internal").ap()
        table3 = nc.dram_tensor("table3", [NP * T3, D], F32, kind="Internal").ap()
        table16 = nc.dram_tensor("table16", [NP * T16, D], F32, kind="Internal").ap()

        xT = sb("xT", [P, NP])
        hT = sb("hT", [P, NP])
        big = sb("big", [P, 3 * NP])
        sumT = big[:, 0:NP]
        attr_sumT = big[:, NP:2 * NP]
        attr_max = big[:, 2 * NP:3 * NP]
        words = sb("words", [P, T], I32)
        idx = sb("idx", [P, T], I32)
        node = sb("node", [P, T + AHEAD])
        w3 = sb("w3", [P, T + AHEAD])
        w16 = sb("w16", [P, T + AHEAD])
        block_dst = sb("block_dst", [1, T], I32)
        block_src = sb("block_src", [1, T], I32)
        attr_count = sb("attr_count", [P, NB])
        rel_inv = sb("rel_inv", [P, NB, RT])
        iota = sb("iota", [P, T3 * P])
        ident = sb("ident", [P, P])
        ones = sb("ones", [P, P])
        mean_w = sb("mean_w", [P, P])
        pidx = sb("pidx", [P, 1])
        eps = sb("eps", [P, 1])
        ps = ctx.enter_context(nc.psum_tensor("ps", [P, 8, 512], F32))

        def grouped(ap, width=1):
            flat = ap if len(ap.shape) == 1 else ap.rearrange("e w -> (e w)")
            whole = (GROUPS - 1) * P * J * width
            return (flat[0:whole].rearrange("(g p j) -> p g j", p=P, j=J * width),
                    flat[whole:E * width].rearrange("(p j) -> p j", j=J * width))

        tmp_i1 = sb("tmp_i1", [P, T], I32)

        n_add, n_mean, n_dev, n_sq = sem("n_add"), sem("n_mean"), sem("n_dev"), sem("n_sq")
        n_var, n_sd, n_rec, n_out = sem("n_var"), sem("n_sd"), sem("n_rec"), sem("n_out")
        h_ready, t_mm, t_ev = sem("h_ready"), sem("t_mm"), sem("t_ev")
        t_dma = [sem("t_dma0", 16), sem("t_dma1", 16)]
        bufs = {}

        def col(i):
            return cut(i * PAIR, PAIR)

        def norm_bufs(to):
            bufs["dev"] = sb("dev", [P, 2, PAIR], F32, to)
            bufs["sq"] = sb("sq", [P, 2, PAIR], F32, to)
            bufs["sd"] = sb("sd", [P, 2, PAIR], F32, to)

        def norm_pe(pe, add=False):
            def variance(j, s):
                pe.wait_ge(n_sq.sem, n_sq.at(j + 1))
                if not first(j, 2):
                    pe.wait_ge(n_sd.sem, n_sd.at(j - 1))
                nc.tensor.matmul(ps[:, 2 + s, 0:PAIR], lhsT=mean_w[:], rhs=bufs["sq"][:, s, :],
                                 start=True, stop=True).then_inc(n_var.sem, 1)

            def step(i, s):
                if add:
                    pe.wait_ge(n_add.sem, n_add.at(i + 1))
                if not first(i, 2):
                    pe.wait_ge(n_dev.sem, n_dev.at(i - 1))
                nc.tensor.matmul(ps[:, s, 0:PAIR], lhsT=mean_w[:], rhs=xT[:, col(i)],
                                 start=True, stop=True).then_inc(n_mean.sem, 1)
                if not first(i, 1):
                    variance(i - 1, 1 - s)

            stepped(pe, STEPS, 2, step, peel=2)
            variance(STEPS - 1, (STEPS - 1) % 2)

        def norm_act(act):
            def deviation(j, s):
                act.wait_ge(n_var.sem, n_var.at(j + 1))
                if not first(j, 2):
                    act.wait_ge(n_rec.sem, n_rec.at(j - 1))
                act.activation(bufs["sd"][:, s, :], ps[:, 2 + s, 0:PAIR], ACT.Sqrt, bias=eps[:, 0:1])\
                    .then_inc(n_sd.sem, 1)

            def step(i, s):
                act.wait_ge(n_dev.sem, n_dev.at(i + 1))
                if not first(i, 2):
                    act.wait_ge(n_var.sem, n_var.at(i - 1))
                act.activation(bufs["sq"][:, s, :], bufs["dev"][:, s, :], ACT.Square).then_inc(n_sq.sem, 1)
                if not first(i, 1):
                    deviation(i - 1, 1 - s)

            stepped(act, STEPS, 2, step, peel=2)
            deviation(STEPS - 1, (STEPS - 1) % 2)

        def norm_dve(v, add=False):
            def output(j, s):
                v.wait_ge(n_sd.sem, n_sd.at(j + 1))
                v.reciprocal(bufs["sd"][:, s, :], bufs["sd"][:, s, :]).then_inc(n_rec.sem, 1)
                v.wait_ge(n_rec.sem, n_rec.at(j + 1))
                v.scalar_tensor_tensor(hT[:, col(j)], bufs["dev"][:, s, :], 0.0, bufs["sd"][:, s, :],
                                       ALU.max, ALU.mult).then_inc(n_out.sem, 1)

            def step(i, s):
                if add:
                    v.tensor_tensor(xT[:, col(i)], xT[:, col(i)], hT[:, col(i)], ALU.add).then_inc(n_add.sem, 1)
                v.wait_ge(n_mean.sem, n_mean.at(i + 1))
                if not first(i, 2):
                    v.wait_ge(n_out.sem, n_out.at(i - 1))
                    v.wait_ge(n_sq.sem, n_sq.at(i - 1))
                v.tensor_tensor(bufs["dev"][:, s, :], xT[:, col(i)], ps[:, s, 0:PAIR], ALU.subtract)\
                    .then_inc(n_dev.sem, 1)
                if not first(i, 1):
                    output(i - 1, 1 - s)

            stepped(v, STEPS, 2, step, peel=2)
            output(STEPS - 1, (STEPS - 1) % 2)

        def norm_over(add=False):
            for c in (n_mean, n_dev, n_sq, n_var, n_sd, n_rec, n_out) + ((n_add,) if add else ()):
                c.done(STEPS)

        def table_bufs(to, width):
            bufs["h"] = sb("h_now", [P, 2, PAIR], F32, to)
            bufs["rows"] = sb("table_rows", [P, 2, 2, width], F32, to)

        def table_pe(pe, i, s, w, width):
            pe.wait_ge(h_ready.sem, h_ready.at(i + 1))
            if not first(i, 2):
                pe.wait_ge(t_ev.sem, t_ev.at(i - 1))
            for j in range(2):
                h = bufs["h"][:, s, j * P:(j + 1) * P]
                if w is None:
                    last = pe.transpose(ps[:, 4 + 2 * s + j, 0:P], h, ident[:])
                else:
                    last = nc.tensor.matmul(ps[:, 4 + 2 * s + j, 0:width], lhsT=h, rhs=w, start=True, stop=True)
            last.then_inc(t_mm.sem, 1)

        def table_dve(v, i, s, bias, width):
            v.wait_ge(t_mm.sem, t_mm.at(i + 1))
            if not first(i, 2):
                v.wait_ge(t_dma[s].sem, (i - s) * 8 + t_dma[s].base)
            for j in range(2):
                to, rows = bufs["rows"][:, s, j, :], ps[:, 4 + 2 * s + j, 0:width]
                last = v.tensor_copy(to, rows) if bias is None else v.tensor_tensor(to, rows, bias, ALU.add)
            last.then_inc(t_ev.sem, 1)

        def table_store(eng, i, s, table, width):
            eng.wait_ge(t_ev.sem, t_ev.at(i + 1))
            eng.dma_start(table.rearrange("(b p r) d -> p b (r d)", p=P, r=width // D)[:, cut(2 * i, 2), :],
                          bufs["rows"][:, s, :, :]).then_inc(t_dma[s].sem, 16)

        def table_stored(eng):
            for s in range(2):
                eng.wait_ge(t_dma[s].sem, t_dma[s].at((STEPS + 1 - s) // 2))

        def table_over():
            for c in (h_ready, t_mm, t_ev):
                c.done(STEPS)
            for s in range(2):
                t_dma[s].done((STEPS + 1 - s) // 2)

        def table_rows(v, chain, at, mask, r):
            chain(v.tensor_scalar(idx[:], words[:], (1 << SRC_BITS) - 1, None, ALU.bitwise_and))
            if r > 1:
                chain(v.tensor_scalar(tmp_i1[:], words[:], at, mask, ALU.logical_shift_right, ALU.bitwise_and))
                chain(v.scalar_tensor_tensor(idx[:], idx[:], float(r), tmp_i1[:], ALU.mult, ALU.add))

        done_chain = [0]
        l0 = ctx.enter_context(ExitStack())
        type3 = sb("type3", [P, T], F32, l0)
        type16 = sb("type16", [P, T], F32, l0)
        gate_w = sb("gate_w", [P, 10, P], F32, l0)
        edge_w = gate_w[:, 6:10, :].rearrange("p t o -> p (t o)")
        edge_bias = sb("edge_bias", [P, T4 * D], F32, l0)
        b_ih = sb("b_ih", [P, 3], F32, l0)
        b_hh = sb("b_hh", [P, 3], F32, l0)
        b_rz = sb("b_rz", [P, 2], F32, l0)

        with ExitStack() as ph:
            addr_src = sb("addr_src", [P, EC], I32, ph)
            lo_src = sb("lo_src", [P, EC], F32, ph)
            with ExitStack() as ph2:
                dst_i = sb("dst_i", [P, EC], I32, ph2)
                src_i = sb("src_i", [P, EC], I32, ph2)
                word = sb("word", [P, EC], I32, ph2)
                tmp_i = sb("tmp_i", [P, EC], I32, ph2)
                tmp2_i = sb("tmp2_i", [P, EC], I32, ph2)
                addr_dst = sb("addr_dst", [P, EC], I32, ph2)
                attr4 = big[:, 2 * NP:2 * NP + 4 * EC]
                best = hT[:, 0:EC]
                less = hT[:, EC:2 * EC]
                rank = hT[:, 2 * EC:4 * EC].rearrange("p (s c) -> p s c", s=2)
                after = xT[:, 0:T]
                iota_t = xT[:, T:2 * T]
                pad_word = xT[:, 2 * T:3 * T].bitcast(I32)
                ones_row = xT[:, 3 * T:3 * T + EC]
                t3_i = xT[:, 4 * T:4 * T + EC].bitcast(I32)
                t16_i = xT[:, 5 * T:5 * T + EC].bitcast(I32)
                bin_f = sb("bin_f", [P, EC], BF16, ph2)
                place = sb("place", [P, EC], F32, ph2)
                strict = sb("strict", [P, P], F32, ph2)
                bins = sb("bins", [P, BLOCKS], F32, ph2)
                count = sb("count", [P, BLOCKS], F32, ph2)
                small = sb("small", [P, 4, BLOCKS], F32, ph2)
                small_i = sb("small_i", [P, BLOCKS], I32, ph2)
                tot = sb("tot", [P, 4], F32, ph2)
                tot_i = sb("tot_i", [P, 1], I32, ph2)
                addr_now = sb("addr_now", [P, 2, J], I32, ph2)
                word_now = sb("word_now", [P, 2, J], I32, ph2)
                member = big[:, 0:(BLOCKS * EC + 3) // 4].bitcast(U8)
                s_keys, s_types, s_pad = sem("keys"), sem("types"), sem("pad_list", 16)
                s_const, s_zero, s_chain = sem("const"), sem("zeroed"), sem("prep_chain")
                s_count, s_prefix, s_col, s_colp = sem("counted"), sem("prefix"), sem("col"), sem("col_prefix")
                s_after, s_blk, s_addr = sem("after"), sem("blk"), sem("addr")
                s_copy, s_scat, s_go = sem("addr_copy"), [sem("scat0"), sem("scat1")], sem("pool_go")
                s_rank, s_base = sem("ranked"), sem("base")
                with nc.Block() as block:
                    @block.sync
                    def _(sp):
                        sp.wait_ge(s_zero.sem, 1)
                        for t, ap in ((dst_i, a["dst"]), (src_i, a["src"])):
                            whole, rest = grouped(ap)
                            sp.dma_start(t[:, 0:EC - J].rearrange("p (g j) -> p g j", j=J), whole)\
                                .then_inc(s_keys.sem, 16)
                            sp.dma_start(t[0:TAIL, EC - J:EC], rest).then_inc(s_keys.sem, 16)
                        sp.wait_ge(s_zero.sem, 2)
                        for t, ap, w in ((t3_i, a["edge_type_3"], 1), (t16_i, a["edge_type_16"], 1),
                                         (attr4, a["edge_attr_4"], 4)):
                            whole, rest = grouped(ap, w)
                            sp.dma_start(t[:, 0:(EC - J) * w].rearrange("p (g j) -> p g j", j=J * w), whole)\
                                .then_inc(s_types.sem, 16)
                            sp.dma_start(t[0:TAIL, (EC - J) * w:EC * w], rest).then_inc(s_types.sem, 16)
                        sp.dma_start(edge_list.rearrange("(p t) o -> p (t o)", p=P), pad_word[:])\
                            .then_inc(s_pad.sem, 16)

                    @block.gpsimd
                    def _(g):
                        c = s_const.sem
                        for k, ins in enumerate((
                            lambda: g.iota(iota[:], [[1, T3 * P]], base=0, channel_multiplier=0,
                                           allow_small_or_imprecise_dtypes=True),
                            lambda: g.iota(iota_t[:], [[1, T]], base=0, channel_multiplier=0,
                                           allow_small_or_imprecise_dtypes=True),
                            lambda: g.iota(bins[:], [[1, BLOCKS]], base=0, channel_multiplier=0,
                                           allow_small_or_imprecise_dtypes=True),
                            lambda: g.iota(pidx[:], [[0, 1]], base=0, channel_multiplier=1,
                                           allow_small_or_imprecise_dtypes=True),
                            lambda: g.memset(ident[:], 0.0),
                            lambda: g.memset(strict[:], 1.0),
                            lambda: g.memset(ones[:], 1.0),
                            lambda: g.memset(mean_w[:], 1.0 / D),
                            lambda: g.memset(eps[:], EPS),
                            lambda: g.memset(ones_row[:], 1.0),
                        )):
                            ins().then_inc(c, 1)
                        g.wait_ge(c, 10)
                        g.affine_select(out=ident[:], in_=ident[:], compare_op=ALU.not_equal, fill=1.0,
                                        base=0, pattern=[[-1, P]], channel_multiplier=1).then_inc(c, 1)
                        g.affine_select(out=strict[:], in_=strict[:], compare_op=ALU.is_gt, fill=0.0,
                                        base=0, pattern=[[1, P]], channel_multiplier=-1).then_inc(c, 1)
                        g.wait_ge(s_pad.sem, 16)
                        g.wait_ge(s_addr.sem, 1)

                        def group(i, s):
                            parts = TAIL if isinstance(i, int) and i == GROUPS - 1 else P
                            if not first(i, 2):
                                g.wait_ge(s_scat[s].sem, (i - s) * (8 * J))
                                g.sem_inc(s_go.sem, 1)
                            g.tensor_copy(addr_now[:, s, :], addr_dst[:, cut(i * J, J)]).then_inc(s_copy.sem, 1)
                            g.tensor_copy(word_now[:, s, :], word[:, cut(i * J, J)]).then_inc(s_copy.sem, 1)
                            g.wait_ge(s_copy.sem, i * 2 + 2)
                            g.sem_inc(s_go.sem, 1)
                            for j in range(J):
                                g.indirect_dma_start(
                                    edge_list, bass.IndirectOffsetOnAxis(ap=addr_now[0:parts, s, j:j + 1], axis=0),
                                    word_now[0:parts, s, j:j + 1], None).then_inc(s_scat[s].sem, 16)

                        stepped(g, GROUPS, 2, group)
                        g.wait_ge(s_scat[0].sem, 16 * J * ((GROUPS + 1) // 2))
                        g.wait_ge(s_scat[1].sem, 16 * J * (GROUPS // 2))

                    @block.tensor
                    def _(pe):
                        pe.wait_ge(s_const.sem, 12)
                        for o in range(2):
                            pe.wait_ge(s_count.sem, (o + 1) * BLOCKS)
                            nc.tensor.matmul(ps[:, 0, 0:BLOCKS], lhsT=strict[:], rhs=count[:], start=True, stop=True)
                            nc.tensor.matmul(ps[:, 1, 0:BLOCKS], lhsT=ones[:], rhs=count[:], start=True, stop=True)
                            nc.tensor.matmul(ps[0:BLOCKS, 2, 0:1], lhsT=count[:], rhs=ones[:, 0:1],
                                             start=True, stop=True).then_inc(s_prefix.sem, 1)
                            pe.wait_ge(s_col.sem, o + 1)
                            nc.tensor.matmul(ps[0:BLOCKS, 3, 0:1], lhsT=strict[0:BLOCKS, 0:BLOCKS],
                                             rhs=tot[0:BLOCKS, 0:1], start=True, stop=True).then_inc(s_colp.sem, 1)
                            pe.wait_ge(s_after.sem, o + 1)
                            for q in range(2):
                                last = nc.tensor.matmul(ps[0:1, 4 + q, 0:T // 2], lhsT=ones[0:BLOCKS, 0:1],
                                                        rhs=after[0:BLOCKS, q * (T // 2):(q + 1) * (T // 2)],
                                                        start=True, stop=True)
                            last.then_inc(s_blk.sem, 1)

                    @block.vector
                    def _(v):
                        n = [0]

                        def chain(ins):
                            n[0] += 1
                            ins.then_inc(s_chain.sem, 1)
                            v.wait_ge(s_chain.sem, s_chain.at(n[0]))

                        v.memset(dst_i[:], -P)
                        v.memset(src_i[:], -P).then_inc(s_zero.sem, 1)
                        v.memset(t3_i[:], 0)
                        v.memset(t16_i[:], 0)
                        v.memset(attr4[:], 0.0)
                        v.memset(pad_word[:], NONE << LO_AT).then_inc(s_zero.sem, 1)
                        chain(v.memset(place[:], 0.0))
                        v.wait_ge(s_const.sem, 12)

                        def order(o, key, addr, blk):
                            chain(v.tensor_scalar(tmp_i[:], key[:], 7, None, ALU.arith_shift_right))
                            chain(v.tensor_copy(bin_f[:], tmp_i[:]))

                            def count_bin(b, s):
                                v.tensor_scalar(member[:, cut(b * EC, EC)], bin_f[:], bins[:, cut(b, 1)], None,
                                                ALU.is_equal, ALU.add, accum_out=count[:, cut(b, 1)])\
                                    .then_inc(s_count.sem, 1)

                            stepped(v, BLOCKS, 7, count_bin)
                            v.wait_ge(s_prefix.sem, o + 1)
                            chain(v.tensor_copy(small_i[:], ps[:, 1, 0:BLOCKS]))
                            chain(v.tensor_scalar(small_i[:], small_i[:], P - 1, None, ALU.add))
                            chain(v.tensor_scalar(small_i[:], small_i[:], 7, None, ALU.arith_shift_right))
                            chain(v.tensor_copy(small[:, 0, :], small_i[:]))
                            chain(v.tensor_tensor_scan(small[:, 1, :], ones_row[:, 0:BLOCKS], small[:, 0, :], 0.0,
                                                       ALU.mult, ALU.add))
                            chain(v.tensor_tensor(small[:, 2, :], small[:, 1, :], small[:, 0, :], ALU.subtract))
                            chain(v.tensor_scalar(small[:, 1, :], small[:, 2, :], float(P), -1.0, ALU.mult, ALU.add))
                            chain(v.tensor_tensor(small[:, 3, :], small[:, 1, :], ps[:, 0, 0:BLOCKS], ALU.add))
                            chain(v.tensor_copy(tot_i[0:BLOCKS, :], ps[0:BLOCKS, 2, 0:1]))
                            chain(v.tensor_scalar(tot_i[0:BLOCKS, :], tot_i[0:BLOCKS, :], P - 1, None, ALU.add))
                            chain(v.tensor_scalar(tot_i[0:BLOCKS, :], tot_i[0:BLOCKS, :], 7, None, ALU.arith_shift_right))
                            v.tensor_copy(tot[0:BLOCKS, 0:1], tot_i[0:BLOCKS, :]).then_inc(s_col.sem, 1)
                            v.wait_ge(s_colp.sem, o + 1)
                            chain(v.tensor_copy(tot[0:BLOCKS, 1:2], ps[0:BLOCKS, 3, 0:1]))
                            v.tensor_scalar(after[0:BLOCKS, :], iota_t[0:BLOCKS, :], tot[0:BLOCKS, 1:2], None,
                                            ALU.is_ge).then_inc(s_after.sem, 1)

                            def rank_bin(b, s):
                                r = rank[:, s % 2, :]
                                m = member[:, cut(b * EC, EC)]
                                v.tensor_tensor_scan(r, ones_row[:], m, small[:, 3, cut(b, 1)], ALU.mult, ALU.add).then_inc(s_rank.sem, 1)
                                v.wait_ge(s_rank.sem, b * 3 + (1 + o * 3 * BLOCKS))
                                v.scalar_tensor_tensor(r, r, 1.0, m, ALU.mult, ALU.mult).then_inc(s_rank.sem, 1)
                                v.wait_ge(s_rank.sem, b * 3 + (2 + o * 3 * BLOCKS))
                                v.tensor_tensor(place[:], place[:], r, ALU.add).then_inc(s_rank.sem, 1)
                                v.wait_ge(s_rank.sem, b * 3 + (3 + o * 3 * BLOCKS))

                            stepped(v, BLOCKS, 7, rank_bin)
                            chain(v.tensor_copy(tmp_i[:], place[:]))
                            chain(v.tensor_scalar(tmp2_i[:], tmp_i[:], P - 1, None, ALU.bitwise_and))
                            chain(v.tensor_scalar(tmp_i[:], tmp_i[:], 7, None, ALU.arith_shift_right))
                            chain(v.scalar_tensor_tensor(addr[:], tmp2_i[:], float(T), tmp_i[:], ALU.mult, ALU.add))
                            v.wait_ge(s_blk.sem, o + 1)
                            for q in range(2):
                                h = slice(q * (T // 2), (q + 1) * (T // 2))
                                chain(v.tensor_scalar(blk[0:1, h], ps[0:1, 4 + q, 0:T // 2], -1.0, None, ALU.add))

                        v.wait_ge(s_keys.sem, 64)
                        order(0, dst_i, addr_dst, block_dst)
                        v.wait_ge(s_types.sem, 96)
                        a4 = attr4.rearrange("p (e w) -> p w e", w=4)
                        chain(v.tensor_tensor(best[:], a4[:, 0, :], a4[:, 1, :], ALU.max))
                        chain(v.tensor_tensor(best[:], best[:], a4[:, 2, :], ALU.max))
                        chain(v.tensor_tensor(best[:], best[:], a4[:, 3, :], ALU.max))
                        chain(v.tensor_tensor(place[:], a4[:, 2, :], best[:], ALU.not_equal))
                        for w in (1, 0):
                            chain(v.tensor_tensor(less[:], a4[:, w, :], best[:], ALU.not_equal))
                            chain(v.scalar_tensor_tensor(place[:], place[:], 1.0, less[:], ALU.add, ALU.mult))
                        chain(v.tensor_copy(word[:], place[:]))
                        chain(v.tensor_scalar(word[:], word[:], E4_AT, None, ALU.logical_shift_left))
                        chain(v.tensor_tensor(word[:], word[:], src_i[:], ALU.bitwise_or))
                        chain(v.tensor_scalar(tmp_i[:], dst_i[:], P - 1, LO_AT, ALU.bitwise_and, ALU.logical_shift_left))
                        chain(v.tensor_tensor(word[:], word[:], tmp_i[:], ALU.bitwise_or))
                        chain(v.tensor_scalar(tmp_i[:], t3_i[:], E3_AT, None, ALU.logical_shift_left))
                        chain(v.tensor_tensor(word[:], word[:], tmp_i[:], ALU.bitwise_or))
                        chain(v.tensor_scalar(tmp_i[:], t16_i[:], E16_AT, None, ALU.logical_shift_left))
                        chain(v.tensor_tensor(word[:], word[:], tmp_i[:], ALU.bitwise_or))
                        v.memset(place[:], 0.0).then_inc(s_addr.sem, 1)
                        chain(v.tensor_scalar(tmp_i[:], src_i[:], P - 1, None, ALU.bitwise_and))
                        chain(v.tensor_copy(lo_src[:], tmp_i[:]))
                        order(1, src_i, addr_src, block_src)
                        done_chain[0] = n[0]
                s_chain.done(done_chain[0])

            s_x, s_tp, s_tpc, s_w, s_fill = sem("x_loaded"), sem("transposed"), sem("evacuated"), sem("w_loaded"), sem("filled")
            s_padr, s_lo, s_rows = sem("pad_rows"), sem("row_ends"), [sem("rows0"), sem("rows1")]
            s_rscat, s_acopy, s_list = [sem("row_scat0"), sem("row_scat1")], sem("addr_copy2"), sem("list_loaded")
            s_unpack, s_wt, s_bb = sem("unpacked"), sem("weights_ready"), sem("bias_ready")
            rows_now = big[:, PADT * ROW:(PADT + 2 * J) * ROW].rearrange("p (s j w) -> p s j w", s=2, w=ROW)
            addr_now = sb("addr_now2", [P, 2, J], I32, ph)
            w_nat = sb("w_nat", [P, 10, P], F32, ph)
            pad_rows = big[:, 0:PADT * ROW]
            x_nat = big[:, 2 * NP:3 * NP]
            row_parts = grouped(a["edge_attr_128"], D)
            x_stage = sb("x_stage", [P, 2, D], F32, ph)
            s_xs = sem("x_staged")
            norm_bufs(ph)
            table_bufs(ph, T4 * D)
            with nc.Block() as block:
                @block.sync
                def _(sp):
                    sp.wait_ge(s_fill.sem, 1)
                    sp.dma_start(x_nat[:, 0:(BLOCKS - 1) * D].rearrange("p (b d) -> p b d", d=D),
                                 a["x"][0:(BLOCKS - 1) * P, :].rearrange("(b p) d -> p b d", p=P)).then_inc(s_x.sem, 16)
                    sp.dma_start(x_nat[0:LAST, (BLOCKS - 1) * D:BLOCKS * D], a["x"][(BLOCKS - 1) * P:N, :])\
                        .then_inc(s_x.sem, 16)
                    sp.dma_start(words[:], edge_list.rearrange("(p t) o -> p (t o)", p=P)).then_inc(s_list.sem, 16)
                    sp.dma_start(w_nat[:, 0:3, :], a["L0_gnn_W_ih"].rearrange("(c p) d -> p c d", p=P)).then_inc(s_w.sem, 16)
                    sp.dma_start(w_nat[:, 3:6, :], a["L0_gnn_W_hh"].rearrange("(c p) d -> p c d", p=P)).then_inc(s_w.sem, 16)
                    sp.dma_start(w_nat[:, 6:10, :], a["L0_gnn_W_edge"].rearrange("t o d -> o t d")).then_inc(s_w.sem, 16)
                    sp.dma_start(edge_bias[0:1, :], a["L0_gnn_b_edge"].rearrange("(o t) d -> o (t d)", o=1)).then_inc(s_w.sem, 16)
                    with nc.allow_non_contiguous_dma(reason="a few biases, one element a partition"):
                        sp.dma_start(b_ih[:], a["L0_gnn_b_ih"].rearrange("(c p) -> p c", p=P)).then_inc(s_w.sem, 16)
                        sp.dma_start(b_hh[:], a["L0_gnn_b_hh"].rearrange("(c p) -> p c", p=P)).then_inc(s_w.sem, 16)
                    sp.wait_ge(s_fill.sem, 2)
                    rows_v = attr_rows.rearrange("(p t) w -> p (t w)", p=P)
                    for q in range(T // PADT):
                        sp.dma_start(rows_v[:, q * PADT * ROW:(q + 1) * PADT * ROW], pad_rows).then_inc(s_padr.sem, 16)

                    def load(i, s):
                        if not first(i, 2):
                            sp.wait_ge(s_rscat[s].sem, (i - s) * (8 * J))
                        dst = rows_now[:, s, :, 0:D]
                        if isinstance(i, int) and i == GROUPS - 1:
                            sp.dma_start(dst[0:TAIL], row_parts[1].rearrange("p (j d) -> p j d", d=D))\
                                .then_inc(s_rows[s].sem, 16)
                        else:
                            part = row_parts[0][:, i, :] if isinstance(i, int) else \
                                row_parts[0][:, ds(i, 1), :].rearrange("p o f -> p (o f)")
                            sp.dma_start(dst, part.rearrange("p (j d) -> p j d", d=D)).then_inc(s_rows[s].sem, 16)

                    stepped(sp, GROUPS, 2, load)


                @block.gpsimd
                def _(g):
                    g.wait_ge(s_w.sem, 96)
                    g.partition_broadcast(edge_bias[:], edge_bias[0:1, :], P).then_inc(s_bb.sem, 1)
                    g.wait_ge(s_fill.sem, 3)
                    g.wait_ge(s_padr.sem, 16 * (T // PADT))

                    def group(i, s):
                        parts = TAIL if isinstance(i, int) and i == GROUPS - 1 else P
                        if not first(i, 2):
                            g.wait_ge(s_rscat[s].sem, (i - s) * (8 * J))
                            g.sem_inc(s_go.sem, 1)
                        g.tensor_copy(addr_now[:, s, :], addr_src[:, cut(i * J, J)]).then_inc(s_acopy.sem, 1)
                        g.tensor_copy(rows_now[:, s, :, D + 1:D + 2].rearrange("p j o -> p (j o)"),
                                      lo_src[:, cut(i * J, J)]).then_inc(s_acopy.sem, 1)
                        g.wait_ge(s_acopy.sem, i * 2 + 2)
                        g.wait_ge(s_rows[s].sem, (i - s) * 8 + 16)
                        g.sem_inc(s_go.sem, 1)
                        for j in range(J):
                            g.indirect_dma_start(
                                attr_rows, bass.IndirectOffsetOnAxis(ap=addr_now[0:parts, s, j:j + 1], axis=0),
                                rows_now[0:parts, s, j, :], None).then_inc(s_rscat[s].sem, 16)

                    stepped(g, GROUPS, 2, group)
                    g.wait_ge(s_rscat[0].sem, 16 * J * ((GROUPS + 1) // 2))
                    g.wait_ge(s_rscat[1].sem, 16 * J * (GROUPS // 2))

                @block.scalar
                def _(act):
                    def x_copy(b, s):
                        act.wait_ge(s_tp.sem, b + 1)
                        act.activation(xT[:, cut(b * P, P)], ps[:, s, 0:P], ACT.Copy).then_inc(s_tpc.sem, 1)

                    stepped(act, NB, 2, x_copy)
                    for k in range(10):
                        act.wait_ge(s_tp.sem, NB + k + 1)
                        act.activation(gate_w[:, k, :], ps[:, k % 2, 0:P], ACT.Copy).then_inc(s_tpc.sem, 1)
                    norm_act(act)

                    def stage(i, s):
                        if not first(i, 2):
                            act.wait_ge(t_mm.sem, t_mm.at(i - 1))
                        act.activation(bufs["h"][:, s, :], hT[:, col(i)], ACT.Copy).then_inc(h_ready.sem, 1)
                        if not first(i, 1):
                            table_store(act, i - 1, 1 - s, table4, T4 * D)

                    act.wait_ge(n_out.sem, n_out.at(STEPS))
                    stepped(act, STEPS, 2, stage, peel=2)
                    table_store(act, STEPS - 1, (STEPS - 1) % 2, table4, T4 * D)
                    table_stored(act)

                @block.tensor
                def _(pe):
                    pe.wait_ge(s_x.sem, 32)

                    def x_transpose(b, s):
                        if not first(b, 2):
                            pe.wait_ge(s_tpc.sem, b - 1)
                        pe.transpose(ps[:, s, 0:P], x_stage[:, s, :], ident[:]).then_inc(s_tp.sem, 1)
                    def x_tr(b, s):
                        pe.wait_ge(s_xs.sem, b + 1)
                        x_transpose(b, s)
                    stepped(pe, NB, 2, x_tr)
                    pe.wait_ge(s_w.sem, 96)
                    for k in range(10):
                        pe.wait_ge(s_tpc.sem, NB + k - 1)
                        pe.transpose(ps[:, k % 2, 0:P], w_nat[:, k, :], ident[:]).then_inc(s_tp.sem, 1)
                    pe.wait_ge(s_tpc.sem, NB + 10)
                    norm_pe(pe)
                    pe.wait_ge(n_out.sem, n_out.at(STEPS))
                    stepped(pe, STEPS, 2, lambda i, s: table_pe(pe, i, s, edge_w, T4 * D))

                @block.vector
                def _(v):
                    v.memset(x_nat[:, (BLOCKS - 1) * D:NB * D], 0.0).then_inc(s_fill.sem, 1)
                    v.memset(pad_rows, 0.0).then_inc(s_unpack.sem, 1)
                    v.wait_ge(s_unpack.sem, 1)
                    v.memset(pad_rows.rearrange("p (t w) -> p t w", w=ROW)[:, :, D + 1:D + 2], float(NONE)).then_inc(s_fill.sem, 1)
                    v.memset(rows_now[:, :, :, D:D + 1].rearrange("p s j o -> p (s j) o"), 1.0).then_inc(s_fill.sem, 1)
                    v.wait_ge(s_x.sem, 32)

                    def x_to_stage(b, s):
                        if not first(b, 2):
                            v.wait_ge(s_tp.sem, b - 1)
                        v.tensor_copy(x_stage[:, s, :], x_nat[:, cut(b * D, D)]).then_inc(s_xs.sem, 1)

                    stepped(v, NB, 2, x_to_stage)
                    v.wait_ge(s_tpc.sem, NB)
                    norm_dve(v)
                    v.wait_ge(s_bb.sem, 1)
                    stepped(v, STEPS, 2, lambda i, s: table_dve(v, i, s, edge_bias[:], T4 * D))
                    v.wait_ge(s_list.sem, 16)
                    n = [0]

                    def chain(ins):
                        n[0] += 1
                        ins.then_inc(s_chain.sem, 1)
                        v.wait_ge(s_chain.sem, s_chain.at(n[0]))

                    v.memset(node[:, T:T + AHEAD], float(NONE))
                    v.memset(w3[:, T:T + AHEAD], 0.0)
                    v.memset(w16[:, T:T + AHEAD], 0.0)
                    for to, at, mask in ((node[:, 0:T], LO_AT, (1 << LO_BITS) - 1), (type3[:], E3_AT, 3),
                                         (type16[:], E16_AT, 15)):
                        chain(v.tensor_scalar(tmp_i1[:], words[:], at, mask, ALU.logical_shift_right, ALU.bitwise_and))
                        chain(v.tensor_copy(to, tmp_i1[:]))
                    table_rows(v, chain, E4_AT, 3, T4)
                    v.tensor_tensor(b_rz[:], b_ih[:, 0:2], b_hh[:, 0:2], ALU.add)
                    done_chain[0] = n[0]
            norm_over()
            table_over()
            s_chain.done(done_chain[0])

        s_idx, s_got = sem("index_copied"), [sem(f"got{k}", 16) for k in range(U)]
        g_oh, g_mm, g_add = sem("one_hot"), sem("summed"), sem("added")

        def gather_bufs(to, width=P):
            bufs["msg"] = sb("msg", [P, U, D], F32, to)
            bufs["oh"] = sb("oh", [P, 4, width], F32, to)
            bufs["idx_now"] = sb("idx_now", [P, 2, HALF], I32, to)

        def gather_pool(g, table):
            def turn(c, _):
                for s in range(U):
                    h = s // HALF
                    if s % HALF == 0:
                        if not first(c, 1):
                            g.wait_ge(g_mm.sem, g_mm.at(c * U + (s + HALF - U)))
                            g.sem_inc(s_go.sem, 1)
                        g.tensor_copy(bufs["idx_now"][:, h, :], idx[:, cut(c * U + s, HALF)])\
                            .then_inc(s_idx.sem, 1)
                        g.wait_ge(s_idx.sem, s_idx.at(c * 2 + (h + 1)))
                        g.sem_inc(s_go.sem, 1)
                    g.indirect_dma_start(
                        bufs["msg"][:, s, :], None, table,
                        bass.IndirectOffsetOnAxis(ap=bufs["idx_now"][:, h, s % HALF:s % HALF + 1], axis=0))\
                        .then_inc(s_got[s].sem, 16)

            stepped(g, T // U, 1, turn)

        def gather_pe(pe, c, s, width=P):
            i = c * U + s
            pe.wait_ge(g_oh.sem, g_oh.at(i + 1))
            pe.wait_ge(s_got[s].sem, s_got[s].at(c + 1))
            if not first(i, 2):
                pe.wait_ge(g_add.sem, g_add.at(i - 1))
            nc.tensor.matmul(ps[:, s % 2, 0:width], lhsT=bufs["msg"][:, s, :], rhs=bufs["oh"][:, s % 4, :],
                             start=True, stop=True).then_inc(g_mm.sem, 1)

        def one_hot(v, i, s, code, weight, width):
            if weight is None:
                ins = v.tensor_scalar(bufs["oh"][:, s % 4, :], iota[:, 0:width], code[:, cut(i, 1)], None, ALU.is_equal)
            else:
                ins = v.tensor_scalar(bufs["oh"][:, s % 4, :], iota[:, 0:width], code[:, cut(i, 1)],
                                      weight[:, cut(i, 1)], ALU.is_equal, ALU.mult)
            ins.then_inc(g_oh.sem, 1)

        def gather_dve(v, c, s, code, weight, width, to):
            i = c * U + s
            b = v.value_load(block_dst[0:1, cut(i, 1)], min_val=0, max_val=BLOCKS - 1)
            one_hot(v, i + AHEAD, s + AHEAD, code, weight, width)
            v.wait_ge(g_mm.sem, g_mm.at(i + 1))
            if not first(i, 1):
                v.wait_ge(g_add.sem, g_add.at(i))
            at = to[:, ds(b * width, width)]
            v.tensor_tensor(at, ps[:, s % 2, 0:width], at, ALU.add).then_inc(g_add.sem, 1)

        def gather_over():
            g_oh.done(T + AHEAD)
            g_mm.done(T)
            g_add.done(T)
            s_idx.done(2 * T // U)
            for k in range(U):
                s_got[k].done(T // U)

        def gather_pass(table, code, weight, width=P, to=sumT):
            with ExitStack() as own:
                gather_bufs(own, width)
                with nc.Block() as block:
                    @block.gpsimd
                    def _(g):
                        gather_pool(g, table)

                    @block.tensor
                    def _(pe):
                        stepped(pe, T // U, 1, lambda c, _: [gather_pe(pe, c, s, width) for s in range(U)])

                    @block.vector
                    def _(v):
                        v.memset(to[:, 0:NB * width], 0.0)
                        for i in range(AHEAD):
                            one_hot(v, i, i, code, weight, width)
                        stepped(v, T // U, 1,
                                lambda c, _: [gather_dve(v, c, s, code, weight, width, to) for s in range(U)])
            gather_over()

        AU = T // 4
        a_ld = [sem(f"attr_rows{k}", 16) for k in range(4)]
        a_oh, a_key, a_dg, a_k, a_s = sem("a_oh"), sem("a_key"), sem("a_diag"), sem("a_keys"), sem("a_sums")
        a_rk, a_pm, a_x, a_sum = sem("a_rank"), sem("a_perm"), sem("a_sorted"), sem("a_added")
        a_ls, a_eq, a_lim, a_c, a_v = sem("a_node_row"), sem("a_same"), sem("a_limit"), sem("a_ends"), sem("a_last")
        a_lo, a_sc, a_t, a_st, a_m = sem("a_last_oh"), sem("a_scan"), sem("a_back"), sem("a_back_sb"), sem("a_picked")
        a_b, a_mx = sem("a_absent"), sem("a_max")
        agg_sems = (a_oh, a_key, a_dg, a_k, a_s, a_rk, a_pm, a_x, a_sum, a_ls, a_eq, a_lim, a_c, a_v, a_lo,
                    a_sc, a_t, a_st, a_m, a_b, a_mx)

        def agg_bufs(to):
            bufs["ar"] = sb("ar", [P, 4, ROW], F32, to)
            bufs["aoh"] = sb("aoh", [P, 2, P], F32, to)
            bufs["cols"] = sb("cols", [P, 4, 4], F32, to)
            bufs["diag"] = sb("diag", [P, 2, P], F32, to)
            bufs["lob"] = sb("lob", [P, 2, P], F32, to)
            bufs["junk"] = sb("junk", [P, P], F32, to)
            bufs["perm"] = sb("perm", [P, 2, P + 1], F32, to)
            bufs["ls"] = sb("ls", [P, P + 1], F32, to)
            bufs["eq"] = sb("eq", [P, P], F32, to)
            bufs["lim"] = sb("lim", [P, P], F32, to)
            bufs["nbig"] = sb("nbig", [P, 1], F32, to)
            bufs["ends"] = sb("ends", [P, 4], F32, to)
            bufs["last"] = sb("last", [P, 2, P], F32, to)
            bufs["scan"] = sb("scan", [P, 2, P], F32, to)
            bufs["back"] = sb("back", [P, P + 1], F32, to)
            bufs["absent"] = sb("absent", [P, 1], F32, to)

        def known(u, stage):
            return not isinstance(u, int) or 0 <= u - stage < AU

        def agg_sp(sp, part, u, s):
            if not first(u, 4):
                sp.wait_ge(a_x.sem, a_x.at(u - 3))
                sp.wait_ge(a_s.sem, a_s.at(u - 3))
                sp.wait_ge(a_dg.sem, a_dg.at(u - 3))
            rows_v = attr_rows.rearrange("(p t) w -> p (t w)", p=P)
            sp.dma_start(bufs["ar"][:, s, :], rows_v[:, cut((u + part * AU) * ROW, ROW)]).then_inc(a_ld[s].sem, 16)

        def agg_act(act, u, s):
            cols, ar = bufs["cols"], bufs["ar"]
            if known(u, 0):
                act.wait_ge(a_key.sem, a_key.at(u + 1))
                if not first(u, 2):
                    act.wait_ge(a_x.sem, a_x.at(u - 1))
                act.activation(bufs["diag"][:, s % 2, :], ident[:], ACT.Copy, scale=cols[:, s, 0:1])
                act.activation(bufs["lob"][:, s % 2, :], ones[:], ACT.Copy, scale=ar[:, s, D + 1:D + 2])\
                    .then_inc(a_dg.sem, 1)
            if known(u, 2):
                k = u - 2
                act.wait_ge(a_x.sem, a_x.at(k + 1))
                if not first(k, 1):
                    act.wait_ge(a_eq.sem, a_eq.at(k))
                act.activation(bufs["ls"][:, 1:P + 1], ps[:, 4, P:2 * P], ACT.Copy).then_inc(a_ls.sem, 1)
                act.wait_ge(a_eq.sem, a_eq.at(k + 1))
                if not first(k, 1):
                    act.wait_ge(a_sc.sem, a_sc.at(k))
                act.activation(bufs["lim"][:], bufs["eq"][:], ACT.Identity, bias=bufs["nbig"][:, 0:1], scale=2 * BIG)\
                    .then_inc(a_lim.sem, 1)
            if known(u, 3):
                m = u - 3
                act.wait_ge(a_t.sem, a_t.at(m + 1))
                if not first(m, 1):
                    act.wait_ge(a_m.sem, a_m.at(m))
                act.activation(bufs["back"][:, 0:P], ps[:, 5, 0:P], ACT.Copy).then_inc(a_st.sem, 1)

        def agg_pe(pe, u, s):
            cols, ar = bufs["cols"], bufs["ar"]
            mm = nc.tensor.matmul
            if known(u, 3):
                m = u - 3
                pe.wait_ge(a_sc.sem, a_sc.at(m + 1))
                if not first(m, 1):
                    pe.wait_ge(a_st.sem, a_st.at(m))
                pe.transpose(ps[:, 5, 0:P], bufs["scan"][:, (s + 1) % 2, :], ident[:]).then_inc(a_t.sem, 1)
            if known(u, 0):
                pe.wait_ge(a_dg.sem, a_dg.at(u + 1))
                if not first(u, 1):
                    pe.wait_ge(a_rk.sem, a_rk.at(u))
                mm(ps[:, 3, 0:P], lhsT=ones[:], rhs=bufs["diag"][:, s % 2, :], start=True, stop=True)\
                    .then_inc(a_k.sem, 1)
                pe.wait_ge(a_oh.sem, a_oh.at(u + 1))
                if not first(u, 1):
                    pe.wait_ge(a_sum.sem, a_sum.at(u))
                mm(ps[:, 2, 0:P], lhsT=ar[:, s, 0:D], rhs=bufs["aoh"][:, s % 2, :], start=True, stop=True)
                mm(ps[:, 2, P:P + 1], lhsT=bufs["aoh"][:, s % 2, :], rhs=ones[:, 0:1], start=True, stop=True)\
                    .then_inc(a_s.sem, 1)
            if known(u, 1):
                j, t = u - 1, (s + 3) % 4
                perm = bufs["perm"][:, t % 2, :]
                pe.wait_ge(a_pm.sem, a_pm.at(j + 1))
                if not first(j, 1):
                    pe.wait_ge(a_sc.sem, a_sc.at(j))
                mm(ps[:, 4, 0:P], lhsT=ar[:, t, 0:D], rhs=perm[:, 0:P], start=True, stop=True)
                mm(ps[:, 4, P:2 * P], lhsT=bufs["lob"][:, t % 2, :], rhs=perm[:, 0:P], start=True, stop=True)
                mm(ps[:, 4, 2 * P:2 * P + 1], lhsT=perm[:, 0:P], rhs=cols[:, t, 1:2], start=True, stop=True)
                mm(ps[:, 4, 2 * P + 1:2 * P + 2], lhsT=perm[:, 1:P + 1], rhs=cols[:, t, 1:2], start=True, stop=True)\
                    .then_inc(a_x.sem, 1)
            if known(u, 3):
                m = u - 3
                pe.wait_ge(a_st.sem, a_st.at(m + 1))
                if not first(m, 1):
                    pe.wait_ge(a_mx.sem, a_mx.at(m))
                mm(ps[:, 6, 0:P + 1], lhsT=bufs["last"][:, (s + 1) % 2, :], rhs=bufs["back"][:, 0:P + 1],
                   start=True, stop=True).then_inc(a_m.sem, 1)

        def agg_dve(v, part, u, s):
            cols, ar = bufs["cols"], bufs["ar"]

            def block_of(t):
                return v.value_load(block_src[0:1, cut(t + part * AU, 1)], min_val=0, max_val=BLOCKS - 1)

            if known(u, 1):
                j, t = u - 1, (s + 3) % 4
                v.wait_ge(a_k.sem, a_k.at(j + 1))
                v.tensor_scalar(bufs["junk"][:], ps[:, 3, 0:P], cols[:, t, 0:1], None, ALU.is_lt, ALU.add,
                                accum_out=cols[:, t, 2:3]).then_inc(a_rk.sem, 1)
                v.wait_ge(a_rk.sem, a_rk.at(j + 1))
                if not first(j, 2):
                    v.wait_ge(a_x.sem, a_x.at(j - 1))
                v.tensor_scalar(bufs["perm"][:, t % 2, 0:P], iota[:, 0:P], cols[:, t, 2:3], None, ALU.is_equal)\
                    .then_inc(a_pm.sem, 1)
            if known(u, 0):
                v.wait_ge(a_ld[s].sem, a_ld[s].at(1) + (u - s) * 4)
                if not first(u, 2):
                    v.wait_ge(a_s.sem, a_s.at(u - 1))
                v.tensor_scalar(bufs["aoh"][:, s % 2, :], iota[:, 0:P], ar[:, s, D + 1:D + 2], None, ALU.is_equal)\
                    .then_inc(a_oh.sem, 1)
                v.tensor_scalar(cols[:, s, 1:2], ar[:, s, D + 1:D + 2], 1.0, None, ALU.add)
                v.scalar_tensor_tensor(cols[:, s, 0:1], ar[:, s, D + 1:D + 2], float(P), pidx[:], ALU.mult, ALU.add)\
                    .then_inc(a_key.sem, 1)
            if known(u, 1):
                b = block_of(j)
                v.wait_ge(a_s.sem, a_s.at(j + 1))
                if not first(j, 1):
                    v.wait_ge(a_sum.sem, a_sum.at(j))
                at = attr_sumT[:, ds(b * P, P)]
                v.tensor_tensor(at, ps[:, 2, 0:P], at, ALU.add)
                at = attr_count[:, ds(b, 1)]
                v.tensor_tensor(at, ps[:, 2, P:P + 1], at, ALU.add).then_inc(a_sum.sem, 1)
            if known(u, 2):
                k = u - 2
                v.wait_ge(a_ls.sem, a_ls.at(k + 1))
                if not first(k, 1):
                    v.wait_ge(a_lim.sem, a_lim.at(k))
                v.tensor_tensor(bufs["eq"][:], bufs["ls"][:, 1:P + 1], bufs["ls"][:, 0:P], ALU.is_equal)\
                    .then_inc(a_eq.sem, 1)
                v.tensor_copy(bufs["ends"][:, 0:2], ps[:, 4, 2 * P:2 * P + 2]).then_inc(a_c.sem, 1)
                v.wait_ge(a_c.sem, a_c.at(k + 1))
                v.scalar_tensor_tensor(bufs["ends"][:, 2:3], bufs["ends"][:, 0:1], bufs["ends"][:, 1:2],
                                       bufs["ends"][:, 0:1], ALU.not_equal, ALU.mult).then_inc(a_v.sem, 1)
                v.wait_ge(a_v.sem, a_v.at(k + 1))
                if not first(k, 2):
                    v.wait_ge(a_m.sem, a_m.at(k - 1))
                v.tensor_scalar(bufs["last"][:, s % 2, :], iota[:, 0:P], 1.0, bufs["ends"][:, 2:3],
                                ALU.add, ALU.is_equal).then_inc(a_lo.sem, 1)
                v.wait_ge(a_lim.sem, a_lim.at(k + 1))
                if not first(k, 2):
                    v.wait_ge(a_t.sem, a_t.at(k - 1))
                v.tensor_tensor_scan(bufs["scan"][:, s % 2, :], bufs["lim"][:], ps[:, 4, 0:P], -BIG, ALU.min, ALU.max)\
                    .then_inc(a_sc.sem, 1)
            if known(u, 3):
                m = u - 3
                b = block_of(m)
                v.wait_ge(a_m.sem, a_m.at(m + 1))
                v.tensor_scalar(bufs["absent"][:], ps[:, 6, P:P + 1], -1.0, FMAX, ALU.add, ALU.mult).then_inc(a_b.sem, 1)
                v.wait_ge(a_b.sem, a_b.at(m + 1))
                if not first(m, 1):
                    v.wait_ge(a_mx.sem, a_mx.at(m))
                at = attr_max[:, ds(b * P, P)]
                v.scalar_tensor_tensor(at, ps[:, 6, 0:P], bufs["absent"][:, 0:1], at, ALU.add, ALU.max)\
                    .then_inc(a_mx.sem, 1)

        def agg_over():
            for c in agg_sems:
                c.done(AU)
            for c in a_ld:
                c.done(AU // 4)

        r_mm, r_rz, r_t1, r_t2 = sem("r_mm"), sem("r_rz"), sem("r_t1"), sem("r_t2")
        r_n, r_d, r_e, r_cp = sem("r_n"), sem("r_d"), sem("r_e"), sem("r_cp")

        def gru(table):
            with ExitStack() as own:
                table_bufs(own, T4 * D)
                rz = sb("rz", [P, 2, 2 * PAIR], F32, own)
                t1 = sb("t1", [P, 2, PAIR], F32, own)
                t2 = sb("t2", [P, 2, PAIR], F32, own)
                nn = sb("nn", [P, 2, PAIR], F32, own)
                h_now = bufs["h"]
                with nc.Block() as block:
                    @block.tensor
                    def _(pe):
                        def step(i, s):
                            a_, h_ = sumT[:, col(i)], hT[:, col(i)]
                            if not first(i, 2):
                                pe.wait_ge(r_t2.sem, r_t2.at(i - 1))
                                pe.wait_ge(r_rz.sem, r_rz.at(i - 1))
                            for k in range(2):
                                o = ps[:, s, k * PAIR:(k + 1) * PAIR]
                                nc.tensor.matmul(o, lhsT=gate_w[:, k, :], rhs=a_, start=True, stop=False)
                                nc.tensor.matmul(o, lhsT=gate_w[:, 3 + k, :], rhs=h_, start=False, stop=True)
                            nc.tensor.matmul(ps[:, 2 + s, 0:PAIR], lhsT=gate_w[:, 2, :], rhs=a_, start=True, stop=True)
                            nc.tensor.matmul(ps[:, 2 + s, PAIR:2 * PAIR], lhsT=gate_w[:, 5, :], rhs=h_,
                                             start=True, stop=True).then_inc(r_mm.sem, 1)
                            if table and not first(i, 1):
                                table_pe(pe, i - 1, 1 - s, edge_w, T4 * D)

                        stepped(pe, STEPS, 2, step, peel=2)
                        if table:
                            table_pe(pe, STEPS - 1, (STEPS - 1) % 2, edge_w, T4 * D)

                    @block.scalar
                    def _(act):
                        def copy(j, s):
                            act.wait_ge(h_ready.sem, h_ready.at(j + 1))
                            act.activation(hT[:, col(j)], h_now[:, s, :], ACT.Copy).then_inc(r_cp.sem, 1)

                        def step(i, s):
                            act.wait_ge(r_mm.sem, r_mm.at(i + 1))
                            if not first(i, 2):
                                act.wait_ge(h_ready.sem, h_ready.at(i - 1))
                            for k in range(2):
                                last = act.activation(rz[:, s, k * PAIR:(k + 1) * PAIR], ps[:, s, k * PAIR:(k + 1) * PAIR],
                                                      ACT.Sigmoid, bias=b_rz[:, k:k + 1])
                            last.then_inc(r_rz.sem, 1)
                            if not first(i, 1):
                                copy(i - 1, 1 - s)
                            act.wait_ge(r_t2.sem, r_t2.at(i + 1))
                            act.activation(nn[:, s, :], t2[:, s, :], ACT.Tanh, bias=b_ih[:, 2:3]).then_inc(r_n.sem, 1)

                        stepped(act, STEPS, 2, step, peel=2)
                        copy(STEPS - 1, (STEPS - 1) % 2)

                    @block.vector
                    def _(v):
                        def step(i, s):
                            r, z = rz[:, s, 0:PAIR], rz[:, s, PAIR:2 * PAIR]
                            v.wait_ge(r_rz.sem, r_rz.at(i + 1))
                            v.scalar_tensor_tensor(t1[:, s, :], ps[:, 2 + s, PAIR:2 * PAIR], b_hh[:, 2:3], r,
                                                   ALU.add, ALU.mult).then_inc(r_t1.sem, 1)
                            v.wait_ge(r_t1.sem, r_t1.at(i + 1))
                            v.tensor_tensor(t2[:, s, :], ps[:, 2 + s, 0:PAIR], t1[:, s, :], ALU.add).then_inc(r_t2.sem, 1)
                            if table and not first(i, 1):
                                table_dve(v, i - 1, 1 - s, edge_bias[:], T4 * D)
                            v.wait_ge(r_n.sem, r_n.at(i + 1))
                            v.tensor_tensor(t1[:, s, :], hT[:, col(i)], nn[:, s, :], ALU.subtract).then_inc(r_d.sem, 1)
                            v.wait_ge(r_d.sem, r_d.at(i + 1))
                            v.tensor_tensor(t2[:, s, :], z, t1[:, s, :], ALU.mult).then_inc(r_e.sem, 1)
                            v.wait_ge(r_e.sem, r_e.at(i + 1))
                            if not first(i, 2):
                                v.wait_ge(r_cp.sem, r_cp.at(i - 1))
                                if table:
                                    v.wait_ge(t_mm.sem, t_mm.at(i - 1))
                            v.tensor_tensor(h_now[:, s, :], nn[:, s, :], t2[:, s, :], ALU.add).then_inc(h_ready.sem, 1)

                        stepped(v, STEPS, 2, step, peel=2)
                        if table:
                            table_dve(v, STEPS - 1, (STEPS - 1) % 2, edge_bias[:], T4 * D)

                    @block.sync
                    def _(sp):
                        if table:
                            stepped(sp, STEPS, 2, lambda i, s: table_store(sp, i, s, table4, T4 * D))
                            table_stored(sp)
            for c in (r_mm, r_rz, r_t1, r_t2, r_n, r_d, r_e, r_cp):
                c.done(STEPS)
            if table:
                table_over()
            else:
                h_ready.done(STEPS)

        s_init = sem("init")
        for part in range(4):
            with ExitStack() as own:
                gather_bufs(own)
                agg_bufs(own)
                with nc.Block() as block:
                    @block.sync
                    def _(sp):
                        stepped(sp, T // U, 1, lambda c, _: [agg_sp(sp, part, c * 4 + s, s) for s in range(4)])

                    @block.gpsimd
                    def _(g):
                        gather_pool(g, table4)

                    @block.scalar
                    def _(act):
                        act.wait_ge(s_init.sem, part + 1)
                        stepped(act, T // U, 1, lambda c, _: [agg_act(act, c * 4 + s, s) for s in range(4)])
                        for s in range(3):
                            agg_act(act, AU + s, s)

                    @block.tensor
                    def _(pe):
                        def turn(c, _):
                            for s in range(U):
                                gather_pe(pe, c, s)
                                if s % 4 == 3:
                                    agg_pe(pe, c * 4 + s // 4, s // 4)

                        stepped(pe, T // U, 1, turn)
                        for s in range(3):
                            agg_pe(pe, AU + s, s)

                    @block.vector
                    def _(v):
                        v.memset(bufs["perm"][:, :, P:P + 1].rearrange("p s o -> p (s o)"), 0.0)
                        v.memset(bufs["ls"][:, 0:1], -1.0)
                        v.memset(bufs["nbig"][:], -BIG)
                        v.memset(bufs["back"][:, P:P + 1], 1.0)
                        if part == 0:
                            v.memset(attr_count[:], 0.0)
                            v.memset(attr_sumT, 0.0)
                            v.memset(attr_max, -FMAX)
                        v.memset(sumT, 0.0).then_inc(s_init.sem, 1)
                        v.wait_ge(s_init.sem, part + 1)
                        for i in range(AHEAD):
                            one_hot(v, i, i, node, None, P)

                        def turn(c, _):
                            for s in range(U):
                                gather_dve(v, c, s, node, None, P, sumT)
                                if s % 4 == 3:
                                    agg_dve(v, part, c * 4 + s // 4, s // 4)

                        stepped(v, T // U, 1, turn)
                        for s in range(3):
                            agg_dve(v, part, AU + s, s)
            gather_over()
            agg_over()
            gru(part < 3)

        c_th, c_mm, c_add = sem("c_types"), sem("c_mm"), sem("c_add")
        k_oh, k_tp, k_cp, k_mm, k_w, k_inv = sem("k_oh"), sem("k_tp"), sem("k_cp"), sem("k_mm"), sem("k_w"), sem("k_inv")
        with ExitStack() as own:
            oh = sb("rel_oh", [P, 2, P], F32, own)
            ohT = sb("rel_ohT", [P, 2, P], F32, own)
            th = sb("rel_th", [P, 2, RT], F32, own)
            junk = sb("rel_junk", [P, 2, T16], F32, own)
            rel = rel_inv[:].rearrange("p b r -> p (b r)")
            with nc.Block() as block:
                @block.tensor
                def _(pe):
                    def count(i, s):
                        pe.wait_ge(c_th.sem, c_th.at(i + 1))
                        if not first(i, 2):
                            pe.wait_ge(c_add.sem, c_add.at(i - 1))
                        nc.tensor.matmul(ps[:, s % 2, 0:RT], lhsT=oh[:, s % 2, :], rhs=th[:, s % 2, :],
                                         start=True, stop=True).then_inc(c_mm.sem, 1)

                    stepped(pe, T, 4, count)

                    def pick(j, s):
                        b = pe.value_load(block_dst[0:1, cut(j, 1)], min_val=0, max_val=BLOCKS - 1)
                        pe.wait_ge(k_cp.sem, k_cp.at(j + 1))
                        if not first(j, 2):
                            pe.wait_ge(k_w.sem, k_w.at(j - 1))
                        nc.tensor.matmul(ps[:, 4 + s % 2, 0:RT], lhsT=ohT[:, s % 2, :], rhs=rel[:, ds(b * RT, RT)],
                                         start=True, stop=True).then_inc(k_mm.sem, 1)

                    def look(i, s):
                        pe.wait_ge(k_oh.sem, k_oh.at(i + 1))
                        if not first(i, 2):
                            pe.wait_ge(k_cp.sem, k_cp.at(i - 1))
                        pe.transpose(ps[:, 2 + s % 2, 0:P], oh[:, s % 2, :], ident[:]).then_inc(k_tp.sem, 1)
                        if not first(i, 1):
                            pick(i - 1, s + 1)

                    pe.wait_ge(k_inv.sem, 2)
                    stepped(pe, T, 4, look)
                    pick(T - 1, T - 1)

                @block.scalar
                def _(act):
                    def copy(i, s):
                        act.wait_ge(k_tp.sem, k_tp.at(i + 1))
                        if not first(i, 2):
                            act.wait_ge(k_mm.sem, k_mm.at(i - 1))
                        act.activation(ohT[:, s % 2, :], ps[:, 2 + s % 2, 0:P], ACT.Copy).then_inc(k_cp.sem, 1)

                    stepped(act, T, 4, copy)

                @block.vector
                def _(v):
                    v.memset(rel, 0.0)

                    def add(j, s):
                        b = v.value_load(block_dst[0:1, cut(j, 1)], min_val=0, max_val=BLOCKS - 1)
                        v.wait_ge(c_mm.sem, c_mm.at(j + 1))
                        if not first(j, 1):
                            v.wait_ge(c_add.sem, c_add.at(j))
                        at = rel[:, ds(b * RT, RT)]
                        v.tensor_tensor(at, ps[:, s % 2, 0:RT], at, ALU.add).then_inc(c_add.sem, 1)

                    def count(i, s):
                        if not first(i, 2):
                            v.wait_ge(c_mm.sem, c_mm.at(i - 1))
                        v.tensor_scalar(oh[:, s % 2, :], iota[:, 0:P], node[:, cut(i, 1)], None, ALU.is_equal)
                        v.tensor_scalar(th[:, s % 2, 0:T16], iota[:, 0:T16], type16[:, cut(i, 1)], None, ALU.is_equal)
                        v.tensor_scalar(th[:, s % 2, T16:RT], iota[:, 0:T3], type3[:, cut(i, 1)], None, ALU.is_equal)\
                            .then_inc(c_th.sem, 1)
                        if not first(i, 1):
                            add(i - 1, s + 1)

                    stepped(v, T, 4, count)
                    add(T - 1, T - 1)
                    v.wait_ge(c_add.sem, T)
                    v.tensor_scalar(rel, rel, 1.0, None, ALU.max).then_inc(k_inv.sem, 1)
                    v.wait_ge(k_inv.sem, 1)
                    v.reciprocal(rel, rel).then_inc(k_inv.sem, 1)

                    def weigh(j, s):
                        v.wait_ge(k_mm.sem, k_mm.at(j + 1))
                        if not first(j, 1):
                            v.wait_ge(k_w.sem, k_w.at(j))
                        v.scalar_tensor_tensor(junk[:, 0, :], iota[:, 0:T16], type16[:, cut(j, 1)],
                                               ps[:, 4 + s % 2, 0:T16], ALU.is_equal, ALU.mult,
                                               accum_out=w16[:, cut(j, 1)])
                        v.scalar_tensor_tensor(junk[:, 1, 0:T3], iota[:, 0:T3], type3[:, cut(j, 1)],
                                               ps[:, 4 + s % 2, T16:RT], ALU.is_equal, ALU.mult,
                                               accum_out=w3[:, cut(j, 1)]).then_inc(k_w.sem, 1)

                    def look(i, s):
                        if not first(i, 2):
                            v.wait_ge(k_tp.sem, k_tp.at(i - 1))
                        v.tensor_scalar(oh[:, s % 2, :], iota[:, 0:P], node[:, cut(i, 1)], None, ALU.is_equal)\
                            .then_inc(k_oh.sem, 1)
                        if not first(i, 1):
                            weigh(i - 1, s + 1)

                    stepped(v, T, 4, look)
                    weigh(T - 1, T - 1)
        l0.close()

        def normalise(add):
            with ExitStack() as own:
                norm_bufs(own)
                with nc.Block() as block:
                    @block.tensor
                    def _(pe):
                        norm_pe(pe, add)

                    @block.scalar
                    def _(act):
                        norm_act(act)

                    @block.vector
                    def _(v):
                        norm_dve(v, add)
            norm_over(add)

        m_h, m_r, m_o = sem("m_hidden"), sem("m_relu"), sem("m_out")

        def hidden_pe(pe, i, chunks, w1, inputs):
            for c in range(chunks):
                if c % 2 == 0 and not first(i, 1):
                    pe.wait_ge(m_r.sem, m_r.at(i * (chunks // 2) + (c // 2 + 1 - chunks // 2)))
                for n, rhs in enumerate(inputs):
                    last = nc.tensor.matmul(ps[:, c // 2, (c % 2) * PAIR:(c % 2 + 1) * PAIR], lhsT=w1(n, c), rhs=rhs,
                                            start=n == 0, stop=n == len(inputs) - 1)
                if c % 2:
                    last.then_inc(m_h.sem, 1)

        def hidden_act(act, i, s, chunks, hid, b1):
            if not first(i, 2):
                act.wait_ge(m_o.sem, m_o.at(i - 1))
            for c in range(chunks):
                if c % 2 == 0:
                    act.wait_ge(m_h.sem, m_h.at(i * (chunks // 2) + (c // 2 + 1)))
                last = act.activation(hid[:, s, c, :], ps[:, c // 2, (c % 2) * PAIR:(c % 2 + 1) * PAIR], ACT.Relu,
                                      bias=b1[:, c:c + 1])
                if c % 2:
                    last.then_inc(m_r.sem, 1)

        def two_over(chunks):
            m_h.done(STEPS * chunks // 2)
            m_r.done(STEPS * chunks // 2)
            m_o.done(STEPS)

        def columns(sp, to, ap, n, load):
            with nc.allow_non_contiguous_dma(reason="a few biases, one element a partition"):
                sp.dma_start(to, ap.rearrange("(c p) -> p c", p=P) if n > 1 else ap.rearrange("(p o) -> p o", o=1))\
                    .then_inc(load, 16)

        normalise(True)
        e_w, e_st, e_tp, e_in, e_x, e_b, e_xx = sem("e_weights"), sem("e_staged"), sem("e_transposed"), sem("e_inputs"), sem("e_x"), sem("e_bias"), sem("e_xx")
        with ExitStack() as own:
            w1 = sb("e_w1", [P, 4, H1], F32, own)
            w2 = sb("e_w2", [P, C1, D], F32, own)
            vec = sb("e_vec", [P, 4, C1], F32, own)
            u0 = sb("e_u", [P, 1], F32, own)
            inv = sb("e_inv", [P, NB], F32, own)
            some = sb("e_some", [P, NB], F32, own)
            nat = sb("e_nat", [P, 2, PAIR], F32, own)
            diag = sb("e_diag", [P, 2, PAIR], F32, own)
            maxT = sb("e_maxT", [P, 2, PAIR], F32, own)
            meanT = sb("e_meanT", [P, 2, PAIR], F32, own)
            hid = sb("e_hid", [P, 2, C1, PAIR], F32, own)
            sumx = sb("e_sumx", [P, PAIR], F32, own)
            with nc.Block() as block:
                @block.sync
                def _(sp):
                    sp.dma_start(w1[:], a["L1_gnn_W1"][0:4 * P, :].rearrange("(c p) h -> p c h", p=P)).then_inc(e_w.sem, 16)
                    sp.dma_start(w2[:], a["L1_gnn_W2"].rearrange("(c p) h -> p c h", p=P)).then_inc(e_w.sem, 16)
                    columns(sp, vec[:, 0, :], a["L1_gnn_b1"], C1, e_w.sem)
                    columns(sp, vec[:, 1, :], a["L1_gnn_W1"][4 * P:4 * P + 1, :].rearrange("o h -> (o h)"), C1, e_w.sem)
                    columns(sp, vec[:, 3, 0:1], a["L1_gnn_b2"], 1, e_w.sem)
                    sp.dma_start(u0[0:1, :], a["L1_gnn_u"][0:1, :]).then_inc(e_w.sem, 16)

                @block.gpsimd
                def _(g):
                    g.wait_ge(e_w.sem, 96)
                    g.partition_broadcast(u0[:], u0[0:1, :], P).then_inc(e_b.sem, 1)

                @block.tensor
                def _(pe):
                    pe.wait_ge(e_w.sem, 96)

                    def hidden(j, s):
                        pe.wait_ge(e_in.sem, j + 1)
                        hidden_pe(pe, j, C1, lambda n, c: w1[:, n, c * P:(c + 1) * P],
                                  [hT[:, col(j)], attr_sumT[:, col(j)], maxT[:, s, :], meanT[:, s, :]])

                    def output(j, s):
                        pe.wait_ge(m_r.sem, m_r.at(j * (C1 // 2) + C1 // 2))
                        if not first(j, 2):
                            pe.wait_ge(e_x.sem, j - 1)
                        for c in range(C1):
                            last = nc.tensor.matmul(ps[:, 4 + s, 0:PAIR], lhsT=w2[:, c, :], rhs=hid[:, s, c, :],
                                                    start=c == 0, stop=c == C1 - 1)
                        last.then_inc(m_o.sem, 1)

                    def step(i, s):
                        pe.wait_ge(e_st.sem, i + 1)
                        if not first(i, 2):
                            pe.wait_ge(e_in.sem, i - 1)
                        for j in range(2):
                            pe.transpose(ps[:, 6 + s, j * P:(j + 1) * P], nat[:, s, j * P:(j + 1) * P], ident[:])
                        nc.tensor.matmul(ps[:, 6 + s, PAIR:2 * PAIR], lhsT=ones[:], rhs=diag[:, s, :],
                                         start=True, stop=True).then_inc(e_tp.sem, 1)
                        if not first(i, 1):
                            hidden(i - 1, 1 - s)
                        if not first(i, 2):
                            output(i - 2, s)

                    stepped(pe, STEPS, 2, step, peel=2)
                    hidden(STEPS - 1, (STEPS - 1) % 2)
                    output(STEPS - 2, STEPS % 2)
                    output(STEPS - 1, (STEPS - 1) % 2)

                @block.scalar
                def _(act):
                    act.wait_ge(e_b.sem, 5)

                    def step(i, s):
                        if not first(i, 2):
                            act.wait_ge(e_tp.sem, i - 1)
                        for j in range(2):
                            blk = cut(2 * i + j, 1)
                            act.activation(nat[:, s, j * P:(j + 1) * P], attr_max[:, cut((2 * i + j) * P, P)],
                                           ACT.Copy, scale=some[:, blk])
                            last = act.activation(diag[:, s, j * P:(j + 1) * P], ident[:], ACT.Copy, scale=inv[:, blk])
                        last.then_inc(e_st.sem, 1)
                        if not first(i, 1):
                            hidden_act(act, i - 1, 1 - s, C1, hid, vec[:, 2, :])

                    stepped(act, STEPS, 2, step, peel=2)
                    hidden_act(act, STEPS - 1, (STEPS - 1) % 2, C1, hid, vec[:, 2, :])

                @block.vector
                def _(v):
                    v.wait_ge(e_b.sem, 1)
                    v.scalar_tensor_tensor(vec[:, 2, :], vec[:, 1, :], u0[:, 0:1], vec[:, 0, :], ALU.mult, ALU.add)\
                        .then_inc(e_b.sem, 1)
                    v.tensor_scalar(some[:], attr_count[:], 1.0, None, ALU.min).then_inc(e_b.sem, 1)
                    v.tensor_scalar(inv[:], attr_count[:], 1.0, None, ALU.max).then_inc(e_b.sem, 1)
                    v.wait_ge(e_b.sem, 4)
                    v.reciprocal(inv[:], inv[:]).then_inc(e_b.sem, 1)

                    def output(j, s):
                        v.wait_ge(m_o.sem, m_o.at(j + 1))
                        v.scalar_tensor_tensor(sumx[:], ps[:, 4 + s, 0:PAIR], vec[:, 3, 0:1], xT[:, col(j)],
                                               ALU.add, ALU.add).then_inc(e_x.sem, 1)
                        v.wait_ge(e_x.sem, j + 1)
                        v.tensor_tensor(xT[:, col(j)], sumx[:], hT[:, col(j)], ALU.add).then_inc(e_xx.sem, 1)
                        v.wait_ge(e_xx.sem, j + 1)

                    def step(i, s):
                        v.wait_ge(e_tp.sem, i + 1)
                        if not first(i, 2):
                            v.wait_ge(m_h.sem, m_h.at((i - 1) * (C1 // 2)))
                        v.tensor_copy(maxT[:, s, :], ps[:, 6 + s, 0:PAIR])
                        v.tensor_tensor(meanT[:, s, :], attr_sumT[:, col(i)], ps[:, 6 + s, PAIR:2 * PAIR], ALU.mult)\
                            .then_inc(e_in.sem, 1)
                        if not first(i, 2):
                            output(i - 2, s)

                    stepped(v, STEPS, 2, step, peel=2)
                    output(STEPS - 2, STEPS % 2)
                    output(STEPS - 1, (STEPS - 1) % 2)
        two_over(C1)
        normalise(False)

        q_w, q_s = sem("q_weights"), sem("q_copied")
        c1w = sb("c1w", [P, T3 + 1, H2], F32, l0)
        c2w = sb("c2w", [P, C2, (T3 + 1) * D], F32, l0)
        v3 = sb("v3", [P, 4, C2], F32, l0)
        node3 = sb("node3", [P, T + AHEAD], F32, l0)
        with ExitStack() as own:
            qw1 = sb("qw1", [P, H2], F32, own)
            qw2 = sb("qw2", [P, C2, D], F32, own)
            table_bufs(own, D)
            hid = sb("q_hid", [P, 2, C2, PAIR], F32, own)
            with nc.Block() as block:
                @block.sync
                def _(sp):
                    w = q_w.sem
                    sp.dma_start(qw1[:], a["L2_gnn_q_w1"]).then_inc(w, 16)
                    sp.dma_start(qw2[:], a["L2_gnn_q_w2"].rearrange("(c p) h -> p c h", p=P)).then_inc(w, 16)
                    columns(sp, v3[:, 0, :], a["L2_gnn_q_b1"], C2, w)
                    columns(sp, v3[:, 1, :], a["L2_gnn_c1_b"], C2, w)
                    columns(sp, v3[:, 2, 0:1], a["L2_gnn_q_b2"], 1, w)
                    columns(sp, v3[:, 3, 0:1], a["L2_gnn_c2_b"], 1, w)
                    sp.dma_start(c1w[:, 0:T3, :], a["L2_gnn_c1_wrel"].rearrange("r p h -> p r h")).then_inc(w, 16)
                    sp.dma_start(c1w[:, T3, :], a["L2_gnn_c1_wroot"]).then_inc(w, 16)
                    for r in range(T3):
                        sp.dma_start(c2w[:, :, r * D:(r + 1) * D],
                                     a["L2_gnn_c2_wrel"][r, :, :].rearrange("(c p) o -> p c o", p=P)).then_inc(w, 16)
                    sp.dma_start(c2w[:, :, T3 * D:], a["L2_gnn_c2_wroot"].rearrange("(c p) o -> p c o", p=P)).then_inc(w, 16)
                    stepped(sp, STEPS, 2, lambda i, s: table_store(sp, i, s, table1, D))
                    table_stored(sp)

                @block.tensor
                def _(pe):
                    pe.wait_ge(q_w.sem, 16 * 12)

                    def output(j, s):
                        pe.wait_ge(m_r.sem, m_r.at(j * (C2 // 2) + C2 // 2))
                        if not first(j, 1):
                            pe.wait_ge(h_ready.sem, h_ready.at(j))
                        for c in range(C2):
                            last = nc.tensor.matmul(ps[:, 3, 0:PAIR], lhsT=qw2[:, c, :], rhs=hid[:, s, c, :],
                                                    start=c == 0, stop=c == C2 - 1)
                        last.then_inc(m_o.sem, 1)

                    def step(i, s):
                        hidden_pe(pe, i, C2, lambda n, c: qw1[:, c * P:(c + 1) * P], [hT[:, col(i)]])
                        if not first(i, 1):
                            output(i - 1, 1 - s)
                        if not first(i, 2):
                            table_pe(pe, i - 2, s, None, D)

                    stepped(pe, STEPS, 2, step, peel=2)
                    output(STEPS - 1, (STEPS - 1) % 2)
                    table_pe(pe, STEPS - 2, STEPS % 2, None, D)
                    table_pe(pe, STEPS - 1, (STEPS - 1) % 2, None, D)

                @block.scalar
                def _(act):
                    act.wait_ge(q_w.sem, 16 * 12)

                    def output(j, s):
                        act.wait_ge(m_o.sem, m_o.at(j + 1))
                        if not first(j, 2):
                            act.wait_ge(t_mm.sem, t_mm.at(j - 1))
                        act.activation(bufs["h"][:, s, :], ps[:, 3, 0:PAIR], ACT.Identity, bias=v3[:, 2, 0:1])\
                            .then_inc(h_ready.sem, 1)
                        act.wait_ge(h_ready.sem, h_ready.at(j + 1))
                        act.activation(hT[:, col(j)], bufs["h"][:, s, :], ACT.Copy).then_inc(q_s.sem, 1)

                    def step(i, s):
                        hidden_act(act, i, s, C2, hid, v3[:, 0, :])
                        if not first(i, 2):
                            output(i - 2, s)

                    stepped(act, STEPS, 2, step, peel=2)
                    output(STEPS - 2, STEPS % 2)
                    output(STEPS - 1, (STEPS - 1) % 2)

                @block.vector
                def _(v):
                    n = [0]

                    def chain(ins):
                        n[0] += 1
                        ins.then_inc(s_chain.sem, 1)
                        v.wait_ge(s_chain.sem, s_chain.at(n[0]))

                    chain(v.tensor_scalar(tmp_i1[:], words[:], LO_AT, (1 << LO_BITS) - 1, ALU.logical_shift_right, ALU.bitwise_and))
                    chain(v.tensor_scalar(idx[:], words[:], E3_AT, 3, ALU.logical_shift_right, ALU.bitwise_and))
                    v.memset(node3[:, T:T + AHEAD], 0.0)
                    chain(v.scalar_tensor_tensor(node3[:, 0:T], idx[:], float(P), tmp_i1[:], ALU.mult, ALU.add))
                    table_rows(v, chain, 0, 0, 1)
                    stepped(v, STEPS, 2, lambda i, s: table_dve(v, i, s, None, D))
                    done_chain[0] = n[0]
        s_chain.done(done_chain[0])
        two_over(C2)
        table_over()

        gather_pass(table1, node3, w3, T3 * P, big[:])

        f_x = sem("f_x")
        rel_sums = big[:].rearrange("p (b r n) -> p b r n", r=T3, n=P)
        with ExitStack() as own:
            table_bufs(own, T3 * D)
            hid = sb("c_hid", [P, 2, C2, PAIR], F32, own)
            with nc.Block() as block:
                @block.sync
                def _(sp):
                    stepped(sp, STEPS, 2, lambda i, s: table_store(sp, i, s, table3, T3 * D))
                    table_stored(sp)

                @block.tensor
                def _(pe):
                    def output(j, s):
                        pe.wait_ge(m_r.sem, m_r.at(j * (C2 // 2) + C2 // 2))
                        if not first(j, 1):
                            pe.wait_ge(h_ready.sem, h_ready.at(j))
                        for c in range(C2):
                            nc.tensor.matmul(ps[:, 3, 0:PAIR], lhsT=c2w[:, c, T3 * D:(T3 + 1) * D],
                                             rhs=hid[:, s, c, :], start=c == 0, stop=c == C2 - 1)
                        if not first(j, 2):
                            pe.wait_ge(t_ev.sem, t_ev.at(j - 1))
                        for k in range(2):
                            for c in range(C2):
                                last = nc.tensor.matmul(ps[:, 4 + 2 * s + k, 0:T3 * D],
                                                        lhsT=hid[:, s, c, k * P:(k + 1) * P],
                                                        rhs=c2w[:, c, 0:T3 * D], start=c == 0, stop=c == C2 - 1)
                        last.then_inc(t_mm.sem, 1)

                    def step(i, s):
                        hidden_pe(pe, i, C2, lambda n, c: c1w[:, n, c * P:(c + 1) * P],
                                  [rel_sums[:, cut(2 * i, 2), r, :] for r in range(T3)] + [hT[:, col(i)]])
                        if not first(i, 1):
                            output(i - 1, 1 - s)

                    stepped(pe, STEPS, 2, step, peel=2)
                    output(STEPS - 1, (STEPS - 1) % 2)

                @block.scalar
                def _(act):
                    def output(j, s):
                        act.wait_ge(t_mm.sem, t_mm.at(j + 1))
                        act.activation(hT[:, col(j)], ps[:, 3, 0:PAIR], ACT.Identity, bias=v3[:, 3, 0:1])\
                            .then_inc(h_ready.sem, 1)

                    def step(i, s):
                        if not first(i, 2):
                            act.wait_ge(t_mm.sem, t_mm.at(i - 1))
                        for c in range(C2):
                            if c % 2 == 0:
                                act.wait_ge(m_h.sem, m_h.at(i * (C2 // 2) + (c // 2 + 1)))
                            last = act.activation(hid[:, s, c, :], ps[:, c // 2, (c % 2) * PAIR:(c % 2 + 1) * PAIR],
                                                  ACT.Relu, bias=v3[:, 1, c:c + 1])
                            if c % 2:
                                last.then_inc(m_r.sem, 1)
                        if not first(i, 1):
                            output(i - 1, 1 - s)

                    stepped(act, STEPS, 2, step, peel=2)
                    output(STEPS - 1, (STEPS - 1) % 2)

                @block.vector
                def _(v):
                    n = [0]

                    def chain(ins):
                        n[0] += 1
                        ins.then_inc(s_chain.sem, 1)
                        v.wait_ge(s_chain.sem, s_chain.at(n[0]))

                    table_rows(v, chain, E3_AT, 3, T3)
                    stepped(v, STEPS, 2, lambda i, s: table_dve(v, i, s, None, T3 * D))
                    done_chain[0] = n[0]
        s_chain.done(done_chain[0])
        m_h.done(STEPS * C2 // 2)
        m_r.done(STEPS * C2 // 2)
        table_over()
        l0.close()

        gather_pass(table3, node, w3)

        y_w, y_a, y_r, y_mm, y_x, y_p = sem("y_weights"), sem("y_sum"), sem("y_relu"), sem("y_mm"), sem("y_x"), sem("y_pre")
        with ExitStack() as own:
            lin = sb("lin", [P, D], F32, own)
            lin_b = sb("lin_b", [P, 1], F32, own)
            st = sb("lin_in", [P, 2, PAIR], F32, own)
            rl = sb("lin_relu", [P, 2, PAIR], F32, own)
            with nc.Block() as block:
                @block.sync
                def _(sp):
                    sp.dma_start(lin[:], a["L2_gnn_lin_w"]).then_inc(y_w.sem, 16)
                    columns(sp, lin_b[:], a["L2_gnn_lin_b"], 1, y_w.sem)

                @block.scalar
                def _(act):
                    def step(i, s):
                        act.wait_ge(y_a.sem, i + 1)
                        if not first(i, 2):
                            act.wait_ge(y_mm.sem, i - 1)
                        act.activation(rl[:, s, :], st[:, s, :], ACT.Relu).then_inc(y_r.sem, 1)

                    stepped(act, STEPS, 2, step)

                @block.tensor
                def _(pe):
                    pe.wait_ge(y_w.sem, 32)

                    def step(i, s):
                        pe.wait_ge(y_r.sem, i + 1)
                        if not first(i, 2):
                            pe.wait_ge(y_x.sem, i - 1)
                        nc.tensor.matmul(ps[:, s, 0:PAIR], lhsT=lin[:], rhs=rl[:, s, :], start=True, stop=True)\
                            .then_inc(y_mm.sem, 1)

                    stepped(pe, STEPS, 2, step)

                @block.vector
                def _(v):
                    v.wait_ge(y_w.sem, 32)

                    def output(j, s):
                        v.wait_ge(y_mm.sem, j + 1)
                        v.scalar_tensor_tensor(xT[:, col(j)], ps[:, s, 0:PAIR], lin_b[:, 0:1], xT[:, col(j)],
                                               ALU.add, ALU.add).then_inc(y_x.sem, 1)

                    def step(i, s):
                        if not first(i, 2):
                            v.wait_ge(y_r.sem, i - 1)
                        v.tensor_tensor(st[:, s, :], sumT[:, col(i)], hT[:, col(i)], ALU.add).then_inc(y_a.sem, 1)
                        if not first(i, 1):
                            output(i - 1, 1 - s)

                    stepped(v, STEPS, 2, step, peel=2)
                    output(STEPS - 1, (STEPS - 1) % 2)
        normalise(False)

        z_w, z_h, z_mm = sem("z_weights"), sem("z_h"), sem("z_mm")
        z_v, z_a, z_dma = sem("z_dve"), sem("z_act"), [sem("z_dma0", 16), sem("z_dma1", 16)]
        r4_mm, r4_a, r4_h = sem("r4_mm"), sem("r4_add"), sem("r4_h")
        rel_w = sb("rel_w", [P, 2, T16 * 32], F32, l0)
        root_w = sb("root_w", [P, 2, D], F32, l0)
        root_b = sb("root_b", [P, 2], F32, l0)

        def table_16(conv):
            with ExitStack() as own:
                hs = sb("z_hs", [P, 2, P], F32, own)
                rows = sb("z_rows", [P, 2, T16, 4, 32], F32, own)
                with nc.Block() as block:
                    @block.sync
                    def _(sp):
                        if conv == 0:
                            for k, n in enumerate(("L3_gnn_W1", "L3_gnn_W2")):
                                sp.dma_start(rel_w[:, k, :].rearrange("p (r o) -> p r o", o=32),
                                             a[n].rearrange("r b i o -> (b i) r o")).then_inc(z_w.sem, 16)
                            for k, n in enumerate(("1", "2")):
                                sp.dma_start(root_w[:, k, :], a["L3_gnn_root" + n]).then_inc(z_w.sem, 16)
                                columns(sp, root_b[:, k:k + 1], a["L3_gnn_bias" + n], 1, z_w.sem)
                        to = table16.rearrange("(b p r) d -> p b (r d)", p=P, r=T16)

                        def store(i, s):
                            sp.wait_ge(z_v.sem, z_v.at(i + 1))
                            sp.wait_ge(z_a.sem, z_a.at(i + 1))
                            at = to[:, i, :] if isinstance(i, int) else to[:, ds(i, 1), :].rearrange("p o f -> p (o f)")
                            sp.dma_start(at, rows[:, s].rearrange("p r b o -> p (r b o)")).then_inc(z_dma[s].sem, 16)

                        stepped(sp, NB, 2, store)
                        for s in range(2):
                            sp.wait_ge(z_dma[s].sem, z_dma[s].at(NB // 2))

                    @block.tensor
                    def _(pe):
                        pe.wait_ge(z_w.sem, 96)

                        def step(i, s):
                            pe.wait_ge(z_h.sem, z_h.at(i + 1))
                            if not first(i, 2):
                                pe.wait_ge(z_v.sem, z_v.at(i - 1))
                                pe.wait_ge(z_a.sem, z_a.at(i - 1))
                            for b in range(4):
                                q = slice(32 * b, 32 * b + 32)
                                last = nc.tensor.matmul(ps[:, 4 * s + b, :], lhsT=hs[q, s, :], rhs=rel_w[q, conv, :],
                                                        start=True, stop=True)
                            last.then_inc(z_mm.sem, 1)

                        stepped(pe, NB, 2, step)

                    @block.scalar
                    def _(act):
                        def evacuate(j, s):
                            act.wait_ge(z_mm.sem, z_mm.at(j + 1))
                            if not first(j, 2):
                                act.wait_ge(z_dma[s].sem, (j - s) * 8 + z_dma[s].base)
                            for b in (2, 3):
                                last = act.activation(rows[:, s, :, b, :], ps[:, 4 * s + b, :].rearrange("p (r o) -> p r o", o=32),
                                                      ACT.Copy)
                            last.then_inc(z_a.sem, 1)

                        def step(i, s):
                            if not first(i, 2):
                                act.wait_ge(z_mm.sem, z_mm.at(i - 1))
                            act.activation(hs[:, s, :], hT[:, cut(i * P, P)], ACT.Copy).then_inc(z_h.sem, 1)
                            if not first(i, 1):
                                evacuate(i - 1, 1 - s)

                        stepped(act, NB, 2, step, peel=2)
                        evacuate(NB - 1, (NB - 1) % 2)

                    @block.vector
                    def _(v):
                        n = [0]

                        def chain(ins):
                            n[0] += 1
                            ins.then_inc(s_chain.sem, 1)
                            v.wait_ge(s_chain.sem, s_chain.at(n[0]))

                        if conv == 0:
                            table_rows(v, chain, E16_AT, 15, T16)
                        done_chain[0] = n[0]

                        def evacuate(j, s):
                            v.wait_ge(z_mm.sem, z_mm.at(j + 1))
                            if not first(j, 2):
                                v.wait_ge(z_dma[s].sem, (j - s) * 8 + z_dma[s].base)
                            for b in (0, 1):
                                last = v.tensor_copy(rows[:, s, :, b, :], ps[:, 4 * s + b, :].rearrange("p (r o) -> p r o", o=32))
                            last.then_inc(z_v.sem, 1)

                        stepped(v, NB, 2, evacuate)
            s_chain.done(done_chain[0])
            for c in (z_h, z_mm, z_v, z_a):
                c.done(NB)
            for c in z_dma:
                c.done(NB // 2)

        table_16(0)
        gather_pass(table16, node, w16)
        with ExitStack() as own:
            st = sb("r4_st", [P, 2, PAIR], F32, own)
            with nc.Block() as block:
                @block.tensor
                def _(pe):
                    def step(i, s):
                        if not first(i, 2):
                            pe.wait_ge(r4_a.sem, r4_a.at(i - 1))
                        nc.tensor.matmul(ps[:, s, 0:PAIR], lhsT=root_w[:, 0, :], rhs=hT[:, col(i)], start=True, stop=True)\
                            .then_inc(r4_mm.sem, 1)

                    stepped(pe, STEPS, 2, step)

                @block.vector
                def _(v):
                    def step(i, s):
                        v.wait_ge(r4_mm.sem, r4_mm.at(i + 1))
                        if not first(i, 2):
                            v.wait_ge(r4_h.sem, r4_h.at(i - 1))
                        v.tensor_tensor(st[:, s, :], sumT[:, col(i)], ps[:, s, 0:PAIR], ALU.add).then_inc(r4_a.sem, 1)

                    stepped(v, STEPS, 2, step)

                @block.scalar
                def _(act):
                    def step(i, s):
                        act.wait_ge(r4_a.sem, r4_a.at(i + 1))
                        act.activation(hT[:, col(i)], st[:, s, :], ACT.Relu, bias=root_b[:, 0:1]).then_inc(r4_h.sem, 1)

                    stepped(act, STEPS, 2, step)
        for c in (r4_mm, r4_a, r4_h):
            c.done(STEPS)
        table_16(1)
        gather_pass(table16, node, w16)

        o_x, o_tp, o_cp, o_dma = sem("o_x"), sem("o_tp"), sem("o_cp"), [sem("o_dma0"), sem("o_dma1")]
        with ExitStack() as own:
            st = sb("o_st", [P, 2, PAIR], F32, own)
            fin = sb("o_fin", [P, 2, PAIR], F32, own)
            nat = sb("o_nat", [P, 2, 2, D], F32, own)
            with nc.Block() as block:
                @block.tensor
                def _(pe):
                    def back(j, s):
                        pe.wait_ge(o_x.sem, j + 1)
                        if not first(j, 2):
                            pe.wait_ge(o_cp.sem, j - 1)
                        for k in range(2):
                            last = pe.transpose(ps[:, 2 + s, k * P:(k + 1) * P], fin[:, s, k * P:(k + 1) * P], ident[:])
                        last.then_inc(o_tp.sem, 1)

                    def step(i, s):
                        if not first(i, 2):
                            pe.wait_ge(r4_a.sem, r4_a.at(i - 1))
                        nc.tensor.matmul(ps[:, s, 0:PAIR], lhsT=root_w[:, 1, :], rhs=hT[:, col(i)], start=True, stop=True)\
                            .then_inc(r4_mm.sem, 1)
                        if not first(i, 1):
                            back(i - 1, 1 - s)

                    stepped(pe, STEPS, 2, step, peel=2)
                    back(STEPS - 1, (STEPS - 1) % 2)

                @block.vector
                def _(v):
                    def step(i, s):
                        v.wait_ge(r4_mm.sem, r4_mm.at(i + 1))
                        if not first(i, 2):
                            v.wait_ge(o_x.sem, i - 1)
                        v.tensor_tensor(st[:, s, :], sumT[:, col(i)], ps[:, s, 0:PAIR], ALU.add).then_inc(r4_a.sem, 1)
                        v.wait_ge(r4_a.sem, r4_a.at(i + 1))
                        if not first(i, 2):
                            v.wait_ge(o_tp.sem, i - 1)
                        v.scalar_tensor_tensor(fin[:, s, :], st[:, s, :], root_b[:, 1:2], xT[:, col(i)], ALU.add, ALU.add)\
                            .then_inc(o_x.sem, 1)

                    stepped(v, STEPS, 2, step)

                @block.scalar
                def _(act):
                    def step(i, s):
                        act.wait_ge(o_tp.sem, i + 1)
                        if not first(i, 2):
                            act.wait_ge(o_dma[s].sem, (i - s) * 8)
                        act.activation(nat[:, s, :, :].rearrange("p k d -> p (k d)"), ps[:, 2 + s, 0:PAIR], ACT.Copy)\
                            .then_inc(o_cp.sem, 1)

                    stepped(act, STEPS, 2, step)

                @block.sync
                def _(sp):
                    whole = N // PAIR
                    to = out[0:whole * PAIR, :].rearrange("(b p) d -> p b d", p=P)

                    def store(i, s):
                        sp.wait_ge(o_cp.sem, i + 1)
                        if isinstance(i, int) and i == whole:
                            sp.dma_start(out[i * PAIR:N, :], nat[0:N - whole * PAIR, s, 0, :]).then_inc(o_dma[s].sem, 16)
                        else:
                            sp.dma_start(to[:, cut(2 * i, 2), :], nat[:, s, :, :]).then_inc(o_dma[s].sem, 16)

                    stepped(sp, STEPS, 2, store)
                    sp.wait_ge(o_dma[0].sem, 16 * ((STEPS + 1) // 2))
                    sp.wait_ge(o_dma[1].sem, 16 * (STEPS // 2))


def kernel(**inputs):
    import numpy as _np
    import concourse.bacc as _bacc
    from concourse.bass_utils import run_bass_kernel_spmd as _run

    nc = _bacc.Bacc("TRN2", target_bir_lowering=False, num_devices=1)
    arrays, args = {}, {}
    for name, value in inputs.items():
        v = _np.ascontiguousarray(value)
        arrays[f"in_{name}"] = v
        args[name] = nc.dram_tensor(f"in_{name}", v.shape, mybir.dt.from_np(v.dtype), kind="ExternalInput").ap()
    out = nc.dram_tensor("out_dram", (N, D), F32, kind="ExternalOutput").ap()
    build(nc, args, out)
    r = _run(nc, [arrays], core_ids=[0])
    return r.results[0]["out_dram"]
```

```python
import math
from contextlib import ExitStack

import concourse.bass as bass
from concourse import mybir

F32 = mybir.dt.float32
I32 = mybir.dt.int32
U8 = mybir.dt.uint8
BF16 = mybir.dt.bfloat16
ALU = mybir.AluOpType
ACT = mybir.ActivationFunctionType

P = 128
D = 128
N = 6250
E = 100000
BLOCKS = math.ceil(N / P)
LAST = N - (BLOCKS - 1) * P
PAIR = 2 * P
STEPS = math.ceil(N / PAIR)
NB = 2 * STEPS
NP = NB * P
J = 16
GROUPS = math.ceil(E / (P * J))
TAIL = (E - (GROUPS - 1) * P * J) // J
EC = GROUPS * J
T = 16 * math.ceil((math.ceil(E / P) + BLOCKS - 1) / 16)
U = 16
PADT = 16
G = 4
TURN = U // G
GROUPS_T = T // G
AHEAD = G
SLOTS = P * T
NONE = P
ROW = D + 1
HALF = 8
BIG = 2.0 ** 126
HUGE = 2.0 ** 119
FMAX = 3.4028234663852886e38
EPS = 1e-5
T4, T3, T16 = 4, 3, 16
RT = T16 + T3
H1, H2 = 512, 768
C1, C2 = H1 // P, H2 // P
SRC_BITS, LO_BITS = 13, 8
LO_AT, E4_AT, E3_AT, E16_AT = 13, 21, 23, 25


class Count:

    def __init__(self, sem, unit=1):
        self.sem, self.unit, self.base = sem, unit, 0

    def at(self, n):
        return n * self.unit + self.base

    def done(self, n):
        self.base += n * self.unit


def stepped(eng, total, unroll, step, peel=1):
    turns = total // unroll - peel
    for i in range(peel * unroll):
        step(i, i % unroll)
    with eng.Fori(0, turns) as q:
        for s in range(unroll):
            step(q * unroll + (peel * unroll + s), s)
    for i in range(unroll * (turns + peel), total):
        step(i, i % unroll)


def cut(i, n):
    return slice(i, i + n) if isinstance(i, int) else bass.ds(i, n)


def first(i, n):
    return isinstance(i, int) and i < n


def blocks_of(nc, eng, table, i):
    _, values = nc.values_load_multi_w_load_instructions(
        table[0:1, cut(i, G)], [eng.engine], min_val=0, max_val=BLOCKS - 1,
        skip_runtime_bounds_check_because="it is how many of the BLOCKS blocks begin at or before the tile, less one")
    return values


def build(nc, a, out):
    ctx = ExitStack()
    sems = {}

    def sem(name, unit=1):
        if name not in sems:
            sems[name] = Count(ctx.enter_context(nc.semaphore(name)), unit)
        return sems[name]

    names = {}

    def sb(name, shape, dt=F32, to=None):
        names[name] = names.get(name, 0) + 1
        name += f"_{names[name]}" if names[name] > 1 else ""
        return (to or ctx).enter_context(nc.sbuf_tensor(name, shape, dt))

    ds = bass.ds
    with ctx:
        edge_list = nc.dram_tensor("edge_list", [SLOTS, 1], I32, kind="Internal").ap()
        attr_rows = nc.dram_tensor("attr_rows", [SLOTS, ROW], F32, kind="Internal").ap()
        table4 = nc.dram_tensor("table4", [NP * T4, D], F32, kind="Internal").ap()
        table1 = nc.dram_tensor("table1", [NP, D], F32, kind="Internal").ap()
        table3 = nc.dram_tensor("table3", [NP * T3, D], F32, kind="Internal").ap()
        table16 = nc.dram_tensor("table16", [NP * T16, D], F32, kind="Internal").ap()

        xT = sb("xT", [P, NP])
        hT = sb("hT", [P, NP])
        big = sb("big", [P, 3 * NP])
        sumT = big[:, 0:NP]
        attr_sumT = big[:, NP:2 * NP]
        attr_max = big[:, 2 * NP:3 * NP]
        words = sb("words", [P, T], I32)
        idx_all = sb("idx", [P, T + HALF], I32)
        idx = idx_all[:, 0:T]
        node = sb("node", [P, T + AHEAD])
        w3 = sb("w3", [P, T + AHEAD])
        w16 = sb("w16", [P, T + AHEAD])
        block_dst = sb("block_dst", [1, T], I32)
        block_src = sb("block_src", [1, T], I32)
        attr_count = sb("attr_count", [P, NB])
        rel_inv = sb("rel_inv", [P, NB, RT])
        iota = sb("iota", [P, T3 * P])
        ident = sb("ident", [P, P])
        ones = sb("ones", [P, P])
        mean_w = sb("mean_w", [P, P])
        pidx = sb("pidx", [P, 1])
        eps = sb("eps", [P, 1])
        ps = ctx.enter_context(nc.psum_tensor("ps", [P, 8, 512], F32))

        def grouped(ap, width=1):
            flat = ap if len(ap.shape) == 1 else ap.rearrange("e w -> (e w)")
            whole = (GROUPS - 1) * P * J * width
            return (flat[0:whole].rearrange("(g p j) -> p g j", p=P, j=J * width),
                    flat[whole:E * width].rearrange("(p j) -> p j", j=J * width))

        tmp_i1 = sb("tmp_i1", [P, T], I32)

        n_add, n_mean, n_dev, n_sq = sem("n_add"), sem("n_mean"), sem("n_dev"), sem("n_sq")
        n_var, n_sd, n_rec, n_out = sem("n_var"), sem("n_sd"), sem("n_rec"), sem("n_out")
        h_ready, t_mm, t_ev = sem("h_ready"), sem("t_mm"), sem("t_ev")
        t_dma = [sem("t_dma0", 16), sem("t_dma1", 16)]
        bufs = {}

        def col(i):
            return cut(i * PAIR, PAIR)

        def norm_bufs():
            for n, name in enumerate(("dev", "sq", "sd")):
                bufs[name] = sumT[:, n * 2 * PAIR:(n + 1) * 2 * PAIR].rearrange("p (s c) -> p s c", s=2)

        def norm_pe(pe, add=False):
            def variance(j, s):
                pe.wait_ge(n_sq.sem, n_sq.at(j + 1))
                if not first(j, 2):
                    pe.wait_ge(n_sd.sem, n_sd.at(j - 1))
                nc.tensor.matmul(ps[:, 2 + s, 0:PAIR], lhsT=mean_w[:], rhs=bufs["sq"][:, s, :],
                                 start=True, stop=True).then_inc(n_var.sem, 1)

            def step(i, s):
                if add:
                    pe.wait_ge(n_add.sem, n_add.at(i + 1))
                if not first(i, 2):
                    pe.wait_ge(n_dev.sem, n_dev.at(i - 1))
                nc.tensor.matmul(ps[:, s, 0:PAIR], lhsT=mean_w[:], rhs=xT[:, col(i)],
                                 start=True, stop=True).then_inc(n_mean.sem, 1)
                if not first(i, 1):
                    variance(i - 1, 1 - s)

            stepped(pe, STEPS, 2, step, peel=2)
            variance(STEPS - 1, (STEPS - 1) % 2)

        def norm_act(act):
            def deviation(j, s):
                act.wait_ge(n_var.sem, n_var.at(j + 1))
                if not first(j, 2):
                    act.wait_ge(n_rec.sem, n_rec.at(j - 1))
                act.activation(bufs["sd"][:, s, :], ps[:, 2 + s, 0:PAIR], ACT.Sqrt, bias=eps[:, 0:1])\
                    .then_inc(n_sd.sem, 1)

            def step(i, s):
                act.wait_ge(n_dev.sem, n_dev.at(i + 1))
                if not first(i, 2):
                    act.wait_ge(n_var.sem, n_var.at(i - 1))
                act.activation(bufs["sq"][:, s, :], bufs["dev"][:, s, :], ACT.Square).then_inc(n_sq.sem, 1)
                if not first(i, 1):
                    deviation(i - 1, 1 - s)

            stepped(act, STEPS, 2, step, peel=2)
            deviation(STEPS - 1, (STEPS - 1) % 2)

        def norm_dve(v, add=False):
            def output(j, s):
                v.wait_ge(n_sd.sem, n_sd.at(j + 1))
                v.reciprocal(bufs["sd"][:, s, :], bufs["sd"][:, s, :]).then_inc(n_rec.sem, 1)
                v.wait_ge(n_rec.sem, n_rec.at(j + 1))
                v.scalar_tensor_tensor(hT[:, col(j)], bufs["dev"][:, s, :], 0.0, bufs["sd"][:, s, :],
                                       ALU.max, ALU.mult).then_inc(n_out.sem, 1)

            def step(i, s):
                if add:
                    v.tensor_tensor(xT[:, col(i)], xT[:, col(i)], hT[:, col(i)], ALU.add).then_inc(n_add.sem, 1)
                v.wait_ge(n_mean.sem, n_mean.at(i + 1))
                if not first(i, 2):
                    v.wait_ge(n_out.sem, n_out.at(i - 1))
                    v.wait_ge(n_sq.sem, n_sq.at(i - 1))
                v.tensor_tensor(bufs["dev"][:, s, :], xT[:, col(i)], ps[:, s, 0:PAIR], ALU.subtract)\
                    .then_inc(n_dev.sem, 1)
                if not first(i, 1):
                    output(i - 1, 1 - s)

            stepped(v, STEPS, 2, step, peel=2)
            output(STEPS - 1, (STEPS - 1) % 2)

        def norm_over(add=False):
            for c in (n_mean, n_dev, n_sq, n_var, n_sd, n_rec, n_out) + ((n_add,) if add else ()):
                c.done(STEPS)

        def table_bufs(to, width):
            bufs["h"] = sb("h_now", [P, 2, PAIR], F32, to)
            bufs["rows"] = sb("table_rows", [P, 2, 2, width], F32, to)

        def table_pe(pe, i, s, w, width):
            pe.wait_ge(h_ready.sem, h_ready.at(i + 1))
            if not first(i, 2):
                pe.wait_ge(t_ev.sem, t_ev.at(i - 1))
            for j in range(2):
                h = bufs["h"][:, s, j * P:(j + 1) * P]
                if w is None:
                    last = pe.transpose(ps[:, 4 + 2 * s + j, 0:P], h, ident[:])
                else:
                    last = nc.tensor.matmul(ps[:, 4 + 2 * s + j, 0:width], lhsT=h, rhs=w, start=True, stop=True)
            last.then_inc(t_mm.sem, 1)

        def table_dve(v, i, s, bias, width):
            v.wait_ge(t_mm.sem, t_mm.at(i + 1))
            if not first(i, 2):
                v.wait_ge(t_dma[s].sem, (i - s) * 8 + t_dma[s].base)
            for j in range(2):
                to, rows = bufs["rows"][:, s, j, :], ps[:, 4 + 2 * s + j, 0:width]
                last = v.tensor_copy(to, rows) if bias is None else v.tensor_tensor(to, rows, bias, ALU.add)
            last.then_inc(t_ev.sem, 1)

        def table_store(eng, i, s, table, width):
            eng.wait_ge(t_ev.sem, t_ev.at(i + 1))
            eng.dma_start(table.rearrange("(b p r) d -> p b (r d)", p=P, r=width // D)[:, cut(2 * i, 2), :],
                          bufs["rows"][:, s, :, :]).then_inc(t_dma[s].sem, 16)

        def table_stored(eng):
            for s in range(2):
                eng.wait_ge(t_dma[s].sem, t_dma[s].at((STEPS + 1 - s) // 2))

        def table_over():
            for c in (h_ready, t_mm, t_ev):
                c.done(STEPS)
            for s in range(2):
                t_dma[s].done((STEPS + 1 - s) // 2)

        def table_rows(v, chain, at, mask, r):
            chain(v.tensor_scalar(idx[:], words[:], (1 << SRC_BITS) - 1, None, ALU.bitwise_and))
            if r > 1:
                chain(v.tensor_scalar(tmp_i1[:], words[:], at, mask, ALU.logical_shift_right, ALU.bitwise_and))
                chain(v.scalar_tensor_tensor(idx[:], idx[:], float(r), tmp_i1[:], ALU.mult, ALU.add))

        done_chain = [0]
        l0 = ctx.enter_context(ExitStack())
        gate_w = sb("gate_w", [P, 10, P], F32, l0)
        edge_w = gate_w[:, 6:10, :].rearrange("p t o -> p (t o)")
        edge_bias = sb("edge_bias", [P, T4 * D], F32, l0)
        b_ih = sb("b_ih", [P, 3], F32, l0)
        b_hh = sb("b_hh", [P, 3], F32, l0)
        b_rz = sb("b_rz", [P, 2], F32, l0)
        ones_b = sb("ones_b", [P, P], BF16, l0)
        ident_row = sb("ident_row", [P, P], F32, l0)
        edge_diag = sb("edge_diag", [P, P], BF16, l0)

        c_th, c_mm, c_add = sem("c_types"), sem("c_mm"), sem("c_add")
        k_oh, k_tp, k_cp, k_mm, k_w = sem("k_oh"), sem("k_tp"), sem("k_cp"), sem("k_mm"), sem("k_w")
        k_inv, k_pr = sem("k_inv"), sem("k_products")
        rel = rel_inv[:].rearrange("p b r -> p (b r)")

        def rel_setup(to):
            bufs["rel_oh"] = sb("rel_oh", [P, 2, G, P], BF16, to)
            bufs["rel_ohT"] = sb("rel_ohT", [P, 2, G, P], F32, to)
            bufs["rel_th"] = sb("rel_th", [P, 2, G, RT], BF16, to)
            bufs["rel_type"] = sb("rel_type", [P, 4, G, RT], F32, to)
            bufs["rel_pick"] = sb("rel_pick", [P, G, RT], F32, to)
            bufs["ident_b"] = sb("ident_b", [P, P], BF16, to)
            bufs["type3"] = attr_sumT[:, 0:T]
            bufs["type16"] = attr_sumT[:, T:2 * T]

        def transposed(s):
            return ps[:, 2 + s % 2, 0:G * P // 2].bitcast(BF16).rearrange("p (k c) -> p k c", k=G)

        def rel_out(bank):
            return ps[:, bank, 0:G * RT].rearrange("p (k r) -> p k r", k=G)

        def rel_pe(pe):
            def count(g, s):
                pe.wait_ge(c_th.sem, c_th.at(g + 1))
                if not first(g, 2):
                    pe.wait_ge(c_add.sem, c_add.at((g - 1) * G))
                for k in range(G):
                    last = nc.tensor.matmul(rel_out(s % 2)[:, k, :], lhsT=bufs["rel_oh"][:, s % 2, k, :],
                                            rhs=bufs["rel_th"][:, s % 2, k, :], start=True, stop=True)
                last.then_inc(c_mm.sem, 1)

            stepped(pe, GROUPS_T, 4, count)

            def pick(j, s):
                pe.wait_ge(k_cp.sem, k_cp.at(j + 1))
                if not first(j, 2):
                    pe.wait_ge(k_pr.sem, k_pr.at(j - 1))
                blocks = blocks_of(nc, pe, block_dst, j * G)
                for k in range(G):
                    last = nc.tensor.matmul(rel_out(4 + s % 2)[:, k, :], lhsT=bufs["rel_ohT"][:, s % 2, k, :],
                                            rhs=rel[:, ds(blocks[k] * RT, RT)], start=True, stop=True)
                last.then_inc(k_mm.sem, 1)

            def look(g, s):
                pe.wait_ge(k_oh.sem, k_oh.at(g + 1))
                if not first(g, 2):
                    pe.wait_ge(k_cp.sem, k_cp.at(g - 1))
                for k in range(G):
                    last = pe.transpose(transposed(s)[:, k, :], bufs["rel_oh"][:, s % 2, k, :], bufs["ident_b"][:])
                last.then_inc(k_tp.sem, 1)
                if not first(g, 1):
                    pick(g - 1, s + 1)

            pe.wait_ge(k_inv.sem, 2)
            stepped(pe, GROUPS_T, 4, look)
            pick(GROUPS_T - 1, GROUPS_T - 1)

        def rel_act(act):
            def copy(g, s):
                act.wait_ge(k_tp.sem, k_tp.at(g + 1))
                if not first(g, 2):
                    act.wait_ge(k_mm.sem, k_mm.at(g - 1))
                act.activation(bufs["rel_ohT"][:, s % 2, :, :], transposed(s), ACT.Copy).then_inc(k_cp.sem, 1)

            stepped(act, GROUPS_T, 4, copy)

        def same(v, to, codes, g, width):
            return v.tensor_tensor(to, iota[:, 0:width].unsqueeze(1).to_broadcast([P, G, width]),
                                   codes[:, cut(g * G, G)].unsqueeze(2).to_broadcast([P, G, width]), ALU.is_equal)

        def rel_dve(v):
            v.tensor_copy(bufs["ident_b"][:], ident[:])
            v.memset(rel, 0.0)

            def add(j, s):
                blocks = blocks_of(nc, v, block_dst, j * G)
                for k in range(G):
                    i = j * G + k
                    if k == 0:
                        v.wait_ge(c_mm.sem, c_mm.at(j + 1))
                    if not first(i, 1):
                        v.wait_ge(c_add.sem, c_add.at(i))
                    at = rel[:, ds(blocks[k] * RT, RT)]
                    v.tensor_tensor(at, rel_out(s % 2)[:, k, :], at, ALU.add).then_inc(c_add.sem, 1)

            def count(g, s):
                if not first(g, 2):
                    v.wait_ge(c_mm.sem, c_mm.at(g - 1))
                same(v, bufs["rel_oh"][:, s % 2, :, :], node, g, P)
                same(v, bufs["rel_th"][:, s % 2, :, 0:T16], bufs["type16"], g, T16)
                same(v, bufs["rel_th"][:, s % 2, :, T16:RT], bufs["type3"], g, T3).then_inc(c_th.sem, 1)
                if not first(g, 1):
                    add(g - 1, s + 1)

            stepped(v, GROUPS_T, 4, count)
            add(GROUPS_T - 1, GROUPS_T - 1)
            v.wait_ge(c_add.sem, T)
            v.tensor_scalar(rel, rel, 1.0, None, ALU.max).then_inc(k_inv.sem, 1)
            v.wait_ge(k_inv.sem, 1)
            v.reciprocal(rel, rel).then_inc(k_inv.sem, 1)

            def weigh(j, s):
                v.wait_ge(k_mm.sem, k_mm.at(j + 1))
                if not first(j, 1):
                    v.wait_ge(k_w.sem, k_w.at(j))
                v.tensor_tensor(bufs["rel_pick"][:], rel_out(4 + s % 2), bufs["rel_type"][:, s % 4, :, :], ALU.mult)\
                    .then_inc(k_pr.sem, 1)
                v.wait_ge(k_pr.sem, k_pr.at(j + 1))
                v.tensor_reduce(w16[:, cut(j * G, G)], bufs["rel_pick"][:, :, 0:T16], mybir.AxisListType.X, ALU.add)
                v.tensor_reduce(w3[:, cut(j * G, G)], bufs["rel_pick"][:, :, T16:RT], mybir.AxisListType.X, ALU.add)\
                    .then_inc(k_w.sem, 1)

            def look(g, s):
                if not first(g, 2):
                    v.wait_ge(k_tp.sem, k_tp.at(g - 1))
                same(v, bufs["rel_oh"][:, s % 2, :, :], node, g, P).then_inc(k_oh.sem, 1)
                if not first(g, 4):
                    v.wait_ge(k_pr.sem, k_pr.at(g - 3))
                same(v, bufs["rel_type"][:, s, :, 0:T16], bufs["type16"], g, T16)
                same(v, bufs["rel_type"][:, s, :, T16:RT], bufs["type3"], g, T3)
                if not first(g, 2):
                    weigh(g - 2, s + 2)

            stepped(v, GROUPS_T, 4, look)
            weigh(GROUPS_T - 2, GROUPS_T - 2)
            weigh(GROUPS_T - 1, GROUPS_T - 1)

        with ExitStack() as ph:
            addr_src = sb("addr_src", [P, EC], I32, ph)
            lo_src = sb("lo_src", [P, EC], F32, ph)
            with ExitStack() as ph2:
                dst_i = sb("dst_i", [P, EC], I32, ph2)
                src_i = sb("src_i", [P, EC], I32, ph2)
                word = sb("word", [P, EC], I32, ph2)
                tmp_i = sb("tmp_i", [P, EC], I32, ph2)
                tmp2_i = sb("tmp2_i", [P, EC], I32, ph2)
                addr_dst = sb("addr_dst", [P, EC], I32, ph2)
                attr4 = big[:, 2 * NP:2 * NP + 4 * EC]
                best = hT[:, 0:EC]
                less = hT[:, EC:2 * EC]
                rank = hT[:, 2 * EC:4 * EC].rearrange("p (s c) -> p s c", s=2)
                after = xT[:, 0:T]
                iota_t = xT[:, T:2 * T]
                pad_word = xT[:, 2 * T:3 * T].bitcast(I32)
                ones_row = xT[:, 3 * T:3 * T + EC]
                t3_i = xT[:, 4 * T:4 * T + EC].bitcast(I32)
                t16_i = xT[:, 5 * T:5 * T + EC].bitcast(I32)
                bin_f = sb("bin_f", [P, EC], BF16, ph2)
                place = sb("place", [P, EC], F32, ph2)
                strict = sb("strict", [P, P], F32, ph2)
                bins = sb("bins", [P, BLOCKS], F32, ph2)
                count = sb("count", [P, BLOCKS], F32, ph2)
                small = sb("small", [P, 4, BLOCKS], F32, ph2)
                small_i = sb("small_i", [P, BLOCKS], I32, ph2)
                tot = sb("tot", [P, 4], F32, ph2)
                tot_i = sb("tot_i", [P, 1], I32, ph2)
                addr_now = sb("addr_now", [P, 2, J], I32, ph2)
                word_now = sb("word_now", [P, 2, J], I32, ph2)
                member = big[:, 0:(BLOCKS * EC + 3) // 4].bitcast(U8)
                pad_rows = big[:, 2 * NP - PADT * ROW:2 * NP]
                s_keys, s_types, s_pad = sem("keys"), sem("types"), sem("pad_list", 16)
                s_const, s_zero, s_chain = sem("const"), sem("zeroed"), sem("prep_chain")
                s_count, s_prefix, s_col, s_colp = sem("counted"), sem("prefix"), sem("col"), sem("col_prefix")
                s_after, s_blk, s_addr = sem("after"), sem("blk"), sem("addr")
                s_copy, s_scat, s_go = sem("addr_copy"), [sem("scat0"), sem("scat1")], sem("pool_go")
                s_padr = sem("pad_rows")
                s_run, s_kept, s_rank = sem("running"), sem("kept"), sem("ranked")
                s_x, s_tp, s_tpc, s_w = sem("x_loaded"), sem("transposed"), sem("evacuated"), sem("w_loaded")
                s_wb, s_bb, s_xs, s_ordered = sem("bias_loaded"), sem("bias_ready"), sem("x_staged"), sem("ordered")
                x_nat = big[:, 2 * NP:3 * NP]
                used = [0]

                def carve(*shape):
                    at, used[0] = used[0], used[0] + math.prod(shape)
                    t = big[:, at:used[0]]
                    if len(shape) == 3:
                        return t.rearrange("p (a b c) -> p a b c", a=shape[0], b=shape[1])
                    return t.rearrange("p (a b) -> p a b", a=shape[0])

                w_nat, x_stage = carve(10, P), carve(2, D)
                for name in ("dev", "sq", "sd", "h"):
                    bufs[name] = carve(2, PAIR)
                bufs["rows"] = carve(2, 2, T4 * D)

                def first_sp(sp):
                    sp.wait_ge(s_ordered.sem, 1)
                    sp.dma_start(x_nat[:, 0:(BLOCKS - 1) * D].rearrange("p (b d) -> p b d", d=D),
                                 a["x"][0:(BLOCKS - 1) * P, :].rearrange("(b p) d -> p b d", p=P)).then_inc(s_x.sem, 16)
                    sp.dma_start(x_nat[0:LAST, (BLOCKS - 1) * D:BLOCKS * D], a["x"][(BLOCKS - 1) * P:N, :])\
                        .then_inc(s_x.sem, 16)
                    sp.dma_start(w_nat[:, 0:3, :], a["L0_gnn_W_ih"].rearrange("(c p) d -> p c d", p=P)).then_inc(s_w.sem, 16)
                    sp.dma_start(w_nat[:, 3:6, :], a["L0_gnn_W_hh"].rearrange("(c p) d -> p c d", p=P)).then_inc(s_w.sem, 16)
                    sp.dma_start(w_nat[:, 6:10, :], a["L0_gnn_W_edge"].rearrange("t o d -> o t d")).then_inc(s_w.sem, 16)

                def first_act(act):
                    act.wait_ge(s_ordered.sem, 1)
                    act.wait_ge(s_pad.sem, 16)
                    def x_copy(b, s):
                        act.wait_ge(s_tp.sem, b + 1)
                        act.activation(xT[:, cut(b * P, P)], ps[:, s, 0:P], ACT.Copy).then_inc(s_tpc.sem, 1)

                    stepped(act, NB, 2, x_copy)
                    for k in range(10):
                        act.wait_ge(s_tp.sem, NB + k + 1)
                        act.activation(gate_w[:, k, :], ps[:, k % 2, 0:P], ACT.Copy).then_inc(s_tpc.sem, 1)
                    norm_act(act)

                    def stage(i, s):
                        if not first(i, 2):
                            act.wait_ge(t_mm.sem, t_mm.at(i - 1))
                        act.activation(bufs["h"][:, s, :], hT[:, col(i)], ACT.Copy).then_inc(h_ready.sem, 1)
                        if not first(i, 1):
                            table_store(act, i - 1, 1 - s, table4, T4 * D)

                    act.wait_ge(n_out.sem, n_out.at(STEPS))
                    stepped(act, STEPS, 2, stage, peel=2)
                    table_store(act, STEPS - 1, (STEPS - 1) % 2, table4, T4 * D)
                    table_stored(act)

                def first_pe(pe):
                    pe.wait_ge(s_x.sem, 32)

                    def x_transpose(b, s):
                        pe.wait_ge(s_xs.sem, b + 1)
                        if not first(b, 2):
                            pe.wait_ge(s_tpc.sem, b - 1)
                        pe.transpose(ps[:, s, 0:P], x_stage[:, s, :], ident[:]).then_inc(s_tp.sem, 1)

                    stepped(pe, NB, 2, x_transpose)
                    pe.wait_ge(s_w.sem, 48)
                    for k in range(10):
                        pe.wait_ge(s_tpc.sem, NB + k - 1)
                        pe.transpose(ps[:, k % 2, 0:P], w_nat[:, k, :], ident[:]).then_inc(s_tp.sem, 1)
                    pe.wait_ge(s_tpc.sem, NB + 10)
                    norm_pe(pe)
                    pe.wait_ge(n_out.sem, n_out.at(STEPS))
                    stepped(pe, STEPS, 2, lambda i, s: table_pe(pe, i, s, edge_w, T4 * D))

                def first_dve(v):
                    v.memset(x_nat[:, (BLOCKS - 1) * D:NB * D], 0.0).then_inc(s_ordered.sem, 1)
                    v.wait_ge(s_x.sem, 32)

                    def x_to_stage(b, s):
                        if not first(b, 2):
                            v.wait_ge(s_tp.sem, b - 1)
                        v.tensor_copy(x_stage[:, s, :], x_nat[:, cut(b * D, D)]).then_inc(s_xs.sem, 1)

                    stepped(v, NB, 2, x_to_stage)
                    v.wait_ge(s_tpc.sem, NB)
                    norm_dve(v)
                    v.wait_ge(s_bb.sem, 1)
                    stepped(v, STEPS, 2, lambda i, s: table_dve(v, i, s, edge_bias[:], T4 * D))

                with nc.Block() as block:
                    @block.sync
                    def _(sp):
                        sp.dma_start(edge_bias[0:1, :], a["L0_gnn_b_edge"].rearrange("(o t) d -> o (t d)", o=1))\
                            .then_inc(s_wb.sem, 16)
                        with nc.allow_non_contiguous_dma(reason="a few biases, one element a partition"):
                            sp.dma_start(b_ih[:], a["L0_gnn_b_ih"].rearrange("(c p) -> p c", p=P)).then_inc(s_wb.sem, 16)
                            sp.dma_start(b_hh[:], a["L0_gnn_b_hh"].rearrange("(c p) -> p c", p=P)).then_inc(s_wb.sem, 16)
                        sp.wait_ge(s_zero.sem, 1)
                        for t, ap in ((dst_i, a["dst"]), (src_i, a["src"])):
                            whole, rest = grouped(ap)
                            sp.dma_start(t[:, 0:EC - J].rearrange("p (g j) -> p g j", j=J), whole)\
                                .then_inc(s_keys.sem, 16)
                            sp.dma_start(t[0:TAIL, EC - J:EC], rest).then_inc(s_keys.sem, 16)
                        sp.wait_ge(s_zero.sem, 2)
                        for t, ap, w in ((t3_i, a["edge_type_3"], 1), (t16_i, a["edge_type_16"], 1),
                                         (attr4, a["edge_attr_4"], 4)):
                            whole, rest = grouped(ap, w)
                            sp.dma_start(t[:, 0:(EC - J) * w].rearrange("p (g j) -> p g j", j=J * w), whole)\
                                .then_inc(s_types.sem, 16)
                            sp.dma_start(t[0:TAIL, (EC - J) * w:EC * w], rest).then_inc(s_types.sem, 16)
                        sp.dma_start(edge_list.rearrange("(p t) o -> p (t o)", p=P), pad_word[:])\
                            .then_inc(s_pad.sem, 16)
                        sp.wait_ge(s_const.sem, 13)
                        rows_v = attr_rows.rearrange("(p t) w -> p (t w)", p=P)
                        for q in range(T // PADT):
                            sp.dma_start(rows_v[:, q * PADT * ROW:(q + 1) * PADT * ROW], pad_rows)\
                                .then_inc(s_padr.sem, 16)
                        first_sp(sp)
                        sp.wait_ge(s_padr.sem, 16 * (T // PADT))

                    @block.gpsimd
                    def _(g):
                        c = s_const.sem
                        for k, ins in enumerate((
                            lambda: g.iota(iota[:], [[1, T3 * P]], base=0, channel_multiplier=0,
                                           allow_small_or_imprecise_dtypes=True),
                            lambda: g.iota(iota_t[:], [[1, T]], base=0, channel_multiplier=0,
                                           allow_small_or_imprecise_dtypes=True),
                            lambda: g.iota(bins[:], [[1, BLOCKS]], base=0, channel_multiplier=0,
                                           allow_small_or_imprecise_dtypes=True),
                            lambda: g.iota(pidx[:], [[0, 1]], base=0, channel_multiplier=1,
                                           allow_small_or_imprecise_dtypes=True),
                            lambda: g.memset(ident[:], 0.0),
                            lambda: g.memset(strict[:], 1.0),
                            lambda: g.memset(ones[:], 1.0),
                            lambda: g.memset(mean_w[:], 1.0 / D),
                            lambda: g.memset(eps[:], EPS),
                            lambda: g.memset(ones_row[:], 1.0),
                            lambda: g.memset(pad_rows, 0.0),
                        )):
                            ins().then_inc(c, 1)
                        g.wait_ge(c, 11)
                        g.memset(pad_rows.rearrange("p (t w) -> p t w", w=ROW)[:, :, D:D + 1], float(NONE))
                        g.affine_select(out=ident[:], in_=ident[:], compare_op=ALU.not_equal, fill=1.0,
                                        base=0, pattern=[[-1, P]], channel_multiplier=1).then_inc(c, 1)
                        g.affine_select(out=strict[:], in_=strict[:], compare_op=ALU.is_gt, fill=0.0,
                                        base=0, pattern=[[1, P]], channel_multiplier=-1).then_inc(c, 1)
                        g.wait_ge(s_wb.sem, 48)
                        g.partition_broadcast(edge_bias[:], edge_bias[0:1, :], P).then_inc(s_bb.sem, 1)
                        g.wait_ge(s_pad.sem, 16)
                        g.wait_ge(s_addr.sem, 1)

                        def group(i, s):
                            parts = TAIL if isinstance(i, int) and i == GROUPS - 1 else P
                            if not first(i, 2):
                                g.wait_ge(s_scat[s].sem, (i - s) * (8 * J))
                                g.sem_inc(s_go.sem, 1)
                            g.tensor_copy(addr_now[:, s, :], addr_dst[:, cut(i * J, J)]).then_inc(s_copy.sem, 1)
                            g.tensor_copy(word_now[:, s, :], word[:, cut(i * J, J)]).then_inc(s_copy.sem, 1)
                            g.wait_ge(s_copy.sem, i * 2 + 2)
                            g.sem_inc(s_go.sem, 1)
                            for j in range(J):
                                g.indirect_dma_start(
                                    edge_list, bass.IndirectOffsetOnAxis(ap=addr_now[0:parts, s, j:j + 1], axis=0),
                                    word_now[0:parts, s, j:j + 1], None).then_inc(s_scat[s].sem, 16)

                        stepped(g, GROUPS, 2, group)
                        g.wait_ge(s_scat[0].sem, 16 * J * ((GROUPS + 1) // 2))
                        g.wait_ge(s_scat[1].sem, 16 * J * (GROUPS // 2))

                    @block.tensor
                    def _(pe):
                        pe.wait_ge(s_const.sem, 13)
                        for o in range(2):
                            pe.wait_ge(s_count.sem, (o + 1) * BLOCKS)
                            nc.tensor.matmul(ps[:, 0, 0:BLOCKS], lhsT=strict[:], rhs=count[:], start=True, stop=True)
                            nc.tensor.matmul(ps[:, 1, 0:BLOCKS], lhsT=ones[:], rhs=count[:], start=True, stop=True)
                            nc.tensor.matmul(ps[0:BLOCKS, 2, 0:1], lhsT=count[:], rhs=ones[:, 0:1],
                                             start=True, stop=True).then_inc(s_prefix.sem, 1)
                            pe.wait_ge(s_col.sem, o + 1)
                            nc.tensor.matmul(ps[0:BLOCKS, 3, 0:1], lhsT=strict[0:BLOCKS, 0:BLOCKS],
                                             rhs=tot[0:BLOCKS, 0:1], start=True, stop=True).then_inc(s_colp.sem, 1)
                            pe.wait_ge(s_after.sem, o + 1)
                            for q in range(2):
                                last = nc.tensor.matmul(ps[0:1, 4 + q, 0:T // 2], lhsT=ones[0:BLOCKS, 0:1],
                                                        rhs=after[0:BLOCKS, q * (T // 2):(q + 1) * (T // 2)],
                                                        start=True, stop=True)
                            last.then_inc(s_blk.sem, 1)
                        first_pe(pe)

                    @block.scalar
                    def _(act):
                        first_act(act)

                    @block.vector
                    def _(v):
                        n = [0]

                        def chain(ins):
                            n[0] += 1
                            ins.then_inc(s_chain.sem, 1)
                            v.wait_ge(s_chain.sem, s_chain.at(n[0]))

                        v.memset(dst_i[:], -P)
                        v.memset(src_i[:], -P).then_inc(s_zero.sem, 1)
                        v.memset(t3_i[:], 0)
                        v.memset(t16_i[:], 0)
                        v.memset(attr4[:], 0.0)
                        v.memset(pad_word[:], NONE << LO_AT).then_inc(s_zero.sem, 1)
                        chain(v.memset(place[:], 0.0))
                        v.wait_ge(s_const.sem, 13)

                        def order(o, key, addr, blk):
                            chain(v.tensor_scalar(tmp_i[:], key[:], 7, None, ALU.arith_shift_right))
                            chain(v.tensor_copy(bin_f[:], tmp_i[:]))

                            def count_bin(b, s):
                                v.tensor_scalar(member[:, cut(b * EC, EC)], bin_f[:], bins[:, cut(b, 1)], None,
                                                ALU.is_equal, ALU.add, accum_out=count[:, cut(b, 1)])\
                                    .then_inc(s_count.sem, 1)

                            stepped(v, BLOCKS, 7, count_bin)
                            v.wait_ge(s_prefix.sem, o + 1)
                            chain(v.tensor_copy(small_i[:], ps[:, 1, 0:BLOCKS]))
                            chain(v.tensor_scalar(small_i[:], small_i[:], P - 1, None, ALU.add))
                            chain(v.tensor_scalar(small_i[:], small_i[:], 7, None, ALU.arith_shift_right))
                            chain(v.tensor_copy(small[:, 0, :], small_i[:]))
                            chain(v.tensor_tensor_scan(small[:, 1, :], ones_row[:, 0:BLOCKS], small[:, 0, :], 0.0,
                                                       ALU.mult, ALU.add))
                            chain(v.tensor_tensor(small[:, 2, :], small[:, 1, :], small[:, 0, :], ALU.subtract))
                            chain(v.tensor_scalar(small[:, 1, :], small[:, 2, :], float(P), -1.0, ALU.mult, ALU.add))
                            chain(v.tensor_tensor(small[:, 3, :], small[:, 1, :], ps[:, 0, 0:BLOCKS], ALU.add))
                            chain(v.tensor_copy(tot_i[0:BLOCKS, :], ps[0:BLOCKS, 2, 0:1]))
                            chain(v.tensor_scalar(tot_i[0:BLOCKS, :], tot_i[0:BLOCKS, :], P - 1, None, ALU.add))
                            chain(v.tensor_scalar(tot_i[0:BLOCKS, :], tot_i[0:BLOCKS, :], 7, None, ALU.arith_shift_right))
                            v.tensor_copy(tot[0:BLOCKS, 0:1], tot_i[0:BLOCKS, :]).then_inc(s_col.sem, 1)
                            v.wait_ge(s_colp.sem, o + 1)
                            chain(v.tensor_copy(tot[0:BLOCKS, 1:2], ps[0:BLOCKS, 3, 0:1]))
                            v.tensor_scalar(after[0:BLOCKS, :], iota_t[0:BLOCKS, :], tot[0:BLOCKS, 1:2], None,
                                            ALU.is_ge).then_inc(s_after.sem, 1)

                            def run(b, s):
                                v.tensor_tensor_scan(rank[:, s % 2, :], ones_row[:], member[:, cut(b * EC, EC)],
                                                     small[:, 3, cut(b, 1)], ALU.mult, ALU.add).then_inc(s_run.sem, 1)

                            def rank_bin(b, s, more=True):
                                r = rank[:, s % 2, :]
                                v.wait_ge(s_run.sem, b + (1 + o * BLOCKS))
                                v.scalar_tensor_tensor(r, r, 1.0, member[:, cut(b * EC, EC)], ALU.mult, ALU.mult)\
                                    .then_inc(s_kept.sem, 1)
                                if more:
                                    if not first(b, 1):
                                        v.wait_ge(s_rank.sem, b + o * BLOCKS)
                                    run(b + 1, s + 1)
                                v.wait_ge(s_kept.sem, b + (1 + o * BLOCKS))
                                v.tensor_tensor(place[:], place[:], r, ALU.add).then_inc(s_rank.sem, 1)

                            run(0, 0)
                            stepped(v, BLOCKS - 1, 8, rank_bin)
                            rank_bin(BLOCKS - 1, BLOCKS - 1, more=False)
                            v.wait_ge(s_rank.sem, (o + 1) * BLOCKS)
                            chain(v.tensor_copy(tmp_i[:], place[:]))
                            chain(v.tensor_scalar(tmp2_i[:], tmp_i[:], P - 1, None, ALU.bitwise_and))
                            chain(v.tensor_scalar(tmp_i[:], tmp_i[:], 7, None, ALU.arith_shift_right))
                            chain(v.scalar_tensor_tensor(addr[:], tmp2_i[:], float(T), tmp_i[:], ALU.mult, ALU.add))
                            v.wait_ge(s_blk.sem, o + 1)
                            for q in range(2):
                                h = slice(q * (T // 2), (q + 1) * (T // 2))
                                chain(v.tensor_scalar(blk[0:1, h], ps[0:1, 4 + q, 0:T // 2], -1.0, None, ALU.add))

                        v.wait_ge(s_keys.sem, 64)
                        order(0, dst_i, addr_dst, block_dst)
                        v.wait_ge(s_types.sem, 96)
                        a4 = attr4.rearrange("p (e w) -> p w e", w=4)
                        chain(v.tensor_tensor(best[:], a4[:, 0, :], a4[:, 1, :], ALU.max))
                        chain(v.tensor_tensor(best[:], best[:], a4[:, 2, :], ALU.max))
                        chain(v.tensor_tensor(best[:], best[:], a4[:, 3, :], ALU.max))
                        chain(v.tensor_tensor(place[:], a4[:, 2, :], best[:], ALU.not_equal))
                        for w in (1, 0):
                            chain(v.tensor_tensor(less[:], a4[:, w, :], best[:], ALU.not_equal))
                            chain(v.scalar_tensor_tensor(place[:], place[:], 1.0, less[:], ALU.add, ALU.mult))
                        chain(v.tensor_copy(word[:], place[:]))
                        chain(v.tensor_scalar(word[:], word[:], E4_AT, None, ALU.logical_shift_left))
                        chain(v.tensor_tensor(word[:], word[:], src_i[:], ALU.bitwise_or))
                        chain(v.tensor_scalar(tmp_i[:], dst_i[:], P - 1, LO_AT, ALU.bitwise_and, ALU.logical_shift_left))
                        chain(v.tensor_tensor(word[:], word[:], tmp_i[:], ALU.bitwise_or))
                        chain(v.tensor_scalar(tmp_i[:], t3_i[:], E3_AT, None, ALU.logical_shift_left))
                        chain(v.tensor_tensor(word[:], word[:], tmp_i[:], ALU.bitwise_or))
                        chain(v.tensor_scalar(tmp_i[:], t16_i[:], E16_AT, None, ALU.logical_shift_left))
                        chain(v.tensor_tensor(word[:], word[:], tmp_i[:], ALU.bitwise_or))
                        v.memset(place[:], 0.0).then_inc(s_addr.sem, 1)
                        chain(v.tensor_scalar(tmp_i[:], src_i[:], P - 1, None, ALU.bitwise_and))
                        chain(v.tensor_copy(lo_src[:], tmp_i[:]))
                        order(1, src_i, addr_src, block_src)
                        first_dve(v)
                        done_chain[0] = n[0]
                s_chain.done(done_chain[0])

            s_rows = [sem("rows0"), sem("rows1")]
            s_rscat, s_acopy, s_list = [sem("row_scat0"), sem("row_scat1")], sem("addr_copy2"), sem("list_loaded")
            rows_now = big[:, 0:2 * J * ROW].rearrange("p (s j w) -> p s j w", s=2, w=ROW)
            addr_now = sb("addr_now2", [P, 2, J], I32, ph)
            row_parts = grouped(a["edge_attr_128"], D)
            rel_setup(ph)
            with nc.Block() as block:
                @block.sync
                def _(sp):
                    sp.dma_start(words[:], edge_list.rearrange("(p t) o -> p (t o)", p=P)).then_inc(s_list.sem, 16)
                    def load(i, s):
                        if not first(i, 2):
                            sp.wait_ge(s_rscat[s].sem, (i - s) * (8 * J))
                        dst = rows_now[:, s, :, 0:D]
                        if isinstance(i, int) and i == GROUPS - 1:
                            sp.dma_start(dst[0:TAIL], row_parts[1].rearrange("p (j d) -> p j d", d=D))\
                                .then_inc(s_rows[s].sem, 16)
                        else:
                            part = row_parts[0][:, i, :] if isinstance(i, int) else \
                                row_parts[0][:, ds(i, 1), :].rearrange("p o f -> p (o f)")
                            sp.dma_start(dst, part.rearrange("p (j d) -> p j d", d=D)).then_inc(s_rows[s].sem, 16)

                    stepped(sp, GROUPS, 2, load)


                @block.gpsimd
                def _(g):
                    def group(i, s):
                        parts = TAIL if isinstance(i, int) and i == GROUPS - 1 else P
                        if not first(i, 2):
                            g.wait_ge(s_rscat[s].sem, (i - s) * (8 * J))
                            g.sem_inc(s_go.sem, 1)
                        g.tensor_copy(addr_now[:, s, :], addr_src[:, cut(i * J, J)]).then_inc(s_acopy.sem, 1)
                        g.tensor_copy(rows_now[:, s, :, D:D + 1].rearrange("p j o -> p (j o)"),
                                      lo_src[:, cut(i * J, J)]).then_inc(s_acopy.sem, 1)
                        g.wait_ge(s_acopy.sem, i * 2 + 2)
                        g.wait_ge(s_rows[s].sem, (i - s) * 8 + 16)
                        g.sem_inc(s_go.sem, 1)
                        for j in range(J):
                            g.indirect_dma_start(
                                attr_rows, bass.IndirectOffsetOnAxis(ap=addr_now[0:parts, s, j:j + 1], axis=0),
                                rows_now[0:parts, s, j, :], None).then_inc(s_rscat[s].sem, 16)

                    stepped(g, GROUPS, 2, group)
                    g.wait_ge(s_rscat[0].sem, 16 * J * ((GROUPS + 1) // 2))
                    g.wait_ge(s_rscat[1].sem, 16 * J * (GROUPS // 2))

                @block.scalar
                def _(act):
                    rel_act(act)

                @block.tensor
                def _(pe):
                    rel_pe(pe)

                @block.vector
                def _(v):
                    v.wait_ge(s_list.sem, 16)
                    n = [0]

                    def chain(ins):
                        n[0] += 1
                        ins.then_inc(s_chain.sem, 1)
                        v.wait_ge(s_chain.sem, s_chain.at(n[0]))

                    v.memset(node[:, T:T + AHEAD], float(NONE))
                    v.memset(idx_all[:, T:T + HALF], 0)
                    v.memset(ones_b[:], 1.0)
                    v.tensor_scalar(ident_row[:], ident[:], float(P), None, ALU.mult)
                    v.tensor_scalar(edge_diag[:], ident[:], pidx[:, 0:1], None, ALU.mult)
                    v.memset(w3[:, T:T + AHEAD], 0.0)
                    v.memset(w16[:, T:T + AHEAD], 0.0)
                    for to, at, mask in ((node[:, 0:T], LO_AT, (1 << LO_BITS) - 1), (bufs["type3"], E3_AT, 3),
                                         (bufs["type16"], E16_AT, 15)):
                        chain(v.tensor_scalar(tmp_i1[:], words[:], at, mask, ALU.logical_shift_right, ALU.bitwise_and))
                        chain(v.tensor_copy(to, tmp_i1[:]))
                    table_rows(v, chain, E4_AT, 3, T4)
                    v.tensor_tensor(b_rz[:], b_ih[:, 0:2], b_hh[:, 0:2], ALU.add)
                    rel_dve(v)
                    done_chain[0] = n[0]
            norm_over()
            table_over()
            s_chain.done(done_chain[0])

        s_idx, s_got = sem("index_copied"), [sem(f"got{k}", 16) for k in range(U)]
        g_oh, g_mm, g_add = sem("one_hot"), sem("summed"), sem("added")

        def gather_bufs(to, width=P):
            bufs["msg"] = sb("msg", [P, U, D], F32, to)
            bufs["oh"] = sb("oh", [P, 2 * G, width], F32, to)
            bufs["idx_now"] = sb("idx_now", [P, 2, HALF], I32, to)

        def gather_pool(g, table):
            def turn(c, _):
                for s in range(U):
                    h = s // HALF
                    if s % HALF == 0:
                        g.wait_ge(s_idx.sem, s_idx.at(c * 2 + (h + 1)))
                        g.sem_inc(s_go.sem, 1)
                    g.indirect_dma_start(
                        bufs["msg"][:, s, :], None, table,
                        bass.IndirectOffsetOnAxis(ap=bufs["idx_now"][:, h, s % HALF:s % HALF + 1], axis=0))\
                        .then_inc(s_got[s].sem, 16)

            stepped(g, T // U, 1, turn)

        def gather_act(act, g, q):
            if q % 2:
                return
            if q >= 0 and not first(g, 1):
                act.wait_ge(g_mm.sem, g_mm.at(g))
            act.activation(bufs["idx_now"][:, (q // 2 + 1) % 2, :], idx_all[:, cut((g + 2) * G, HALF)], ACT.Copy)\
                .then_inc(s_idx.sem, 1)

        def gather_pe(pe, g, q, width=P):
            pe.wait_ge(g_oh.sem, g_oh.at(g + 1))
            if not first(g, 2):
                pe.wait_ge(g_add.sem, g_add.at((g - 1) * G))
            for k in range(G):
                got = s_got[q * G + k]
                pe.wait_ge(got.sem, (g - q) * (16 // TURN) + got.at(1))
                last = nc.tensor.matmul(sum_of(q, k, width), lhsT=bufs["msg"][:, q * G + k, :],
                                        rhs=bufs["oh"][:, (q % 2) * G + k, :], start=True, stop=True)
            last.then_inc(g_mm.sem, 1)

        def sum_of(q, k, width):
            if width * G <= 512:
                return ps[:, q % 2, k * width:(k + 1) * width]
            return ps[:, (q % 2) * G + k, 0:width]

        def one_hot(v, g, q, code, weight, width):
            if not first(g, 2):
                v.wait_ge(g_mm.sem, g_mm.at(g - 1))
            if weight is None:
                v.tensor_tensor(bufs["oh"][:, (q % 2) * G:(q % 2 + 1) * G, :],
                                iota[:, 0:width].unsqueeze(1).to_broadcast([P, G, width]),
                                code[:, cut(g * G, G)].unsqueeze(2).to_broadcast([P, G, width]), ALU.is_equal)\
                    .then_inc(g_oh.sem, 1)
                return
            for k in range(G):
                last = v.tensor_scalar(bufs["oh"][:, (q % 2) * G + k, :], iota[:, 0:width], code[:, cut(g * G + k, 1)],
                                       weight[:, cut(g * G + k, 1)], ALU.is_equal, ALU.mult)
            last.then_inc(g_oh.sem, 1)

        def add_sum(v, g, q, k, blocks, width, to):
            i = g * G + k
            if k == 0:
                v.wait_ge(g_mm.sem, g_mm.at(g + 1))
            if not first(i, 1):
                v.wait_ge(g_add.sem, g_add.at(i))
            at = to[:, ds(blocks[k] * width, width)]
            v.tensor_tensor(at, sum_of(q, k, width), at, ALU.add).then_inc(g_add.sem, 1)

        def gather_over():
            g_oh.done(GROUPS_T + 1)
            g_mm.done(GROUPS_T)
            g_add.done(T)
            s_idx.done(GROUPS_T // 2 + 1)
            for k in range(U):
                s_got[k].done(T // U)

        def turns(eng, step, peel=1):
            stepped(eng, GROUPS_T, TURN, step, peel)

        def gather_pass(table, code, weight, width=P, to=sumT):
            with ExitStack() as own:
                gather_bufs(own, width)
                with nc.Block() as block:
                    @block.gpsimd
                    def _(g):
                        gather_pool(g, table)

                    @block.scalar
                    def _(act):
                        gather_act(act, -2, -2)
                        turns(act, lambda g, q: gather_act(act, g, q))

                    @block.tensor
                    def _(pe):
                        turns(pe, lambda g, q: gather_pe(pe, g, q, width))

                    @block.vector
                    def _(v):
                        v.memset(to[:, 0:NB * width], 0.0)
                        one_hot(v, 0, 0, code, weight, width)

                        def step(g, q):
                            one_hot(v, g + 1, q + 1, code, weight, width)
                            blocks = blocks_of(nc, v, block_dst, g * G)
                            for k in range(G):
                                add_sum(v, g, q, k, blocks, width, to)

                        turns(v, step)
            gather_over()

        AU = GROUPS_T
        FLUSH = 12
        a_ld = [sem(f"attr_rows{k}", 16) for k in range(8)]
        a_dve, a_act, a_pe, a_self = sem("a_dve"), sem("a_act"), sem("a_pe"), sem("a_dve_own")
        KEY, SUM, CNT, PICK = 0, P, 2 * P, 2 * P + 1
        FEAT, NODES, ENDS, BACK = 0, P, 2 * P + 1, 2 * P + 3

        def agg_bufs(to):
            bufs["ar"] = sb("ar", [P, 8, ROW], F32, to)
            bufs["cols"] = sb("cols", [P, 8, 4], F32, to)
            bufs["node1"] = sb("node1", [P, 8, 1], BF16, to)
            bufs["aoh"] = sb("aoh", [P, 2, P], F32, to)
            bufs["diag"] = sb("diag", [P, 2, P], BF16, to)
            bufs["perm"] = sb("perm", [P, 4, P], F32, to)
            bufs["permb"] = sb("permb", [P, 2, P + 2], BF16, to)
            bufs["lob"] = sb("lob", [P, 2, P], BF16, to)
            bufs["sorted"] = sb("sorted", [P, 2, 2 * P + 3], F32, to)
            bufs["fall"] = sb("fall", [P, P], F32, to)
            bufs["scan"] = sb("scan", [P, 2, P], F32, to)
            bufs["last"] = sb("last", [P, 4, P], F32, to)
            bufs["back"] = sb("back", [P, 2, P + 1], F32, to)
            bufs["absent"] = sb("absent", [P, 1], F32, to)
            bufs["junk"] = sb("junk", [P, P], F32, to)
            bufs["huge"] = sb("huge", [P, 1], F32, to)

        def known(u, stage):
            return not isinstance(u, int) or 0 <= u - stage < AU

        def agg_sp(sp, part, u, s):
            if not first(u, 8):
                sp.wait_ge(a_pe.sem, a_pe.at(u - 1))
            rows_v = attr_rows.rearrange("(p t) w -> p (t w)", p=P)
            sp.dma_start(bufs["ar"][:, s, :], rows_v[:, cut((u + part * AU) * ROW, ROW)]).then_inc(a_ld[s].sem, 16)

        def signal(eng, last, step, u):
            if last is None:
                if not first(u, 1):
                    eng.wait_ge(step.sem, step.at(u))
                eng.sem_inc(step.sem, 1)
            else:
                last.then_inc(step.sem, 1)

        def agg_act(act, u, s):
            cols, ar, last = bufs["cols"], bufs["ar"], None

            def at(stage, n):
                return (s - stage) % n

            if not first(u, 1):
                act.wait_ge(a_dve.sem, a_dve.at(u))
                act.wait_ge(a_pe.sem, a_pe.at(u))
            if known(u, 7):
                last = act.activation(bufs["sorted"][:, at(7, 2), :], ps[:, 4 + at(1, 2), 0:2 * P + 3], ACT.Copy)
            if known(u, 10):
                last = act.activation(bufs["back"][:, at(10, 2), 0:P], ps[:, 4 + at(1, 2), BACK:BACK + P], ACT.Copy)
            if known(u, 5):
                last = act.activation(bufs["permb"][:, at(5, 2), 1:P + 1], bufs["perm"][:, at(5, 4), :], ACT.Copy)
                last = act.activation(bufs["lob"][:, at(5, 2), :], ones[:], ACT.Copy, scale=cols[:, at(5, 8), 2:3])
            if known(u, 1):
                t, n = at(1, 8), ar[:, at(1, 8), D:D + 1]
                act.wait_ge(a_ld[t].sem, a_ld[t].at(1) + (u - 1 - t) * 2)
                act.activation(cols[:, t, 0:1], n, ACT.Identity, bias=pidx[:, 0:1], scale=float(P))
                act.activation(cols[:, t, 2:3], n, ACT.Identity, bias=bufs["huge"][:, 0:1], scale=HUGE)
                last = act.activation(bufs["node1"][:, t, :], n, ACT.Identity, bias=ones[:, 0:1])
            if known(u, 2):
                last = act.activation(bufs["diag"][:, at(2, 2), :], ident_row[:], ACT.Copy, scale=ar[:, at(2, 8), D:D + 1])
            signal(act, last, a_act, u)

        def agg_pe(pe, u, s):
            ar, mm = bufs["ar"], nc.tensor.matmul
            dve_bank, act_bank = ps[:, 2 + s % 2, :], ps[:, 4 + s % 2, :]
            last = None

            def at(stage, n):
                return (s - stage) % n

            if not first(u, 1):
                pe.wait_ge(a_dve.sem, a_dve.at(u))
                pe.wait_ge(a_act.sem, a_act.at(u))
            if known(u, 3):
                mm(dve_bank[:, KEY:KEY + P], lhsT=ones_b[:], rhs=bufs["diag"][:, at(3, 2), :], start=True, stop=False)
                mm(dve_bank[:, KEY:KEY + P], lhsT=ones_b[:], rhs=edge_diag[:], start=False, stop=True)
                one = bufs["aoh"][:, at(3, 2), :]
                mm(dve_bank[:, SUM:SUM + P], lhsT=ar[:, at(3, 8), 0:D], rhs=one, start=True, stop=True)
                last = mm(dve_bank[:, CNT:CNT + 1], lhsT=one, rhs=ones[:, 0:1], start=True, stop=True)
            if known(u, 6):
                permb, node1 = bufs["permb"][:, at(6, 2), :], bufs["node1"][:, at(6, 8), :]
                mm(act_bank[:, FEAT:FEAT + P], lhsT=ar[:, at(6, 8), 0:D], rhs=bufs["perm"][:, at(6, 4), :],
                   start=True, stop=True)
                mm(act_bank[:, NODES:NODES + P + 1], lhsT=bufs["lob"][:, at(6, 2), :], rhs=permb[:, 0:P + 1],
                   start=True, stop=True)
                mm(act_bank[:, ENDS:ENDS + 1], lhsT=permb[:, 1:P + 1], rhs=node1, start=True, stop=True)
                last = mm(act_bank[:, ENDS + 1:ENDS + 2], lhsT=permb[:, 2:P + 2], rhs=node1, start=True, stop=True)
            if known(u, 9):
                last = pe.transpose(act_bank[:, BACK:BACK + P], bufs["scan"][:, at(9, 2), :], ident[:])
            if known(u, 11):
                last = mm(dve_bank[:, PICK:PICK + P + 1], lhsT=bufs["last"][:, at(11, 4), :],
                          rhs=bufs["back"][:, at(11, 2), :], start=True, stop=True)
            signal(pe, last, a_pe, u)

        def agg_dve(v, part, u, s):
            cols, ar, last = bufs["cols"], bufs["ar"], None
            bank = ps[:, 2 + (s - 1) % 2, :]

            def at(stage, n):
                return (s - stage) % n

            if s % G == 0:
                for name, stage in (("sum_blocks", 4), ("max_blocks", 12)):
                    if known(u, stage):
                        bufs[name] = blocks_of(nc, v, block_src, u + (part * AU - stage))
            if known(u, 1):
                blocks = blocks_of(nc, v, block_dst, (u - 1) * G)

            def add(k):
                if known(u, 1):
                    add_sum(v, u - 1, s - 1, k, blocks, P, sumT)

            if not first(u, 1):
                v.wait_ge(a_dve.sem, a_dve.at(u))
                v.wait_ge(a_pe.sem, a_pe.at(u))
                v.wait_ge(a_act.sem, a_act.at(u))
            add(0)
            if known(u, 4):
                v.tensor_scalar(bufs["junk"][:], bank[:, KEY:KEY + P], cols[:, at(4, 8), 0:1], None, ALU.is_lt, ALU.add,
                                accum_out=cols[:, at(4, 8), 1:2]).then_inc(a_self.sem, 1)
            if known(u, 8):
                x = bufs["sorted"][:, at(8, 2), :]
                v.tensor_tensor(bufs["fall"][:], x[:, NODES:NODES + P], x[:, NODES + 1:NODES + P + 1], ALU.subtract)\
                    .then_inc(a_self.sem, 1)
                v.scalar_tensor_tensor(cols[:, at(8, 8), 3:4], x[:, ENDS:ENDS + 1], x[:, ENDS + 1:ENDS + 2],
                                       x[:, ENDS:ENDS + 1], ALU.not_equal, ALU.mult)
            if known(u, 12):
                v.tensor_scalar(bufs["absent"][:], bank[:, PICK + P:PICK + P + 1], -1.0, FMAX, ALU.add, ALU.mult)\
                    .then_inc(a_self.sem, 1)
            if known(u, 2):
                last = v.tensor_scalar(bufs["aoh"][:, at(2, 2), :], iota[:, 0:P], ar[:, at(2, 8), D:D + 1], None, ALU.is_equal)
            own = a_own(u)
            add(1)
            if known(u, 4):
                v.wait_ge(a_self.sem, own(1))
                last = v.tensor_scalar(bufs["perm"][:, at(4, 4), :], iota[:, 0:P], cols[:, at(4, 8), 1:2], None, ALU.is_equal)
            if known(u, 8):
                v.wait_ge(a_self.sem, own(2))
                last = v.tensor_tensor_scan(bufs["scan"][:, at(8, 2), :], bufs["fall"][:], x[:, FEAT:FEAT + P], -BIG, ALU.add, ALU.max)
            add(2)
            if known(u, 9):
                last = v.tensor_scalar(bufs["last"][:, at(9, 4), :], iota[:, 0:P], 1.0, cols[:, at(9, 8), 3:4],
                                ALU.add, ALU.is_equal)
            if known(u, 12):
                v.wait_ge(a_self.sem, own(3))
                to = attr_max[:, ds(bufs["max_blocks"][s % G] * P, P)]
                last = v.scalar_tensor_tensor(to, bank[:, PICK:PICK + P], bufs["absent"][:, 0:1], to, ALU.add, ALU.max)
            add(3)
            if known(u, 4):
                b = bufs["sum_blocks"][s % G]
                to = attr_sumT[:, ds(b * P, P)]
                v.tensor_tensor(to, bank[:, SUM:SUM + P], to, ALU.add)
                to = attr_count[:, ds(b, 1)]
                last = v.tensor_tensor(to, bank[:, CNT:CNT + 1], to, ALU.add)
            signal(v, last, a_dve, u)

        def a_own(u):
            def before(stage):
                return u - stage if not isinstance(u, int) else min(max(u - stage, 0), AU)

            def own(k):
                total = a_self.base
                for n, stage in enumerate((4, 8, 12)):
                    total = before(stage) + total
                    if n < k and known(u, stage):
                        total = total + 1
                return total

            return own

        def agg_over():
            for c in (a_dve, a_act, a_pe):
                c.done(AU + FLUSH)
            a_self.done(3 * AU)
            for c in a_ld:
                c.done(AU // 8)

        r_mm, r_rz, r_t1, r_t2 = sem("r_mm"), sem("r_rz"), sem("r_t1"), sem("r_t2")
        r_n, r_d, r_e, r_cp = sem("r_n"), sem("r_d"), sem("r_e"), sem("r_cp")

        def gru(table):
            with ExitStack() as own:
                table_bufs(own, T4 * D)
                rz = sb("rz", [P, 2, 2 * PAIR], F32, own)
                t1 = sb("t1", [P, 2, PAIR], F32, own)
                t2 = sb("t2", [P, 2, PAIR], F32, own)
                nn = sb("nn", [P, 2, PAIR], F32, own)
                h_now = bufs["h"]
                with nc.Block() as block:
                    @block.tensor
                    def _(pe):
                        def step(i, s):
                            a_, h_ = sumT[:, col(i)], hT[:, col(i)]
                            if not first(i, 2):
                                pe.wait_ge(r_t2.sem, r_t2.at(i - 1))
                                pe.wait_ge(r_rz.sem, r_rz.at(i - 1))
                            for k in range(2):
                                o = ps[:, s, k * PAIR:(k + 1) * PAIR]
                                nc.tensor.matmul(o, lhsT=gate_w[:, k, :], rhs=a_, start=True, stop=False)
                                nc.tensor.matmul(o, lhsT=gate_w[:, 3 + k, :], rhs=h_, start=False, stop=True)
                            nc.tensor.matmul(ps[:, 2 + s, 0:PAIR], lhsT=gate_w[:, 2, :], rhs=a_, start=True, stop=True)
                            nc.tensor.matmul(ps[:, 2 + s, PAIR:2 * PAIR], lhsT=gate_w[:, 5, :], rhs=h_,
                                             start=True, stop=True).then_inc(r_mm.sem, 1)
                            if table and not first(i, 1):
                                table_pe(pe, i - 1, 1 - s, edge_w, T4 * D)

                        stepped(pe, STEPS, 2, step, peel=2)
                        if table:
                            table_pe(pe, STEPS - 1, (STEPS - 1) % 2, edge_w, T4 * D)

                    @block.scalar
                    def _(act):
                        def copy(j, s):
                            act.wait_ge(h_ready.sem, h_ready.at(j + 1))
                            act.activation(hT[:, col(j)], h_now[:, s, :], ACT.Copy).then_inc(r_cp.sem, 1)

                        def step(i, s):
                            act.wait_ge(r_mm.sem, r_mm.at(i + 1))
                            if not first(i, 2):
                                act.wait_ge(h_ready.sem, h_ready.at(i - 1))
                            for k in range(2):
                                last = act.activation(rz[:, s, k * PAIR:(k + 1) * PAIR], ps[:, s, k * PAIR:(k + 1) * PAIR],
                                                      ACT.Sigmoid, bias=b_rz[:, k:k + 1])
                            last.then_inc(r_rz.sem, 1)
                            if not first(i, 1):
                                copy(i - 1, 1 - s)
                            act.wait_ge(r_t2.sem, r_t2.at(i + 1))
                            act.activation(nn[:, s, :], t2[:, s, :], ACT.Tanh, bias=b_ih[:, 2:3]).then_inc(r_n.sem, 1)

                        stepped(act, STEPS, 2, step, peel=2)
                        copy(STEPS - 1, (STEPS - 1) % 2)

                    @block.vector
                    def _(v):
                        def step(i, s):
                            r, z = rz[:, s, 0:PAIR], rz[:, s, PAIR:2 * PAIR]
                            v.wait_ge(r_rz.sem, r_rz.at(i + 1))
                            v.scalar_tensor_tensor(t1[:, s, :], ps[:, 2 + s, PAIR:2 * PAIR], b_hh[:, 2:3], r,
                                                   ALU.add, ALU.mult).then_inc(r_t1.sem, 1)
                            v.wait_ge(r_t1.sem, r_t1.at(i + 1))
                            v.tensor_tensor(t2[:, s, :], ps[:, 2 + s, 0:PAIR], t1[:, s, :], ALU.add).then_inc(r_t2.sem, 1)
                            if table and not first(i, 1):
                                table_dve(v, i - 1, 1 - s, edge_bias[:], T4 * D)
                            v.wait_ge(r_n.sem, r_n.at(i + 1))
                            v.tensor_tensor(t1[:, s, :], hT[:, col(i)], nn[:, s, :], ALU.subtract).then_inc(r_d.sem, 1)
                            v.wait_ge(r_d.sem, r_d.at(i + 1))
                            v.tensor_tensor(t2[:, s, :], z, t1[:, s, :], ALU.mult).then_inc(r_e.sem, 1)
                            v.wait_ge(r_e.sem, r_e.at(i + 1))
                            if not first(i, 2):
                                v.wait_ge(r_cp.sem, r_cp.at(i - 1))
                                if table:
                                    v.wait_ge(t_mm.sem, t_mm.at(i - 1))
                            v.tensor_tensor(h_now[:, s, :], nn[:, s, :], t2[:, s, :], ALU.add).then_inc(h_ready.sem, 1)

                        stepped(v, STEPS, 2, step, peel=2)
                        if table:
                            table_dve(v, STEPS - 1, (STEPS - 1) % 2, edge_bias[:], T4 * D)

                    @block.sync
                    def _(sp):
                        if table:
                            stepped(sp, STEPS, 2, lambda i, s: table_store(sp, i, s, table4, T4 * D))
                            table_stored(sp)
            for c in (r_mm, r_rz, r_t1, r_t2, r_n, r_d, r_e, r_cp):
                c.done(STEPS)
            if table:
                table_over()
            else:
                h_ready.done(STEPS)

        s_init = sem("init")
        for part in range(4):
            with ExitStack() as own:
                gather_bufs(own)
                agg_bufs(own)
                with nc.Block() as block:
                    @block.sync
                    def _(sp):
                        stepped(sp, AU, 8, lambda u, s: agg_sp(sp, part, u, s))

                    @block.gpsimd
                    def _(g):
                        gather_pool(g, table4)

                    @block.scalar
                    def _(act):
                        gather_act(act, -2, -2)
                        act.wait_ge(s_init.sem, part + 1)

                        def step(u, s):
                            if known(u, 0):
                                gather_act(act, u, s)
                            agg_act(act, u, s)

                        stepped(act, AU, 8, step, peel=2)
                        for s in range(FLUSH):
                            step(AU + s, s)

                    @block.tensor
                    def _(pe):
                        def step(u, s):
                            if known(u, 0):
                                gather_pe(pe, u, s % TURN)
                            agg_pe(pe, u, s)

                        stepped(pe, AU, 8, step, peel=2)
                        for s in range(FLUSH):
                            step(AU + s, s)

                    @block.vector
                    def _(v):
                        v.memset(bufs["permb"][:, :, 0:1].rearrange("p s o -> p (s o)"), 0.0)
                        v.memset(bufs["permb"][:, :, P + 1:P + 2].rearrange("p s o -> p (s o)"), 0.0)
                        v.memset(bufs["huge"][:], HUGE)
                        v.memset(bufs["back"][:, :, P:P + 1].rearrange("p s o -> p (s o)"), 1.0)
                        if part == 0:
                            v.memset(attr_count[:], 0.0)
                            v.memset(attr_sumT, 0.0)
                            v.memset(attr_max, -FMAX)
                        v.memset(sumT, 0.0).then_inc(s_init.sem, 1)
                        v.wait_ge(s_init.sem, part + 1)
                        one_hot(v, 0, 0, node, None, P)

                        def step(u, s):
                            if known(u, 0):
                                one_hot(v, u + 1, s + 1, node, None, P)
                            agg_dve(v, part, u, s)

                        stepped(v, AU, 8, step, peel=2)
                        for s in range(FLUSH):
                            step(AU + s, s)
            gather_over()
            agg_over()
            gru(part < 3)

        l0.close()

        def normalise(add, load=None):
            norm_bufs()
            with nc.Block() as block:
                @block.tensor
                def _(pe):
                    norm_pe(pe, add)

                @block.scalar
                def _(act):
                    norm_act(act)

                @block.vector
                def _(v):
                    norm_dve(v, add)

                if load:
                    @block.sync
                    def _(sp):
                        load(sp)
            norm_over(add)

        m_h, m_r, m_o = sem("m_hidden"), sem("m_relu"), sem("m_out")

        def hidden_pe(pe, i, chunks, w1, inputs):
            for c in range(chunks):
                if c % 2 == 0 and not first(i, 1):
                    pe.wait_ge(m_r.sem, m_r.at(i * (chunks // 2) + (c // 2 + 1 - chunks // 2)))
                for n, rhs in enumerate(inputs):
                    last = nc.tensor.matmul(ps[:, c // 2, (c % 2) * PAIR:(c % 2 + 1) * PAIR], lhsT=w1(n, c), rhs=rhs,
                                            start=n == 0, stop=n == len(inputs) - 1)
                if c % 2:
                    last.then_inc(m_h.sem, 1)

        def hidden_act(act, i, s, chunks, hid, b1):
            if not first(i, 2):
                act.wait_ge(m_o.sem, m_o.at(i - 1))
            for c in range(chunks):
                if c % 2 == 0:
                    act.wait_ge(m_h.sem, m_h.at(i * (chunks // 2) + (c // 2 + 1)))
                last = act.activation(hid[:, s, c, :], ps[:, c // 2, (c % 2) * PAIR:(c % 2 + 1) * PAIR], ACT.Relu,
                                      bias=b1[:, c:c + 1])
                if c % 2:
                    last.then_inc(m_r.sem, 1)

        def two_over(chunks):
            m_h.done(STEPS * chunks // 2)
            m_r.done(STEPS * chunks // 2)
            m_o.done(STEPS)

        def columns(sp, to, ap, n, load):
            with nc.allow_non_contiguous_dma(reason="a few biases, one element a partition"):
                sp.dma_start(to, ap.rearrange("(c p) -> p c", p=P) if n > 1 else ap.rearrange("(p o) -> p o", o=1))\
                    .then_inc(load, 16)

        e_w, e_st, e_tp, e_in, e_x, e_b, e_xx = sem("e_weights"), sem("e_staged"), sem("e_transposed"), sem("e_inputs"), sem("e_x"), sem("e_bias"), sem("e_xx")
        with ExitStack() as own:
            w1 = sb("e_w1", [P, 4, H1], F32, own)
            w2 = sb("e_w2", [P, C1, D], F32, own)
            vec = sb("e_vec", [P, 4, C1], F32, own)
            u0 = sb("e_u", [P, 1], F32, own)
            inv = sb("e_inv", [P, NB], F32, own)
            some = sb("e_some", [P, NB], F32, own)
            nat = sb("e_nat", [P, 2, PAIR], F32, own)
            diag = sb("e_diag", [P, 2, PAIR], F32, own)
            maxT = sb("e_maxT", [P, 2, PAIR], F32, own)
            meanT = sb("e_meanT", [P, 2, PAIR], F32, own)
            hid = sb("e_hid", [P, 2, C1, PAIR], F32, own)
            sumx = sb("e_sumx", [P, PAIR], F32, own)
            def load_weights(sp):
                sp.dma_start(w1[:], a["L1_gnn_W1"][0:4 * P, :].rearrange("(c p) h -> p c h", p=P)).then_inc(e_w.sem, 16)
                sp.dma_start(w2[:], a["L1_gnn_W2"].rearrange("(c p) h -> p c h", p=P)).then_inc(e_w.sem, 16)
                columns(sp, vec[:, 0, :], a["L1_gnn_b1"], C1, e_w.sem)
                columns(sp, vec[:, 1, :], a["L1_gnn_W1"][4 * P:4 * P + 1, :].rearrange("o h -> (o h)"), C1, e_w.sem)
                columns(sp, vec[:, 3, 0:1], a["L1_gnn_b2"], 1, e_w.sem)
                sp.dma_start(u0[0:1, :], a["L1_gnn_u"][0:1, :]).then_inc(e_w.sem, 16)

            normalise(True, load_weights)
            with nc.Block() as block:
                @block.gpsimd
                def _(g):
                    g.wait_ge(e_w.sem, 96)
                    g.partition_broadcast(u0[:], u0[0:1, :], P).then_inc(e_b.sem, 1)

                @block.tensor
                def _(pe):
                    pe.wait_ge(e_w.sem, 96)

                    def hidden(j, s):
                        pe.wait_ge(e_in.sem, j + 1)
                        hidden_pe(pe, j, C1, lambda n, c: w1[:, n, c * P:(c + 1) * P],
                                  [hT[:, col(j)], attr_sumT[:, col(j)], maxT[:, s, :], meanT[:, s, :]])

                    def output(j, s):
                        pe.wait_ge(m_r.sem, m_r.at(j * (C1 // 2) + C1 // 2))
                        if not first(j, 2):
                            pe.wait_ge(e_x.sem, j - 1)
                        for c in range(C1):
                            last = nc.tensor.matmul(ps[:, 4 + s, 0:PAIR], lhsT=w2[:, c, :], rhs=hid[:, s, c, :],
                                                    start=c == 0, stop=c == C1 - 1)
                        last.then_inc(m_o.sem, 1)

                    def step(i, s):
                        pe.wait_ge(e_st.sem, i + 1)
                        if not first(i, 2):
                            pe.wait_ge(e_in.sem, i - 1)
                        for j in range(2):
                            pe.transpose(ps[:, 6 + s, j * P:(j + 1) * P], nat[:, s, j * P:(j + 1) * P], ident[:])
                        nc.tensor.matmul(ps[:, 6 + s, PAIR:2 * PAIR], lhsT=ones[:], rhs=diag[:, s, :],
                                         start=True, stop=True).then_inc(e_tp.sem, 1)
                        if not first(i, 1):
                            hidden(i - 1, 1 - s)
                        if not first(i, 2):
                            output(i - 2, s)

                    stepped(pe, STEPS, 2, step, peel=2)
                    hidden(STEPS - 1, (STEPS - 1) % 2)
                    output(STEPS - 2, STEPS % 2)
                    output(STEPS - 1, (STEPS - 1) % 2)

                @block.scalar
                def _(act):
                    act.wait_ge(e_b.sem, 5)

                    def step(i, s):
                        if not first(i, 2):
                            act.wait_ge(e_tp.sem, i - 1)
                        for j in range(2):
                            blk = cut(2 * i + j, 1)
                            act.activation(nat[:, s, j * P:(j + 1) * P], attr_max[:, cut((2 * i + j) * P, P)],
                                           ACT.Copy, scale=some[:, blk])
                            last = act.activation(diag[:, s, j * P:(j + 1) * P], ident[:], ACT.Copy, scale=inv[:, blk])
                        last.then_inc(e_st.sem, 1)
                        if not first(i, 1):
                            hidden_act(act, i - 1, 1 - s, C1, hid, vec[:, 2, :])

                    stepped(act, STEPS, 2, step, peel=2)
                    hidden_act(act, STEPS - 1, (STEPS - 1) % 2, C1, hid, vec[:, 2, :])

                @block.vector
                def _(v):
                    v.wait_ge(e_b.sem, 1)
                    v.scalar_tensor_tensor(vec[:, 2, :], vec[:, 1, :], u0[:, 0:1], vec[:, 0, :], ALU.mult, ALU.add)\
                        .then_inc(e_b.sem, 1)
                    v.tensor_scalar(some[:], attr_count[:], 1.0, None, ALU.min).then_inc(e_b.sem, 1)
                    v.tensor_scalar(inv[:], attr_count[:], 1.0, None, ALU.max).then_inc(e_b.sem, 1)
                    v.wait_ge(e_b.sem, 4)
                    v.reciprocal(inv[:], inv[:]).then_inc(e_b.sem, 1)

                    def output(j, s):
                        v.wait_ge(m_o.sem, m_o.at(j + 1))
                        v.scalar_tensor_tensor(sumx[:], ps[:, 4 + s, 0:PAIR], vec[:, 3, 0:1], xT[:, col(j)],
                                               ALU.add, ALU.add).then_inc(e_x.sem, 1)
                        v.wait_ge(e_x.sem, j + 1)
                        v.tensor_tensor(xT[:, col(j)], sumx[:], hT[:, col(j)], ALU.add).then_inc(e_xx.sem, 1)
                        v.wait_ge(e_xx.sem, j + 1)

                    def step(i, s):
                        v.wait_ge(e_tp.sem, i + 1)
                        if not first(i, 2):
                            v.wait_ge(m_h.sem, m_h.at((i - 1) * (C1 // 2)))
                        v.tensor_copy(maxT[:, s, :], ps[:, 6 + s, 0:PAIR])
                        v.tensor_tensor(meanT[:, s, :], attr_sumT[:, col(i)], ps[:, 6 + s, PAIR:2 * PAIR], ALU.mult)\
                            .then_inc(e_in.sem, 1)
                        if not first(i, 2):
                            output(i - 2, s)

                    stepped(v, STEPS, 2, step, peel=2)
                    output(STEPS - 2, STEPS % 2)
                    output(STEPS - 1, (STEPS - 1) % 2)
        two_over(C1)

        q_w, q_s, c_w = sem("q_weights"), sem("q_copied"), sem("conv_weights")
        c1w = sb("c1w", [P, T3 + 1, H2], F32, l0)
        c2w = sb("c2w", [P, C2, (T3 + 1) * D], F32, l0)
        v3 = sb("v3", [P, 4, C2], F32, l0)
        node3 = sb("node3", [P, T + AHEAD], F32, l0)
        with ExitStack() as own:
            qw1 = sb("qw1", [P, H2], F32, own)
            qw2 = sb("qw2", [P, C2, D], F32, own)
            table_bufs(own, D)
            hid = sb("q_hid", [P, 2, C2, PAIR], F32, own)
            def load_weights(sp):
                sp.dma_start(qw1[:], a["L2_gnn_q_w1"]).then_inc(q_w.sem, 16)
                sp.dma_start(qw2[:], a["L2_gnn_q_w2"].rearrange("(c p) h -> p c h", p=P)).then_inc(q_w.sem, 16)
                columns(sp, v3[:, 0, :], a["L2_gnn_q_b1"], C2, q_w.sem)
                columns(sp, v3[:, 1, :], a["L2_gnn_c1_b"], C2, q_w.sem)
                columns(sp, v3[:, 2, 0:1], a["L2_gnn_q_b2"], 1, q_w.sem)
                columns(sp, v3[:, 3, 0:1], a["L2_gnn_c2_b"], 1, q_w.sem)
                sp.dma_start(c1w[:, 0:T3, :], a["L2_gnn_c1_wrel"].rearrange("r p h -> p r h")).then_inc(c_w.sem, 16)
                sp.dma_start(c1w[:, T3, :], a["L2_gnn_c1_wroot"]).then_inc(c_w.sem, 16)
                for r in range(T3):
                    sp.dma_start(c2w[:, :, r * D:(r + 1) * D],
                                 a["L2_gnn_c2_wrel"][r, :, :].rearrange("(c p) o -> p c o", p=P)).then_inc(c_w.sem, 16)
                sp.dma_start(c2w[:, :, T3 * D:], a["L2_gnn_c2_wroot"].rearrange("(c p) o -> p c o", p=P)).then_inc(c_w.sem, 16)

            normalise(False, load_weights)
            with nc.Block() as block:
                @block.sync
                def _(sp):
                    stepped(sp, STEPS, 2, lambda i, s: table_store(sp, i, s, table1, D))
                    table_stored(sp)

                @block.tensor
                def _(pe):
                    pe.wait_ge(q_w.sem, 16 * 6)

                    def output(j, s):
                        pe.wait_ge(m_r.sem, m_r.at(j * (C2 // 2) + C2 // 2))
                        if not first(j, 1):
                            pe.wait_ge(h_ready.sem, h_ready.at(j))
                        for c in range(C2):
                            last = nc.tensor.matmul(ps[:, 3, 0:PAIR], lhsT=qw2[:, c, :], rhs=hid[:, s, c, :],
                                                    start=c == 0, stop=c == C2 - 1)
                        last.then_inc(m_o.sem, 1)

                    def step(i, s):
                        hidden_pe(pe, i, C2, lambda n, c: qw1[:, c * P:(c + 1) * P], [hT[:, col(i)]])
                        if not first(i, 1):
                            output(i - 1, 1 - s)
                        if not first(i, 2):
                            table_pe(pe, i - 2, s, None, D)

                    stepped(pe, STEPS, 2, step, peel=2)
                    output(STEPS - 1, (STEPS - 1) % 2)
                    table_pe(pe, STEPS - 2, STEPS % 2, None, D)
                    table_pe(pe, STEPS - 1, (STEPS - 1) % 2, None, D)

                @block.scalar
                def _(act):
                    act.wait_ge(q_w.sem, 16 * 6)

                    def output(j, s):
                        act.wait_ge(m_o.sem, m_o.at(j + 1))
                        if not first(j, 2):
                            act.wait_ge(t_mm.sem, t_mm.at(j - 1))
                        act.activation(bufs["h"][:, s, :], ps[:, 3, 0:PAIR], ACT.Identity, bias=v3[:, 2, 0:1])\
                            .then_inc(h_ready.sem, 1)
                        act.wait_ge(h_ready.sem, h_ready.at(j + 1))
                        act.activation(hT[:, col(j)], bufs["h"][:, s, :], ACT.Copy).then_inc(q_s.sem, 1)

                    def step(i, s):
                        hidden_act(act, i, s, C2, hid, v3[:, 0, :])
                        if not first(i, 2):
                            output(i - 2, s)

                    stepped(act, STEPS, 2, step, peel=2)
                    output(STEPS - 2, STEPS % 2)
                    output(STEPS - 1, (STEPS - 1) % 2)

                @block.vector
                def _(v):
                    n = [0]

                    def chain(ins):
                        n[0] += 1
                        ins.then_inc(s_chain.sem, 1)
                        v.wait_ge(s_chain.sem, s_chain.at(n[0]))

                    chain(v.tensor_scalar(tmp_i1[:], words[:], LO_AT, (1 << LO_BITS) - 1, ALU.logical_shift_right, ALU.bitwise_and))
                    chain(v.tensor_scalar(idx[:], words[:], E3_AT, 3, ALU.logical_shift_right, ALU.bitwise_and))
                    v.memset(node3[:, T:T + AHEAD], 0.0)
                    chain(v.scalar_tensor_tensor(node3[:, 0:T], idx[:], float(P), tmp_i1[:], ALU.mult, ALU.add))
                    table_rows(v, chain, 0, 0, 1)
                    stepped(v, STEPS, 2, lambda i, s: table_dve(v, i, s, None, D))
                    done_chain[0] = n[0]
        s_chain.done(done_chain[0])
        two_over(C2)
        table_over()

        gather_pass(table1, node3, w3, T3 * P, big[:])

        rel_sums = big[:].rearrange("p (b r n) -> p b r n", r=T3, n=P)
        with ExitStack() as own:
            table_bufs(own, T3 * D)
            hid = sb("c_hid", [P, 2, C2, PAIR], F32, own)
            with nc.Block() as block:
                @block.sync
                def _(sp):
                    stepped(sp, STEPS, 2, lambda i, s: table_store(sp, i, s, table3, T3 * D))
                    table_stored(sp)

                @block.tensor
                def _(pe):
                    def output(j, s):
                        pe.wait_ge(m_r.sem, m_r.at(j * (C2 // 2) + C2 // 2))
                        if not first(j, 1):
                            pe.wait_ge(h_ready.sem, h_ready.at(j))
                        for c in range(C2):
                            nc.tensor.matmul(ps[:, 3, 0:PAIR], lhsT=c2w[:, c, T3 * D:(T3 + 1) * D],
                                             rhs=hid[:, s, c, :], start=c == 0, stop=c == C2 - 1)
                        if not first(j, 2):
                            pe.wait_ge(t_ev.sem, t_ev.at(j - 1))
                        for k in range(2):
                            for c in range(C2):
                                last = nc.tensor.matmul(ps[:, 4 + 2 * s + k, 0:T3 * D],
                                                        lhsT=hid[:, s, c, k * P:(k + 1) * P],
                                                        rhs=c2w[:, c, 0:T3 * D], start=c == 0, stop=c == C2 - 1)
                        last.then_inc(t_mm.sem, 1)

                    pe.wait_ge(c_w.sem, 16 * (2 + T3 + 1))

                    def step(i, s):
                        hidden_pe(pe, i, C2, lambda n, c: c1w[:, n, c * P:(c + 1) * P],
                                  [rel_sums[:, cut(2 * i, 2), r, :] for r in range(T3)] + [hT[:, col(i)]])
                        if not first(i, 1):
                            output(i - 1, 1 - s)

                    stepped(pe, STEPS, 2, step, peel=2)
                    output(STEPS - 1, (STEPS - 1) % 2)

                @block.scalar
                def _(act):
                    def output(j, s):
                        act.wait_ge(t_mm.sem, t_mm.at(j + 1))
                        act.activation(hT[:, col(j)], ps[:, 3, 0:PAIR], ACT.Identity, bias=v3[:, 3, 0:1])\
                            .then_inc(h_ready.sem, 1)

                    def step(i, s):
                        if not first(i, 2):
                            act.wait_ge(t_mm.sem, t_mm.at(i - 1))
                        for c in range(C2):
                            if c % 2 == 0:
                                act.wait_ge(m_h.sem, m_h.at(i * (C2 // 2) + (c // 2 + 1)))
                            last = act.activation(hid[:, s, c, :], ps[:, c // 2, (c % 2) * PAIR:(c % 2 + 1) * PAIR],
                                                  ACT.Relu, bias=v3[:, 1, c:c + 1])
                            if c % 2:
                                last.then_inc(m_r.sem, 1)
                        if not first(i, 1):
                            output(i - 1, 1 - s)

                    stepped(act, STEPS, 2, step, peel=2)
                    output(STEPS - 1, (STEPS - 1) % 2)

                @block.vector
                def _(v):
                    n = [0]

                    def chain(ins):
                        n[0] += 1
                        ins.then_inc(s_chain.sem, 1)
                        v.wait_ge(s_chain.sem, s_chain.at(n[0]))

                    table_rows(v, chain, E3_AT, 3, T3)
                    stepped(v, STEPS, 2, lambda i, s: table_dve(v, i, s, None, T3 * D))
                    done_chain[0] = n[0]
        s_chain.done(done_chain[0])
        m_h.done(STEPS * C2 // 2)
        m_r.done(STEPS * C2 // 2)
        table_over()
        l0.close()

        gather_pass(table3, node, w3)

        y_w, y_a, y_r, y_mm, y_x = sem("y_weights"), sem("y_sum"), sem("y_relu"), sem("y_mm"), sem("y_x")
        with ExitStack() as own:
            lin = sb("lin", [P, D], F32, own)
            lin_b = sb("lin_b", [P, 1], F32, own)
            st = sb("lin_in", [P, 2, PAIR], F32, own)
            rl = sb("lin_relu", [P, 2, PAIR], F32, own)
            with nc.Block() as block:
                @block.sync
                def _(sp):
                    sp.dma_start(lin[:], a["L2_gnn_lin_w"]).then_inc(y_w.sem, 16)
                    columns(sp, lin_b[:], a["L2_gnn_lin_b"], 1, y_w.sem)

                @block.scalar
                def _(act):
                    def step(i, s):
                        act.wait_ge(y_a.sem, i + 1)
                        if not first(i, 2):
                            act.wait_ge(y_mm.sem, i - 1)
                        act.activation(rl[:, s, :], st[:, s, :], ACT.Relu).then_inc(y_r.sem, 1)

                    stepped(act, STEPS, 2, step)

                @block.tensor
                def _(pe):
                    pe.wait_ge(y_w.sem, 32)

                    def step(i, s):
                        pe.wait_ge(y_r.sem, i + 1)
                        if not first(i, 2):
                            pe.wait_ge(y_x.sem, i - 1)
                        nc.tensor.matmul(ps[:, s, 0:PAIR], lhsT=lin[:], rhs=rl[:, s, :], start=True, stop=True)\
                            .then_inc(y_mm.sem, 1)

                    stepped(pe, STEPS, 2, step)

                @block.vector
                def _(v):
                    v.wait_ge(y_w.sem, 32)

                    def output(j, s):
                        v.wait_ge(y_mm.sem, j + 1)
                        v.scalar_tensor_tensor(xT[:, col(j)], ps[:, s, 0:PAIR], lin_b[:, 0:1], xT[:, col(j)],
                                               ALU.add, ALU.add).then_inc(y_x.sem, 1)

                    def step(i, s):
                        if not first(i, 2):
                            v.wait_ge(y_r.sem, i - 1)
                        v.tensor_tensor(st[:, s, :], sumT[:, col(i)], hT[:, col(i)], ALU.add).then_inc(y_a.sem, 1)
                        if not first(i, 1):
                            output(i - 1, 1 - s)

                    stepped(v, STEPS, 2, step, peel=2)
                    output(STEPS - 1, (STEPS - 1) % 2)

        z_w, z_h, z_mm = sem("z_weights"), sem("z_h"), sem("z_mm")
        z_v, z_a, z_dma = sem("z_dve"), sem("z_act"), [sem("z_dma0", 16), sem("z_dma1", 16)]
        r4_mm, r4_a, r4_h = sem("r4_mm"), sem("r4_add"), sem("r4_h")
        rel_w = sb("rel_w", [P, 2, T16 * 32], F32, l0)
        root_w = sb("root_w", [P, 2, D], F32, l0)
        root_b = sb("root_b", [P, 2], F32, l0)

        def load_weights(sp):
            for k, n in enumerate(("L3_gnn_W1", "L3_gnn_W2")):
                sp.dma_start(rel_w[:, k, :].rearrange("p (r o) -> p r o", o=32),
                             a[n].rearrange("r b i o -> (b i) r o")).then_inc(z_w.sem, 16)
            for k, n in enumerate(("1", "2")):
                sp.dma_start(root_w[:, k, :], a["L3_gnn_root" + n]).then_inc(z_w.sem, 16)
                columns(sp, root_b[:, k:k + 1], a["L3_gnn_bias" + n], 1, z_w.sem)

        normalise(False, load_weights)

        def table_16(conv):
            with ExitStack() as own:
                hs = sb("z_hs", [P, 2, P], F32, own)
                rows = sb("z_rows", [P, 2, T16, 4, 32], F32, own)
                with nc.Block() as block:
                    @block.sync
                    def _(sp):
                        to = table16.rearrange("(b p r) d -> p b (r d)", p=P, r=T16)

                        def store(i, s):
                            sp.wait_ge(z_v.sem, z_v.at(i + 1))
                            sp.wait_ge(z_a.sem, z_a.at(i + 1))
                            at = to[:, i, :] if isinstance(i, int) else to[:, ds(i, 1), :].rearrange("p o f -> p (o f)")
                            sp.dma_start(at, rows[:, s].rearrange("p r b o -> p (r b o)")).then_inc(z_dma[s].sem, 16)

                        stepped(sp, NB, 2, store)
                        for s in range(2):
                            sp.wait_ge(z_dma[s].sem, z_dma[s].at(NB // 2))

                    @block.tensor
                    def _(pe):
                        pe.wait_ge(z_w.sem, 96)

                        def step(i, s):
                            pe.wait_ge(z_h.sem, z_h.at(i + 1))
                            if not first(i, 2):
                                pe.wait_ge(z_v.sem, z_v.at(i - 1))
                                pe.wait_ge(z_a.sem, z_a.at(i - 1))
                            for b in range(4):
                                q = slice(32 * b, 32 * b + 32)
                                last = nc.tensor.matmul(ps[:, 4 * s + b, :], lhsT=hs[q, s, :], rhs=rel_w[q, conv, :],
                                                        start=True, stop=True)
                            last.then_inc(z_mm.sem, 1)

                        stepped(pe, NB, 2, step)

                    @block.scalar
                    def _(act):
                        def evacuate(j, s):
                            act.wait_ge(z_mm.sem, z_mm.at(j + 1))
                            if not first(j, 2):
                                act.wait_ge(z_dma[s].sem, (j - s) * 8 + z_dma[s].base)
                            for b in (2, 3):
                                last = act.activation(rows[:, s, :, b, :], ps[:, 4 * s + b, :].rearrange("p (r o) -> p r o", o=32),
                                                      ACT.Copy)
                            last.then_inc(z_a.sem, 1)

                        def step(i, s):
                            if not first(i, 2):
                                act.wait_ge(z_mm.sem, z_mm.at(i - 1))
                            act.activation(hs[:, s, :], hT[:, cut(i * P, P)], ACT.Copy).then_inc(z_h.sem, 1)
                            if not first(i, 1):
                                evacuate(i - 1, 1 - s)

                        stepped(act, NB, 2, step, peel=2)
                        evacuate(NB - 1, (NB - 1) % 2)

                    @block.vector
                    def _(v):
                        n = [0]

                        def chain(ins):
                            n[0] += 1
                            ins.then_inc(s_chain.sem, 1)
                            v.wait_ge(s_chain.sem, s_chain.at(n[0]))

                        if conv == 0:
                            table_rows(v, chain, E16_AT, 15, T16)
                        done_chain[0] = n[0]

                        def evacuate(j, s):
                            v.wait_ge(z_mm.sem, z_mm.at(j + 1))
                            if not first(j, 2):
                                v.wait_ge(z_dma[s].sem, (j - s) * 8 + z_dma[s].base)
                            for b in (0, 1):
                                last = v.tensor_copy(rows[:, s, :, b, :], ps[:, 4 * s + b, :].rearrange("p (r o) -> p r o", o=32))
                            last.then_inc(z_v.sem, 1)

                        stepped(v, NB, 2, evacuate)
            s_chain.done(done_chain[0])
            for c in (z_h, z_mm, z_v, z_a):
                c.done(NB)
            for c in z_dma:
                c.done(NB // 2)

        table_16(0)
        gather_pass(table16, node, w16)
        with ExitStack() as own:
            st = sb("r4_st", [P, 2, PAIR], F32, own)
            with nc.Block() as block:
                @block.tensor
                def _(pe):
                    def step(i, s):
                        if not first(i, 2):
                            pe.wait_ge(r4_a.sem, r4_a.at(i - 1))
                        nc.tensor.matmul(ps[:, s, 0:PAIR], lhsT=root_w[:, 0, :], rhs=hT[:, col(i)], start=True, stop=True)\
                            .then_inc(r4_mm.sem, 1)

                    stepped(pe, STEPS, 2, step)

                @block.vector
                def _(v):
                    def step(i, s):
                        v.wait_ge(r4_mm.sem, r4_mm.at(i + 1))
                        if not first(i, 2):
                            v.wait_ge(r4_h.sem, r4_h.at(i - 1))
                        v.tensor_tensor(st[:, s, :], sumT[:, col(i)], ps[:, s, 0:PAIR], ALU.add).then_inc(r4_a.sem, 1)

                    stepped(v, STEPS, 2, step)

                @block.scalar
                def _(act):
                    def step(i, s):
                        act.wait_ge(r4_a.sem, r4_a.at(i + 1))
                        act.activation(hT[:, col(i)], st[:, s, :], ACT.Relu, bias=root_b[:, 0:1]).then_inc(r4_h.sem, 1)

                    stepped(act, STEPS, 2, step)
        for c in (r4_mm, r4_a, r4_h):
            c.done(STEPS)
        table_16(1)
        gather_pass(table16, node, w16)

        o_x, o_tp, o_cp, o_dma = sem("o_x"), sem("o_tp"), sem("o_cp"), [sem("o_dma0"), sem("o_dma1")]
        with ExitStack() as own:
            st = sb("o_st", [P, 2, PAIR], F32, own)
            fin = sb("o_fin", [P, 2, PAIR], F32, own)
            nat = sb("o_nat", [P, 2, 2, D], F32, own)
            with nc.Block() as block:
                @block.tensor
                def _(pe):
                    def back(j, s):
                        pe.wait_ge(o_x.sem, j + 1)
                        if not first(j, 2):
                            pe.wait_ge(o_cp.sem, j - 1)
                        for k in range(2):
                            last = pe.transpose(ps[:, 2 + s, k * P:(k + 1) * P], fin[:, s, k * P:(k + 1) * P], ident[:])
                        last.then_inc(o_tp.sem, 1)

                    def step(i, s):
                        if not first(i, 2):
                            pe.wait_ge(r4_a.sem, r4_a.at(i - 1))
                        nc.tensor.matmul(ps[:, s, 0:PAIR], lhsT=root_w[:, 1, :], rhs=hT[:, col(i)], start=True, stop=True)\
                            .then_inc(r4_mm.sem, 1)
                        if not first(i, 1):
                            back(i - 1, 1 - s)

                    stepped(pe, STEPS, 2, step, peel=2)
                    back(STEPS - 1, (STEPS - 1) % 2)

                @block.vector
                def _(v):
                    def step(i, s):
                        v.wait_ge(r4_mm.sem, r4_mm.at(i + 1))
                        if not first(i, 2):
                            v.wait_ge(o_x.sem, i - 1)
                        v.tensor_tensor(st[:, s, :], sumT[:, col(i)], ps[:, s, 0:PAIR], ALU.add).then_inc(r4_a.sem, 1)
                        v.wait_ge(r4_a.sem, r4_a.at(i + 1))
                        if not first(i, 2):
                            v.wait_ge(o_tp.sem, i - 1)
                        v.scalar_tensor_tensor(fin[:, s, :], st[:, s, :], root_b[:, 1:2], xT[:, col(i)], ALU.add, ALU.add)\
                            .then_inc(o_x.sem, 1)

                    stepped(v, STEPS, 2, step)

                @block.scalar
                def _(act):
                    def step(i, s):
                        act.wait_ge(o_tp.sem, i + 1)
                        if not first(i, 2):
                            act.wait_ge(o_dma[s].sem, (i - s) * 8)
                        act.activation(nat[:, s, :, :].rearrange("p k d -> p (k d)"), ps[:, 2 + s, 0:PAIR], ACT.Copy)\
                            .then_inc(o_cp.sem, 1)

                    stepped(act, STEPS, 2, step)

                @block.sync
                def _(sp):
                    whole = N // PAIR
                    to = out[0:whole * PAIR, :].rearrange("(b p) d -> p b d", p=P)

                    def store(i, s):
                        sp.wait_ge(o_cp.sem, i + 1)
                        if isinstance(i, int) and i == whole:
                            sp.dma_start(out[i * PAIR:N, :], nat[0:N - whole * PAIR, s, 0, :]).then_inc(o_dma[s].sem, 16)
                        else:
                            sp.dma_start(to[:, cut(2 * i, 2), :], nat[:, s, :, :]).then_inc(o_dma[s].sem, 16)

                    stepped(sp, STEPS, 2, store)
                    sp.wait_ge(o_dma[0].sem, 16 * ((STEPS + 1) // 2))
                    sp.wait_ge(o_dma[1].sem, 16 * (STEPS // 2))


def kernel(**inputs):
    import numpy as _np
    import concourse.bacc as _bacc
    from concourse.bass_utils import run_bass_kernel_spmd as _run

    nc = _bacc.Bacc("TRN2", target_bir_lowering=False, num_devices=1)
    arrays, args = {}, {}
    for name, value in inputs.items():
        v = _np.ascontiguousarray(value)
        arrays[f"in_{name}"] = v
        args[name] = nc.dram_tensor(f"in_{name}", v.shape, mybir.dt.from_np(v.dtype), kind="ExternalInput").ap()
    out = nc.dram_tensor("out_dram", (N, D), F32, kind="ExternalOutput").ap()
    build(nc, args, out)
    r = _run(nc, [arrays], core_ids=[0])
    return r.results[0]["out_dram"]
```
